# Optimizing a Trainium2 kernel written in Bass

```python
import numpy as np
import jax
import jax.numpy as jnp

def _softmax(x, axis=-1):
    return jax.nn.softmax(x, axis=axis)

def _gelu(x):
    return jax.nn.gelu(x, approximate=True)

def _silu(x):
    return jax.nn.silu(x)

def _sigmoid(x):
    return jax.nn.sigmoid(x)

def _layernorm(x, axis=-1, eps=1e-05):
    m = jnp.mean(x, axis=axis, keepdims=True)
    v = jnp.var(x, axis=axis, keepdims=True)
    return (x - m) / jnp.sqrt(v + eps)

def _scatter_add(tgt, idx, src, axis=0):
    return tgt.at[idx].add(src)

def _segment_sum(src, seg, n):
    return jax.ops.segment_sum(src, seg, n)
kernel_name = 'mk_sandwich_d2_jaxref_r8_f634f7'

def setup_inputs(seed: int=0):
    np.random.seed(seed)
    _w = jnp.asarray

    def _L0_attn_setup():
        import jax, jax.numpy as jnp
        import numpy as np
        HIDDEN = 256
        KEY_DIM = 256
        NUM_HEADS = 16
        HEAD_DIM = KEY_DIM // NUM_HEADS
        ROPE_THETA = 10000.0
        EPS = 1e-05

        def rms_norm(x, w, eps=EPS):
            var = jnp.mean(x * x, axis=-1, keepdims=True)
            return x * jax.lax.rsqrt(var + eps) * w

        def apply_rope(x, theta_base=ROPE_THETA):
            b, s, h, d = x.shape
            half = d // 2
            freqs = theta_base ** (jnp.arange(half, dtype=x.dtype) * (-2.0 / d))
            freqs = jnp.concatenate([freqs, freqs], axis=-1)
            pos = jnp.arange(s, dtype=x.dtype)
            ang = pos[:, None] * freqs[None, :]
            cos = jnp.cos(ang)[None, :, None, :]
            sin = jnp.sin(ang)[None, :, None, :]
            x_even = x[..., 0::2]
            x_odd = x[..., 1::2]
            x1 = jnp.concatenate([x_even, x_even], axis=-1)
            x2 = jnp.concatenate([x_odd, x_odd], axis=-1)
            even_mask = (jnp.arange(d) % 2 == 0)[None, None, None, :]
            return jnp.where(even_mask, cos * x1 - sin * x2, sin * x1 + cos * x2)
        key = jax.random.key(seed)
        ks = jax.random.split(key, 10)
        B, S = (2, 256)
        s_in = 1.0 / np.sqrt(HIDDEN)
        s_k = 1.0 / np.sqrt(KEY_DIM)
        return {'x': jax.random.normal(ks[0], (B, S, HIDDEN), dtype=jnp.float32), 'rms_w': jnp.ones((HIDDEN,), dtype=jnp.float32), 'wq': jax.random.normal(ks[1], (HIDDEN, KEY_DIM), dtype=jnp.float32) * s_in, 'bq': jnp.zeros((KEY_DIM,), dtype=jnp.float32), 'wk': jax.random.normal(ks[2], (HIDDEN, KEY_DIM), dtype=jnp.float32) * s_in, 'bk': jnp.zeros((KEY_DIM,), dtype=jnp.float32), 'wv': jax.random.normal(ks[3], (HIDDEN, KEY_DIM), dtype=jnp.float32) * s_in, 'bv': jnp.zeros((KEY_DIM,), dtype=jnp.float32), 'wo': jax.random.normal(ks[4], (KEY_DIM, HIDDEN), dtype=jnp.float32) * s_k, 'bo': jnp.zeros((HIDDEN,), dtype=jnp.float32)}
    _L0_attn_in = _L0_attn_setup()

    def _L0_ffn_setup():
        import jax, jax.numpy as jnp
        import numpy as np
        H = 256
        E = 8
        K = 2
        I = 16
        key = jax.random.key(seed)
        k1, k2, k3, k4 = jax.random.split(key, 4)
        B, T = (2, 512)
        x = jax.random.normal(k1, (B, T, H), dtype=jnp.float32)
        router_w = jax.random.normal(k2, (E, H), dtype=jnp.float32) / np.sqrt(H)
        down_w = jax.random.normal(k3, (E, I, H), dtype=jnp.float32) / np.sqrt(H)
        up_w = jax.random.normal(k4, (E, H, I), dtype=jnp.float32) / np.sqrt(I)
        return {'x': x, 'router_w': router_w, 'down_w': down_w, 'up_w': up_w}
    _L0_ffn_in = _L0_ffn_setup()

    def _L1_attn_setup():
        import jax, jax.numpy as jnp
        import numpy as np
        N_HEAD_HALF = 8
        LAMBDA_INIT = 0.2
        RMS_EPS = 1.1920929e-07
        ROPE_BASE = 10000.0

        def _rms_norm(x):
            var = jnp.mean(x * x, axis=-1, keepdims=True)
            return x * jax.lax.rsqrt(var + RMS_EPS)

        def _rotary(x):
            d = x.shape[-1]
            inv_freq = (1.0 / ROPE_BASE) ** (jnp.arange(0, d, 2, dtype=jnp.float32) / d)
            t = jnp.arange(x.shape[1], dtype=jnp.float32)
            freqs = jnp.outer(t, inv_freq)
            cos = jnp.cos(freqs)[None, :, None, :]
            sin = jnp.sin(freqs)[None, :, None, :]
            x1, x2 = jnp.split(x, 2, axis=-1)
            return jnp.concatenate((x1 * cos + x2 * sin, -x1 * sin + x2 * cos), axis=-1)

        def _causal_attn(q, k, v, scale):
            T = q.shape[2]
            s = jnp.einsum('bhqd,bhkd->bhqk', q, k) * scale
            mask = jnp.tril(jnp.ones((T, T), dtype=bool))
            s = jnp.where(mask, s, jnp.float32(-jnp.inf))
            p = jax.nn.softmax(s, axis=-1)
            return jnp.einsum('bhqk,bhkd->bhqd', p, v)
        key = jax.random.key(seed)
        ks = jax.random.split(key, 9)
        B, T, C = (2, 256, 256)
        HD = C // N_HEAD_HALF
        s = 0.02
        return {'x': jax.random.normal(ks[0], (B, T, C), jnp.float32), 'wq': jax.random.normal(ks[1], (C, C), jnp.float32) * s, 'wk': jax.random.normal(ks[2], (C, C), jnp.float32) * s, 'wv': jax.random.normal(ks[3], (C, C), jnp.float32) * s, 'wo': jax.random.normal(ks[4], (C, C), jnp.float32) * s, 'lq1': jax.random.normal(ks[5], (HD,), jnp.float32) * 0.1, 'lk1': jax.random.normal(ks[6], (HD,), jnp.float32) * 0.1, 'lq2': jax.random.normal(ks[7], (HD,), jnp.float32) * 0.1, 'lk2': jax.random.normal(ks[8], (HD,), jnp.float32) * 0.1}
    _L1_attn_in = _L1_attn_setup()

    def _L1_ffn_setup():
        import jax, jax.numpy as jnp
        import numpy as np
        B, T, D = (2, 128, 256)
        E, F, K = (64, 64, 4)
        S, HS = (2, 64 * 4)
        key = jax.random.key(seed)
        ks = jax.random.split(key, 9)
        s = 0.02
        f32 = jnp.float32
        return {'x': jax.random.normal(ks[0], (B, T, D), f32), 'router_w': jax.random.normal(ks[1], (D, E), f32) * s, 'router_bias': jnp.zeros((E,), f32), 'wg': jax.random.normal(ks[2], (E, D, F), f32) * s, 'wu': jax.random.normal(ks[3], (E, D, F), f32) * s, 'wd': jax.random.normal(ks[4], (E, F, D), f32) * s, 'swg': jax.random.normal(ks[5], (S, D, HS), f32) * s, 'swu': jax.random.normal(ks[6], (S, D, HS), f32) * s, 'swd': jax.random.normal(ks[7], (S, HS, D), f32) * s}
    _L1_ffn_in = _L1_ffn_setup()
    _d = {'L0_attn_x': _L0_attn_in['x'], 'L0_attn_rms_w': _L0_attn_in['rms_w'], 'L0_attn_wq': _L0_attn_in['wq'], 'L0_attn_bq': _L0_attn_in['bq'], 'L0_attn_wk': _L0_attn_in['wk'], 'L0_attn_bk': _L0_attn_in['bk'], 'L0_attn_wv': _L0_attn_in['wv'], 'L0_attn_bv': _L0_attn_in['bv'], 'L0_attn_wo': _L0_attn_in['wo'], 'L0_attn_bo': _L0_attn_in['bo'], 'L0_ffn_router_w': _L0_ffn_in['router_w'], 'L0_ffn_down_w': _L0_ffn_in['down_w'], 'L0_ffn_up_w': _L0_ffn_in['up_w'], 'L1_attn_wq': _L1_attn_in['wq'], 'L1_attn_wk': _L1_attn_in['wk'], 'L1_attn_wv': _L1_attn_in['wv'], 'L1_attn_wo': _L1_attn_in['wo'], 'L1_attn_lq1': _L1_attn_in['lq1'], 'L1_attn_lk1': _L1_attn_in['lk1'], 'L1_attn_lq2': _L1_attn_in['lq2'], 'L1_attn_lk2': _L1_attn_in['lk2'], 'L1_ffn_router_w': _L1_ffn_in['router_w'], 'L1_ffn_router_bias': _L1_ffn_in['router_bias'], 'L1_ffn_wg': _L1_ffn_in['wg'], 'L1_ffn_wu': _L1_ffn_in['wu'], 'L1_ffn_wd': _L1_ffn_in['wd'], 'L1_ffn_swg': _L1_ffn_in['swg'], 'L1_ffn_swu': _L1_ffn_in['swu'], 'L1_ffn_swd': _L1_ffn_in['swd']}
    _x0 = _d['L0_attn_x']
    _d['L0_attn_x'] = jax.random.normal(jax.random.fold_in(jax.random.key(seed), 1), (2, 512, 256), dtype=_x0.dtype)
    del _x0
    return _d

def reference(L0_attn_x, L0_attn_rms_w, L0_attn_wq, L0_attn_bq, L0_attn_wk, L0_attn_bk, L0_attn_wv, L0_attn_bv, L0_attn_wo, L0_attn_bo, L0_ffn_router_w, L0_ffn_down_w, L0_ffn_up_w, L1_attn_wq, L1_attn_wk, L1_attn_wv, L1_attn_wo, L1_attn_lq1, L1_attn_lk1, L1_attn_lq2, L1_attn_lk2, L1_ffn_router_w, L1_ffn_router_bias, L1_ffn_wg, L1_ffn_wu, L1_ffn_wd, L1_ffn_swg, L1_ffn_swu, L1_ffn_swd):

    def _L0_attn_ref(x, rms_w, wq, bq, wk, bk, wv, bv, wo, bo):
        import jax, jax.numpy as jnp
        import numpy as np
        HIDDEN = 256
        KEY_DIM = 256
        NUM_HEADS = 16
        HEAD_DIM = KEY_DIM // NUM_HEADS
        ROPE_THETA = 10000.0
        EPS = 1e-05

        def rms_norm(x, w, eps=EPS):
            var = jnp.mean(x * x, axis=-1, keepdims=True)
            return x * jax.lax.rsqrt(var + eps) * w

        def apply_rope(x, theta_base=ROPE_THETA):
            b, s, h, d = x.shape
            half = d // 2
            freqs = theta_base ** (jnp.arange(half, dtype=x.dtype) * (-2.0 / d))
            freqs = jnp.concatenate([freqs, freqs], axis=-1)
            pos = jnp.arange(s, dtype=x.dtype)
            ang = pos[:, None] * freqs[None, :]
            cos = jnp.cos(ang)[None, :, None, :]
            sin = jnp.sin(ang)[None, :, None, :]
            x_even = x[..., 0::2]
            x_odd = x[..., 1::2]
            x1 = jnp.concatenate([x_even, x_even], axis=-1)
            x2 = jnp.concatenate([x_odd, x_odd], axis=-1)
            even_mask = (jnp.arange(d) % 2 == 0)[None, None, None, :]
            return jnp.where(even_mask, cos * x1 - sin * x2, sin * x1 + cos * x2)
        B, S, _ = x.shape
        residual = x
        xn = rms_norm(x, rms_w)
        q = (xn @ wq + bq).reshape(B, S, NUM_HEADS, HEAD_DIM)
        k = (xn @ wk + bk).reshape(B, S, NUM_HEADS, HEAD_DIM)
        v = (xn @ wv + bv).reshape(B, S, NUM_HEADS, HEAD_DIM)
        q = apply_rope(q)
        k = apply_rope(k)
        scores = jnp.einsum('bshd,bthd->bhst', q, k) / jnp.sqrt(jnp.asarray(HEAD_DIM, dtype=x.dtype))
        causal = jnp.tril(jnp.ones((S, S), dtype=bool))[None, None]
        scores = jnp.where(causal, scores, -jnp.inf)
        probs = jax.nn.softmax(scores, axis=-1)
        out = jnp.einsum('bhst,bthd->bshd', probs, v).reshape(B, S, KEY_DIM)
        return out @ wo + bo + residual

    def _L0_ffn_ref(x, router_w, down_w, up_w):
        import jax, jax.numpy as jnp
        import numpy as np
        H = 256
        E = 8
        K = 2
        I = 16
        logits = jnp.einsum('bth,eh->bte', x, router_w)
        weights = jax.nn.softmax(logits, axis=-1)
        top_w, top_idx = jax.lax.top_k(weights, K)
        topk_mask = jnp.sum(jax.nn.one_hot(top_idx, E, dtype=x.dtype), axis=-2)
        gate = weights * topk_mask
        h = jnp.einsum('bth,eih->beti', x, down_w)
        a = jax.nn.silu(h)
        expert_out = jnp.einsum('beti,ehi->beth', a, up_w)
        out = jnp.einsum('beth,bte->bth', expert_out, gate)
        return out

    def _L1_attn_ref(x, wq, wk, wv, wo, lq1, lk1, lq2, lk2):
        import jax, jax.numpy as jnp
        import numpy as np
        N_HEAD_HALF = 8
        LAMBDA_INIT = 0.2
        RMS_EPS = 1.1920929e-07
        ROPE_BASE = 10000.0

        def _rms_norm(x):
            var = jnp.mean(x * x, axis=-1, keepdims=True)
            return x * jax.lax.rsqrt(var + RMS_EPS)

        def _rotary(x):
            d = x.shape[-1]
            inv_freq = (1.0 / ROPE_BASE) ** (jnp.arange(0, d, 2, dtype=jnp.float32) / d)
            t = jnp.arange(x.shape[1], dtype=jnp.float32)
            freqs = jnp.outer(t, inv_freq)
            cos = jnp.cos(freqs)[None, :, None, :]
            sin = jnp.sin(freqs)[None, :, None, :]
            x1, x2 = jnp.split(x, 2, axis=-1)
            return jnp.concatenate((x1 * cos + x2 * sin, -x1 * sin + x2 * cos), axis=-1)

        def _causal_attn(q, k, v, scale):
            T = q.shape[2]
            s = jnp.einsum('bhqd,bhkd->bhqk', q, k) * scale
            mask = jnp.tril(jnp.ones((T, T), dtype=bool))
            s = jnp.where(mask, s, jnp.float32(-jnp.inf))
            p = jax.nn.softmax(s, axis=-1)
            return jnp.einsum('bhqk,bhkd->bhqd', p, v)
        B, T, C = x.shape
        NH = N_HEAD_HALF
        HD = C // NH
        HH = HD // 2
        lam1 = jnp.exp(jnp.sum(lq1 * lk1))
        lam2 = jnp.exp(jnp.sum(lq2 * lk2))
        lam = lam1 - lam2 + LAMBDA_INIT
        q = (x @ wq.T).reshape(B, T, NH, 2, HH).transpose(0, 2, 1, 3, 4)
        k = (x @ wk.T).reshape(B, T, NH, 2, HH).transpose(0, 2, 1, 3, 4)
        v = (x @ wv.T).reshape(B, T, NH, HD).transpose(0, 2, 1, 3)
        q1 = _rotary(_rms_norm(q[..., 0, :]))
        q2 = _rotary(_rms_norm(q[..., 1, :]))
        k1 = _rotary(_rms_norm(k[..., 0, :]))
        k2 = _rotary(_rms_norm(k[..., 1, :]))
        scale = 1.0 / jnp.sqrt(jnp.float32(HH))
        y = _causal_attn(q1, k1, v, scale) - lam * _causal_attn(q2, k2, v, scale)
        y = y.transpose(0, 2, 1, 3).reshape(B, T, C)
        y = y @ wo.T * (1.0 - LAMBDA_INIT)
        return y

    def _L1_ffn_ref(x, router_w, router_bias, wg, wu, wd, swg, swu, swd):
        import jax, jax.numpy as jnp
        import numpy as np
        B, T, D = (2, 128, 256)
        E, F, K = (64, 64, 4)
        S, HS = (2, 64 * 4)
        b, t, d = x.shape
        flat = x.reshape(b * t, d)
        n = flat.shape[0]
        logits = flat @ router_w
        scores = jax.nn.softmax(logits, axis=-1)
        _, topk_idx = jax.lax.top_k(logits + router_bias, K)
        topk_scores = jnp.take_along_axis(scores, topk_idx, axis=-1)
        topk_scores = topk_scores / topk_scores.sum(axis=-1, keepdims=True)
        comb = jnp.zeros((n, E), dtype=flat.dtype).at[jnp.arange(n)[:, None], topk_idx].set(topk_scores)
        g = jax.nn.silu(jnp.einsum('nd,edf->nef', flat, wg))
        u = jnp.einsum('nd,edf->nef', flat, wu)
        routed = jnp.einsum('ne,nef,efd->nd', comb, g * u, wd)
        sg = jax.nn.silu(jnp.einsum('nd,sdh->nsh', flat, swg))
        su = jnp.einsum('nd,sdh->nsh', flat, swu)
        shared = jnp.einsum('nsh,shd->nd', sg * su, swd)
        return (routed + shared).reshape(b, t, d)
    x = L0_attn_x
    x = x + _layernorm(_L0_attn_ref(_layernorm(x, axis=-1), L0_attn_rms_w, L0_attn_wq, L0_attn_bq, L0_attn_wk, L0_attn_bk, L0_attn_wv, L0_attn_bv, L0_attn_wo, L0_attn_bo), axis=-1)
    x = x + _layernorm(_L0_ffn_ref(_layernorm(x, axis=-1), L0_ffn_router_w, L0_ffn_down_w, L0_ffn_up_w), axis=-1)
    x = x + _layernorm(_L1_attn_ref(_layernorm(x, axis=-1), L1_attn_wq, L1_attn_wk, L1_attn_wv, L1_attn_wo, L1_attn_lq1, L1_attn_lk1, L1_attn_lq2, L1_attn_lk2), axis=-1)
    x = x + _layernorm(_L1_ffn_ref(_layernorm(x, axis=-1), L1_ffn_router_w, L1_ffn_router_bias, L1_ffn_wg, L1_ffn_wu, L1_ffn_wd, L1_ffn_swg, L1_ffn_swu, L1_ffn_swd), axis=-1)
    return x

_drawn_inputs = setup_inputs


def setup_inputs(seed=0):
    import zlib

    import numpy as np

    out = dict(_drawn_inputs(seed))
    spreads = {'L0_attn_rms_w': (1.0, 0.2),
     'L0_attn_bq': (0.0, 0.1),
     'L0_attn_bk': (0.0, 0.1),
     'L0_attn_bv': (0.0, 0.1),
     'L0_attn_bo': (0.0, 0.1),
     'L1_ffn_router_bias': (0.0, 0.1)}
    factors = {'L1_attn_lk1': 4.507, 'L1_attn_lq2': 7.161, 'L1_attn_lk2': 198.408}
    for name, (base, spread) in spreads.items():
        noise = np.random.default_rng([zlib.crc32(name.encode()), seed]).standard_normal(out[name].shape)
        drawn = base * np.exp(spread * noise) if base else spread * noise
        out[name] = jnp.asarray(drawn.astype(out[name].dtype))
    for name, factor in factors.items():
        out[name] = (out[name] * factor).astype(out[name].dtype)
    return out
```

```python
import math
from contextlib import ExitStack

import numpy as np

import concourse.bass as bass
from concourse import mybir

P = 128
B, S, D = 2, 512, 256
TOK = B * S
NT = TOK // P
TB = S // P
KT = D // P
HEADS0, HD0 = 16, 16
ROT = HD0 // 2
MAPS = 16
HEADS1, HD1 = 8, 32
HH = HD1 // 2
E0, I0 = 8, 16
E1, F1, TOPK1 = 64, 64, 4
SH, HS = 2, 256
EPS = 1e-5
RMS_EPS1 = 1.1920929e-07
LAMBDA_INIT = 0.2
NEG = -1.0e30

SLOT = (32, 64)
DH = (ROT, HH)
GROUPS = (4, 8)
PCOL = [0, 512, 1024, 896]
PW = 1280
PSLOTS = 6
PAIRS = E1 // 2 + SH * HS // P
RING = 4


def build(nc, x, rms_w, wqkv0, bqkv0, wo0, bo0, wrd0, up0, wqkv1, wo1, lvec, router1, rbias1, wmoe,
          rope, ident_in, mask_in, out, comb_dram):
    f32, f32r, bf16, u32 = mybir.dt.float32, mybir.dt.float32r, mybir.dt.bfloat16, mybir.dt.uint32
    ALU, ACT, AX = mybir.AluOpType, mybir.ActivationFunctionType, mybir.AxisListType

    ctx = ExitStack()
    with ctx:
        def sb(name, shape, dt=f32):
            return ctx.enter_context(nc.sbuf_tensor(name, shape, dt))

        def sem(name):
            return ctx.enter_context(nc.semaphore(name))

        X = sb("X", [P, NT, D])
        H = sb("H", [P, NT, D])
        XN = sb("XN", [P, NT, D])
        XT = sb("XT", [P, B, KT, S])
        XTall = XT[:, :, :, :]
        QK = sb("QK", [P, 2, 2 * D])
        RA = sb("RA", [P, 2 * D])
        RB = sb("RB", [P, 2 * D])
        QP0 = sb("QP0", [P, B, TB, 2 * D])
        KP0 = sb("KP0", [P, 2, 2 * D])
        QKP1 = QP0[:, :, :, :].rearrange("p b t c -> p b (t c)").rearrange(
            "p r (a c) -> p r a c", a=2)
        QT = sb("QT", [P, B, 8, S], f32r)
        KTr = sb("KTr", [P, B, 8, S], f32r)
        VA = sb("VA", [P, NT, HEADS0, 32])
        V1 = VA[:, :, :, :].rearrange("p t h c -> p t (h c)")[:, :, 0:D]
        PR = sb("PR", [P, PSLOTS, PW])
        OT = sb("OT", [P, 4, S])
        ones32 = sb("ones32", [P, 32])
        ident = sb("ident", [P, P])
        identb = sb("identb", [P, P], bf16)
        masks = sb("masks", [P, 2, P])
        masksb = sb("masksb", [P, 2, P], bf16)
        rope_sb = sb("rope_sb", [P, TB, 4, ROT])
        wq_sb = sb("wq_sb", [P, KT, 3 * D])
        wo_sb = sb("wo_sb", [P, KT, D])
        bqkv_sb = sb("bqkv_sb", [P, 3 * D])
        bo_sb = sb("bo_sb", [P, D])
        rms_sb = sb("rms_sb", [P, KT])
        wrd_sb = sb("wrd_sb", [P, KT, E0 + E0 * I0])
        up_sb = sb("up_sb", [P, D])
        lv_sb = sb("lv_sb", [P, 4, HD1])
        lam_sb = sb("lam_sb", [P, 4])
        r1_sb = sb("r1_sb", [P, KT, E1])
        rb_sb = sb("rb_sb", [P, E1])
        iota_f = sb("iota_f", [P, E1])
        st = sb("st", [P, NT, 6])
        mv = sb("mv", [P, NT, 2])
        lnv = sb("lnv", [P, NT])
        rstd = sb("rstd", [P, NT])
        msq = sb("msq", [P, NT])
        rr = sb("rr", [P, NT])
        mx = sb("mx", [P, NT, HEADS0])
        ss = sb("ss", [P, 2, 32])
        rs1 = sb("rs1", [P, 2, 32])
        den = sb("den", [P, HEADS0])
        lgs = sb("lgs", [P, TB, E1])
        shl = sb("shl", [P, TB, E1])
        exl = sb("exl", [P, TB, E1])
        oh = sb("oh", [P, TB, E1])
        oh2 = sb("oh2", [P, TB, E1])
        top = sb("top", [P, TB, 8])
        idx = sb("idx", [P, TB, 8], u32)
        idxf = sb("idxf", [P, TB, 8])
        red = sb("red", [P, 2 * TB])
        eps_sb = sb("eps_sb", [P, 2])
        NA, NB = RA, RB
        ringW = PR[:, 0:3, :].rearrange("p a c -> p (a c)")[:, 0:RING * 768].rearrange(
            "p (r c) -> p r c", r=RING)
        combB = QP0[:, :, :, :].rearrange("p b t c -> p (b t c)").rearrange("p (r c) -> p r c", r=4)
        act = OT[:, 0:2, :]
        act2 = OT[:, 2:4, :]
        combT = QK[:, :, :].rearrange("p a c -> p (a c)")

        PSUM = ctx.enter_context(nc.psum_tensor("PSUM", [P, 8, 512], f32))

        def bank(n, k=1):
            return PSUM[:, n:n + k, :].rearrange("p a c -> p (a c)")

        s_ld = sem("s_ld")
        s_x = sem("s_x")
        s_w0 = sem("s_w0")
        s_w1 = sem("s_w1")
        s_w1o = sem("s_w1o")
        s_dv = sem("s_dv")
        s_ac = sem("s_ac")
        s_pool = sem("s_pool")
        s_const = sem("s_const")
        s_var = sem("s_var")
        s_rstd = sem("s_rstd")
        s_msq = sem("s_msq")
        s_rr = sem("s_rr")
        s_xn = sem("s_xn")
        s_xtps = sem("s_xtps")
        s_xt = sem("s_xt")
        s_qkv = sem("s_qkv")
        s_qkve = sem("s_qkve")
        s_ss = sem("s_ss")
        s_rs1 = sem("s_rs1")
        s_pad = sem("s_pad")
        s_tps = sem("s_tps")
        s_tev = sem("s_tev")
        s_mps = sem("s_mps")
        s_mrd = sem("s_mrd")
        s_neg = sem("s_neg")
        s_rqps = sem("s_rqps")
        s_rq = sem("s_rq")
        s_sc = sem("s_sc")
        s_p = sem("s_p")
        s_pv = sem("s_pv")
        s_pve = sem("s_pve")
        s_otps = sem("s_otps")
        s_on = sem("s_on")
        s_ontps = sem("s_ontps")
        s_ont = sem("s_ont")
        s_wo = sem("s_wo")
        s_woe = sem("s_woe")
        s_qkve1 = sem("s_qkve1")
        s_woe1 = sem("s_woe1")
        s_ones = sem("s_ones")
        s_g1 = sem("s_g1")
        s_rd = sem("s_rd")
        s_lmax = sem("s_lmax")
        s_ex = sem("s_ex")
        s_aw = sem("s_aw")
        s_awps = sem("s_awps")
        s_awt = sem("s_awt")
        s_up = sem("s_up")
        s_upe = sem("s_upe")
        s_lamd = sem("s_lamd")
        s_lame = sem("s_lame")
        s_rt = sem("s_rt")
        s_rte = sem("s_rte")
        s_rex = sem("s_rex")
        s_comb = sem("s_comb")
        s_cps = sem("s_cps")
        s_cT = sem("s_cT")
        s_cd = sem("s_cd")
        s_wr = [sem(f"s_wr{r}") for r in range(RING)]
        s_gu = sem("s_gu")
        s_sg = sem("s_sg")
        s_gt = sem("s_gt")
        s_dn = sem("s_dn")
        s_yT = sem("s_yT")
        s_yps = sem("s_yps")
        s_fin = sem("s_fin")
        s_out = sem("s_out")

        block = ctx.enter_context(nc.Block())

        def slot(l, m):
            per = P // SLOT[l]
            return m // per, SLOT[l] * (m % per)

        def tunits(l):
            return [(a, 4 * n) for a in (0, 1) for n in range(GROUPS[l] // 4)]

        MUNITS = [(i, u) for i in range(TB) for u in range((2, 4, 8, 8)[i])]
        MHEADS = (8, 4, 2, 2)
        NTU = 2

        def tcount(l, b, i):
            n = b * TB + i + 1
            return 2 * n if l == 0 else 2 * NT + 4 * n

        def split_parts(dv, did, settle, qp, kp, rq, rk, d):
            did(dv.tensor_copy(qp[:, :, 0:d].bitcast(f32r), rq))
            did(dv.tensor_copy(kp[:, :, 0:d].bitcast(f32r), rk))
            settle()
            did(dv.tensor_copy(qp[:, :, d:2 * d], qp[:, :, 0:d]))
            did(dv.tensor_copy(kp[:, :, 2 * d:3 * d], kp[:, :, 0:d]))
            did(dv.tensor_tensor(qp[:, :, 2 * d:3 * d], rq, qp[:, :, 0:d], ALU.subtract))
            did(dv.tensor_tensor(kp[:, :, d:2 * d], rk, kp[:, :, 0:d], ALU.subtract), s_pad)

        @block.sync
        def _(sp):
            sp.dma_start(X[:, 0:TB, :], x[0:S, :].rearrange("(t p) d -> p t d", p=P)).then_inc(s_x, 16)
            sp.dma_start(ident[:, :], ident_in).then_inc(s_ld, 16)
            sp.dma_start(masks[:, :, :], mask_in).then_inc(s_ld, 16)
            sp.dma_start(X[:, TB:NT, :], x[S:TOK, :].rearrange("(t p) d -> p t d", p=P)).then_inc(s_x, 16)
            sp.dma_start(rms_sb[:, :], rms_w).then_inc(s_w0, 16)
            sp.dma_start(wq_sb[:, :, :], wqkv0.rearrange("(k p) n -> p k n", p=P)).then_inc(s_w0, 16)
            sp.dma_start(bqkv_sb[:, :], bqkv0.partition_broadcast(P)).then_inc(s_w0, 16)
            sp.dma_start(rope_sb[:, :, :, :], rope).then_inc(s_w0, 16)
            sp.dma_start(bo_sb[:, :], bo0.partition_broadcast(P)).then_inc(s_w0, 16)
            sp.dma_start(wo_sb[:, :, :], wo0.rearrange("(k p) n -> p k n", p=P)).then_inc(s_w0, 16)
            sp.dma_start(wrd_sb[:, :, :], wrd0.rearrange("(k p) n -> p k n", p=P)).then_inc(s_w0, 16)
            sp.dma_start(up_sb[:, :], up0).then_inc(s_w0, 16)
            sp.dma_start(lv_sb[:, :, :].rearrange("p a c -> p (a c)"), lvec.partition_broadcast(P)).then_inc(s_ld, 16)
            sp.dma_start(r1_sb[:, :, :], router1.rearrange("(k p) n -> p k n", p=P)).then_inc(s_ld, 16)
            sp.dma_start(rb_sb[:, :], rbias1.partition_broadcast(P)).then_inc(s_ld, 16)
            sp.wait_ge(s_qkv, NT)
            sp.dma_start(wq_sb[:, :, :], wqkv1.rearrange("(k p) n -> p k n", p=P)).then_inc(s_w1, 16)
            sp.wait_ge(s_wo, NT)
            sp.dma_start(wo_sb[:, :, :], wo1.rearrange("(k p) n -> p k n", p=P)).then_inc(s_w1o, 16)
            sp.wait_ge(s_cT, 2)
            sp.wait_ge(s_ones, 1)
            sp.dma_start(comb_dram[0:E1, :], combT[0:E1, :]).then_inc(s_cd, 16)
            sp.dma_start(comb_dram[E1:2 * PAIRS, :], H[0:2 * PAIRS - E1, 0:4, :].rearrange("p t c -> p (t c)")).then_inc(s_cd, 16)
            sp.wait_ge(s_cd, 32)

            wblk = wmoe.rearrange("(a r) p c -> a r p c", r=RING)
            cblk = comb_dram.rearrange("(a r h) t -> a r h t", r=RING, h=2)

            def load(it, r, first):
                if not first:
                    sp.wait_ge(s_dn, 2 * RING * it + 2 * (r - RING + 1))
                at = it if first else bass.ds(it, 1)
                w = wblk[at, r] if first else wblk[at, r].rearrange("a p c -> p (a c)")
                sp.dma_start(ringW[:, r, :], w).then_inc(s_wr[r], 16)
                for h in range(2):
                    row = cblk[at, r, h] if first else cblk[at, r, h].rearrange("a t -> (a t)")
                    sp.dma_start(combB[64 * h:64 * h + 64, r, :], row.partition_broadcast(64)).then_inc(s_wr[r], 16)

            for r in range(RING):
                load(0, r, True)
            with sp.Fori(1, PAIRS // RING) as it:
                for r in range(RING):
                    load(it, r, False)
            sp.wait_ge(s_fin, 1)
            sp.dma_start(out[0:S, :].rearrange("(t p) d -> p t d", p=P), X[:, 0:TB, :]).then_inc(s_out, 16)
            sp.wait_ge(s_fin, 2)
            sp.dma_start(out[S:TOK, :].rearrange("(t p) d -> p t d", p=P), X[:, TB:NT, :]).then_inc(s_out, 16)
            sp.wait_ge(s_out, 32)

        @block.gpsimd
        def _(pool):
            pool.iota(iota_f[:, :], [[1, E1]], base=0, channel_multiplier=0,
                      allow_small_or_imprecise_dtypes=True).then_inc(s_pool, 1)

        @block.tensor
        def _(pe):
            def turn_tokens(k, b):
                pe.wait_ge(s_xn, 2 * k + b + 1)
                for kt in range(KT):
                    for i in range(TB):
                        mm = pe.transpose(bank(2 * b + kt)[:, i * P:(i + 1) * P],
                                          XN[:, b * TB + i, kt * P:(kt + 1) * P], ident[:, :])
                mm.then_inc(s_xtps, 1)

            def project(l, b, i):
                c = b * TB + i
                if c >= 2:
                    pe.wait_ge((s_qkve, s_qkve1)[l], c - 1)
                for kt in range(KT):
                    pe.matmul(bank(4 + i % 2), XT[:, b, kt, i * P:(i + 1) * P], wq_sb[:, kt, 0:2 * D],
                              start=(kt == 0), stop=(kt == KT - 1))
                for kt in range(KT):
                    mm = pe.matmul(bank(6 + i % 2)[:, 0:D], XT[:, b, kt, i * P:(i + 1) * P],
                                   wq_sb[:, kt, 2 * D:3 * D], start=(kt == 0), stop=(kt == KT - 1))
                mm.then_inc(s_qkv, 1)

            def turn_padded(l, b, i):
                c = b * TB + i
                pe.wait_ge(s_pad, l * NT + c + 1)
                for n, (q, g0) in enumerate(tunits(l)):
                    u = tcount(l, b, i) - len(tunits(l)) + n
                    if u >= 4:
                        pe.wait_ge(s_tev, u - 3)
                    for g in range(4):
                        if l == 0:
                            src = (QP0[:, b, i, :] if q else KP0[:, c % 2, :])
                        else:
                            src = QKP1[:, c % 2, q, :]
                        mm = pe.transpose(bank(u % 4)[:, g * P:(g + 1) * P],
                                          src[:, (g0 + g) * P:(g0 + g + 1) * P], ident[:, :])
                    mm.then_inc(s_tps, 1)

            def prepare(l, b):
                pe.wait_ge(s_xt, 4 * l + 2)
                for i in range(TB):
                    project(l, b, i)
                    if i >= 1:
                        turn_padded(l, b, i - 1)
                turn_padded(l, b, TB - 1)

            def maxima(b):
                for m, (i, u) in enumerate(MUNITS):
                    cnt = b * len(MUNITS) + m
                    if cnt >= 4:
                        pe.wait_ge(s_mrd, cnt - 3)
                    nk = (i + 1) * P
                    for k in range(MHEADS[i]):
                        n = MHEADS[i] * u + k
                        g, row = n % 4, 32 * (n // 4)
                        off = k * nk if i < 2 else k * 512
                        o = bank(2 * (cnt % 4), 2)[:, off:off + nk]
                        pe.matmul(o, QT[row:row + 32, b, g, i * P:(i + 1) * P], KTr[row:row + 32, b, g, 0:nk],
                                  start=True, stop=False)
                        mm = pe.matmul(o[:, i * P:nk], identb[:, :], masksb[:, 1, :], start=False, stop=True)
                    mm.then_inc(s_mps, 1)

            def turn_again(b, i):
                pe.wait_ge(s_neg, b * TB + i + 1)
                pe.wait_ge(s_mrd, (b + 1) * len(MUNITS))
                for g in range(4):
                    mm = pe.transpose(bank(i)[:, g * P:(g + 1) * P], QP0[:, b, i, g * P:(g + 1) * P], ident[:, :])
                mm.then_inc(s_rqps, 1)

            def order1(n):
                G, half, c = n // 8, n // 4 % 2, n % 4
                return 2 * (4 * G + c) + half

            def weigh0(b, g):
                pe.wait_ge(s_p, b * MAPS + 4 * g + 4)
                c = b * 4 + g
                if c >= 2:
                    pe.wait_ge(s_pve, c - 1)
                for j in range(TB):
                    for k in range(4):
                        mm = pe.matmul(bank(6 + g % 2)[32 * k:32 * k + 32, j * P:S], VA[:, b * TB + j, 4 * g + k, :],
                                       PR[:, (b * MAPS + 4 * g + k) % PSLOTS, PCOL[j]:PCOL[j] + S - j * P],
                                       start=(j == 0), stop=(j == TB - 1), tile_position=(0, 32 * k))
                mm.then_inc(s_pv, 1)

            def weigh1(b, q):
                base = (2 + b) * MAPS + 4 * q
                pe.wait_ge(s_p, base + 4)
                c = 8 + b * 4 + q
                pe.wait_ge(s_pve, c)
                G = q // 2
                for j in range(TB):
                    for k in range(4):
                        pr = PR[:, (base + k) % PSLOTS, PCOL[j]:PCOL[j] + S - j * P]
                        pe.matmul(bank(6)[32 * k:32 * k + 32, j * P:S], V1[:, b * TB + j, (4 * G + k) * 32:(4 * G + k + 1) * 32],
                                  pr, start=(j == 0), stop=(j == TB - 1), tile_position=(0, 32 * k))
                    for k in range(4):
                        pr = PR[:, (base + k) % PSLOTS, PCOL[j]:PCOL[j] + S - j * P]
                        mm = pe.matmul(bank(7)[32 * k:32 * k + 32, j * P:S], ones32[:, :], pr,
                                       start=(j == 0), stop=(j == TB - 1), tile_position=(0, 32 * k))
                mm.then_inc(s_pv, 1)

            def attend(l, b):
                for n in range(MAPS):
                    scores_n(l, b, n)
                    if n >= 5 and n % 4 == 1:
                        (weigh0 if l == 0 else weigh1)(b, n // 4 - 1)
                (weigh0 if l == 0 else weigh1)(b, 3)

            def scores_n(l, b, n):
                c = (2 * l + b) * MAPS + n
                if c >= 2:
                    pe.wait_ge(s_p, c - 1)
                m = n if l == 0 else order1(n)
                g, row = slot(l, m)
                o = bank(3 * (n % 2), 3)
                for j in (0, 1, 3, 2):
                    w = S - j * P
                    blk = o[:, PCOL[j]:PCOL[j] + w]
                    pe.matmul(blk, KTr[row:row + SLOT[l], b, g, j * P:(j + 1) * P],
                              QT[row:row + SLOT[l], b, g, j * P:S], start=True, stop=False)
                    mm = pe.matmul(blk[:, 0:P], identb[:, :], masksb[:, 0, :], start=False, stop=True)
                mm.then_inc(s_sc, 1)

            def out_proj(l, b, i, lhs):
                c = b * TB + i
                if c >= 2:
                    pe.wait_ge((s_woe, s_woe1)[l], c - 1)
                for kt in range(KT):
                    mm = pe.matmul(bank(4 + i % 2)[:, 0:D], lhs(kt), wo_sb[:, kt, :],
                                   start=(kt == 0), stop=(kt == KT - 1))
                mm.then_inc(s_wo, 1)

            pe.wait_ge(s_ld, 80)
            pe.wait_ge(s_w0, 128)
            pe.wait_ge(s_const, 1)
            for b in range(B):
                turn_tokens(0, b)
            for b in range(B):
                prepare(0, b)
            for b in range(B):
                pe.wait_ge(s_tev, tcount(0, B - 1, TB - 1))
                pe.wait_ge(s_qkve, NT)
                if b:
                    pe.wait_ge(s_p, MAPS)
                    pe.wait_ge(s_pve, 4)
                    pe.wait_ge(s_ont, TB)
                    pe.wait_ge(s_woe, TB)
                maxima(b)
                for i in range(TB):
                    turn_again(b, i)
                pe.wait_ge(s_rq, (b + 1) * TB)
                attend(0, b)
                pe.wait_ge(s_pve, 4 * (b + 1))
                pe.wait_ge(s_p, MAPS * (b + 1))
                for i in range(TB):
                    c = b * TB + i
                    if c >= 2:
                        pe.wait_ge(s_on, c - 1)
                    for g in range(4):
                        mm = pe.transpose(bank(i % 2)[:, g * P:(g + 1) * P], OT[:, g, i * P:(i + 1) * P], ident[:, :])
                    mm.then_inc(s_otps, 1)
                    pe.wait_ge(s_on, c + 1)
                    if c >= 2:
                        pe.wait_ge(s_ont, c - 1)
                    for kt in range(KT):
                        mm = pe.transpose(bank(2 + i % 2)[:, kt * P:(kt + 1) * P],
                                          XN[:, c, kt * P:(kt + 1) * P], ident[:, :])
                    mm.then_inc(s_ontps, 1)
                    pe.wait_ge(s_ont, c + 1)
                    out_proj(0, b, i, lambda kt: XT[:, b, kt, i * P:(i + 1) * P])

            pe.wait_ge(s_woe, NT)
            for b in range(B):
                turn_tokens(1, b)
            for b in range(B):
                pe.wait_ge(s_xt, 2 + b + 1)
                for i in range(TB):
                    xt = [XT[:, b, kt, i * P:(i + 1) * P] for kt in range(KT)]
                    for kt in range(KT):
                        pe.matmul(bank(4 + 2 * b)[:, i * E0:(i + 1) * E0], xt[kt], wrd_sb[:, kt, 0:E0],
                                  start=(kt == 0), stop=(kt == KT - 1))
                    for kt in range(KT):
                        mm = pe.matmul(bank(5 + 2 * b)[:, i * P:(i + 1) * P], xt[kt], wrd_sb[:, kt, E0:E0 + E0 * I0],
                                       start=(kt == 0), stop=(kt == KT - 1))
                mm.then_inc(s_rd, 1)
            for b in range(B):
                pe.wait_ge(s_aw, b + 1)
                for i in range(TB):
                    mm = pe.transpose(bank(2 * b)[:, i * P:(i + 1) * P], RB[:, i * P:(i + 1) * P], ident[:, :])
                mm.then_inc(s_awps, 1)
                pe.wait_ge(s_awt, b + 1)
                for i in range(TB):
                    mm = pe.matmul(bank(4 + 2 * b + i // 2)[:, i % 2 * D:(i % 2 + 1) * D], RA[:, i * P:(i + 1) * P],
                                   up_sb[:, :], start=True, stop=True)
                mm.then_inc(s_up, 1)

            pe.wait_ge(s_upe, B)
            for b in range(B):
                turn_tokens(2, b)
            pe.wait_ge(s_w1, 16)
            for b in range(B):
                prepare(1, b)
            pe.wait_ge(s_tev, tcount(1, B - 1, TB - 1))
            pe.wait_ge(s_qkve1, NT)
            pe.wait_ge(s_w1o, 16)
            for b in range(B):
                attend(1, b)
            pe.wait_ge(s_pve, 16)
            pe.wait_ge(s_p, 4 * MAPS)
            for b in range(B):
                for i in range(TB):
                    out_proj(1, b, i, lambda kt: XT[:, b, kt, i * P:(i + 1) * P])

            pe.wait_ge(s_woe1, NT)
            for b in range(B):
                turn_tokens(3, b)
            for b in range(B):
                pe.wait_ge(s_xt, 6 + b + 1)
                for i in range(TB):
                    for kt in range(KT):
                        mm = pe.matmul(bank(4 + b)[:, i * E1:(i + 1) * E1], XT[:, b, kt, i * P:(i + 1) * P],
                                       r1_sb[:, kt, :], start=(kt == 0), stop=(kt == KT - 1))
                mm.then_inc(s_rt, 1)
            for b in range(B):
                pe.wait_ge(s_comb, b + 1)
                for i in range(TB):
                    mm = pe.transpose(bank(6 + b)[0:E1, i * P:(i + 1) * P], exl[:, i, :], ident[:, :])
                mm.then_inc(s_cps, 1)

            pe.wait_ge(s_cT, 2)
            pe.wait_ge(s_rte, B)

            def gate_up(n, r, h):
                for part in range(2):
                    for kt in range(KT):
                        w0 = (part * KT + kt) * P
                        mm = pe.matmul(bank(2 * h + part), ringW[:, r, w0:w0 + P], XT[:, h, kt, :],
                                       start=(kt == 0), stop=(kt == KT - 1))
                mm.then_inc(s_gu, 1)

            def down(r, h, start, stop):
                for half in range(2):
                    mm = pe.matmul(bank(4 + 2 * h + half), ringW[:, r, 512 + half * P:512 + (half + 1) * P],
                                   act[:, h, :], start=start, stop=stop, skip_group_check=True)
                mm.then_inc(s_dn, 1)

            def blocks(it, r, first):
                n = RING * it
                for h in range(2):
                    if not (first and r == 0):
                        pe.wait_ge(s_gt, 2 * (n + r) + h - 1)
                    if h == 0:
                        pe.wait_ge(s_wr[r], 48 * it + 48)
                    gate_up(n, r, h)
                if not (first and r == 0):
                    for h in range(2):
                        pe.wait_ge(s_gt, 2 * (n + r) + h - 1)
                        down((r - 1) % RING, h, first and r == 1, False)

            for r in range(RING):
                blocks(0, r, True)
            with pe.Fori(1, PAIRS // RING) as it:
                for r in range(RING):
                    blocks(it, r, False)
            for h in range(2):
                pe.wait_ge(s_gt, 2 * PAIRS - 1 + h)
                down(RING - 1, h, False, True)

            pe.wait_ge(s_yT, 4)
            for c in range(NT):
                for half in range(2):
                    mm = pe.transpose(bank(c // 2)[:, (c % 2) * D + half * P:(c % 2) * D + (half + 1) * P],
                                      OT[:, 2 * (c // TB) + half, c % TB * P:(c % TB + 1) * P], ident[:, :])
                mm.then_inc(s_yps, 1)

        @block.scalar
        def _(sc):
            last = [None, 0]
            counts = {}

            def did(ins, s=None):
                s = s or s_ac
                ins.then_inc(s, 1)
                counts[id(s)] = counts.get(id(s), 0) + 1
                last[:] = [s, counts[id(s)]]

            def settle():
                sc.wait_ge(last[0], last[1])

            def root(src, dst, bias, s):
                did(sc.activation(dst, src, ACT.Ln, bias=bias, scale=1.0))
                settle()
                did(sc.activation(dst, dst, ACT.Exp, scale=-0.5), s)

            def rstd_of(k, b):
                sc.wait_ge(s_var, 2 * k + b + 1)
                t = slice(b * TB, (b + 1) * TB)
                root(mv[:, t, 1], rstd[:, t], eps_sb[:, 0:1], s_rstd)

            def store_xt(k, b):
                sc.wait_ge(s_xtps, 2 * k + b + 1)
                for kt in range(KT):
                    ins = sc.activation(XT[:, b, kt, :], bank(2 * b + kt), ACT.Copy,
                                        scale=rms_sb[:, kt:kt + 1] if k == 0 else 1.0)
                    did(ins, s_xt if kt == KT - 1 else None)

            def store_padded(l, b, i):
                for n, (q, g0) in enumerate(tunits(l)):
                    u = tcount(l, b, i) - len(tunits(l)) + n
                    sc.wait_ge(s_tps, u + 1)
                    dst = (QT if q else KTr)[:, b, g0:g0 + 4, i * P:(i + 1) * P]
                    did(sc.activation(dst, bank(u % 4).rearrange("p (g c) -> p g c", g=4), ACT.Copy), s_tev)

            def exps(l, b):
                for n in range(MAPS):
                    c = (2 * l + b) * MAPS + n
                    sc.wait_ge(s_sc, c + 1)
                    if c >= PSLOTS:
                        sc.wait_ge(s_pv, (c - PSLOTS) // 4 + 1)
                    did(sc.activation(PR[:, c % PSLOTS, :], bank(3 * (n % 2), 3)[:, 0:PW], ACT.Exp,
                                      scale=0.5 if l == 0 else 4.0), s_p)

            sc.preload_act_table_set("natural_log_exp_and_others")
            sc.wait_ge(s_const, 1)
            sc.wait_ge(s_lamd, 1)
            did(sc.activation(lam_sb[:, 2:4], lam_sb[:, 0:2], ACT.Exp), s_lame)
            for b in range(B):
                rstd_of(0, b)
                sc.wait_ge(s_msq, b + 1)
                root(msq[:, b * TB:(b + 1) * TB], rr[:, b * TB:(b + 1) * TB], eps_sb[:, 0:1], s_rr)
            sc.wait_ge(s_w0, 128)
            for b in range(B):
                store_xt(0, b)
            for b in range(B):
                for i in range(TB):
                    store_padded(0, b, i)
            for b in range(B):
                for i in range(TB):
                    sc.wait_ge(s_rqps, b * TB + i + 1)
                    did(sc.activation(QT[:, b, 0:4, i * P:(i + 1) * P],
                                      bank(i).rearrange("p (g c) -> p g c", g=4), ACT.Copy), s_rq)
                exps(0, b)
                for i in range(TB):
                    c = b * TB + i
                    sc.wait_ge(s_ontps, c + 1)
                    did(sc.activation(XT[:, b, :, i * P:(i + 1) * P],
                                      bank(2 + i % 2)[:, 0:D].rearrange("p (k c) -> p k c", k=KT), ACT.Copy), s_ont)
            for b in range(B):
                rstd_of(1, b)
            for b in range(B):
                rstd_of(2, b)
            for b in range(B):
                store_xt(1, b)
            for b in range(B):
                sc.wait_ge(s_lmax, b + 1)
                did(sc.activation(exl[:, :, 0:E0], shl[:, :, 0:E0], ACT.Exp))
                did(sc.activation(RB[:, :], RA[:, :], ACT.Exp, scale=-1.0), s_ex)
                sc.wait_ge(s_awps, b + 1)
                did(sc.activation(RA[:, :], bank(2 * b), ACT.Copy), s_awt)
            for b in range(B):
                rstd_of(3, b)
            for b in range(B):
                rstd_of(4, b)
            for b in range(B):
                store_xt(2, b)
            for b in range(B):
                for i in range(TB):
                    c = b * TB + i
                    sc.wait_ge(s_qkv, NT + c + 1)
                    if c >= 2:
                        sc.wait_ge(s_pad, NT + c - 1)
                    did(sc.activation(QK[:, c % 2, :], bank(4 + i % 2), ACT.Copy))
                    did(sc.activation(V1[:, c, :], bank(6 + i % 2)[:, 0:D], ACT.Copy), s_qkve1)
                    sc.wait_ge(s_ss, c + 1)
                    root(ss[:, c % 2, :], rs1[:, c % 2, :], eps_sb[:, 1:2], s_rs1)
                    store_padded(1, b, i)
            for b in range(B):
                exps(1, b)
            for b in range(B):
                for i in range(TB):
                    c = b * TB + i
                    sc.wait_ge(s_wo, NT + c + 1)
                    did(sc.activation(H[:, c, :], bank(4 + i % 2)[:, 0:D], ACT.Copy, scale=1.0 - LAMBDA_INIT), s_woe1)
            for b in range(B):
                rstd_of(5, b)
            for b in range(B):
                rstd_of(6, b)
            for b in range(B):
                store_xt(3, b)
            for g in range(B):
                sc.wait_ge(s_rte, g + 1)
                did(sc.activation(exl[:, :, :], shl[:, :, :], ACT.Exp), s_rex)
                sc.wait_ge(s_cps, g + 1)
                did(sc.activation(combT[0:E1, g * S:(g + 1) * S], bank(6 + g)[0:E1, :], ACT.Copy), s_cT)

            def silus(it, r):
                n = RING * it
                for h in range(2):
                    sc.wait_ge(s_gu, 2 * (n + r) + h + 1)
                    if isinstance(n, int) and n + r == 0:
                        pass
                    else:
                        sc.wait_ge(s_gt, 2 * (n + r) + h - 1)
                    sc.activation(act2[:, h, :], bank(2 * h), ACT.Silu).then_inc(s_sg, 1)

            for r in range(RING):
                silus(0, r)
            with sc.Fori(1, PAIRS // RING) as it:
                for r in range(RING):
                    silus(it, r)
            sc.wait_ge(s_dn, 2 * PAIRS)
            for k in range(4):
                did(sc.activation(OT[:, k, :], bank(4 + k), ACT.Copy), s_yT)
            for b in range(B):
                rstd_of(7, b)

        @block.vector
        def _(dv):
            last = [None, 0]
            counts = {}

            def did(ins, s=None):
                s = s or s_dv
                ins.then_inc(s, 1)
                counts[id(s)] = counts.get(id(s), 0) + 1
                last[:] = [s, counts[id(s)]]

            def settle():
                dv.wait_ge(last[0], last[1])

            def stats(k, b, src):
                for i in range(TB):
                    did(dv.bn_stats(st[:, b * TB + i, :], src[:, b * TB + i, :]))
                settle()
                for i in range(TB):
                    t = b * TB + i
                    did(dv.bn_aggr(mv[:, t, :], st[:, t, :]), s_var if i == TB - 1 else None)

            def normalise(k, b, src, dst, s=None):
                dv.wait_ge(s_rstd, 2 * k + b + 1)
                for i in range(TB):
                    t = b * TB + i
                    did(dv.tensor_scalar(dst[:, t, :], src[:, t, :], mv[:, t, 0:1], rstd[:, t:t + 1],
                                         ALU.subtract, ALU.mult), s if i == TB - 1 else None)

            def add_norm(k, b):
                normalise(k, b, H, H)
                settle()
                t = slice(b * TB, (b + 1) * TB)
                did(dv.tensor_tensor(X[:, t, :], X[:, t, :], H[:, t, :], ALU.add))
                settle()

            def bc(ap, n):
                return ap.unsqueeze(1).broadcast_to([P, n, ap.shape[-1]])

            dv.wait_ge(s_ld, 80)
            did(dv.tensor_copy(identb[:, :], ident[:, :]))
            did(dv.tensor_copy(masksb[:, :, :], masks[:, :, :]))
            did(dv.memset(ones32[:, :], 1.0))
            did(dv.memset(eps_sb[:, 0:1], EPS))
            did(dv.memset(eps_sb[:, 1:2], HH * RMS_EPS1))
            did(dv.memset(QP0[:, :, :, :], 0.0))
            did(dv.memset(KP0[:, :, :], 0.0))
            did(dv.memset(VA[:, :, :, :], 0.0))
            settle()
            did(dv.memset(VA[:, :, :, HD0:HD0 + 1], 1.0))
            did(dv.memset(KP0[:, :, :].rearrange("p r (h c) -> p r h c", c=32)[:, :, :, 3 * ROT:3 * ROT + 2], 1.0), s_const)
            did(dv.tensor_tensor(lv_sb[:, 0:4:2, :], lv_sb[:, 0:4:2, :], lv_sb[:, 1:4:2, :], ALU.mult))
            settle()
            did(dv.tensor_reduce(lam_sb[:, 0:2], lv_sb[:, 0:4:2, :], AX.X, ALU.add), s_lamd)
            dv.wait_ge(s_lame, 1)
            did(dv.tensor_tensor(lam_sb[:, 0:1], lam_sb[:, 3:4], lam_sb[:, 2:3], ALU.subtract))
            settle()
            did(dv.tensor_scalar(lam_sb[:, 1:2], lam_sb[:, 0:1], -LAMBDA_INIT, None, ALU.add))

            dv.wait_ge(s_x, 32)
            for b in range(B):
                stats(0, b, X)
            for b in range(B):
                t = slice(b * TB, (b + 1) * TB)
                dv.wait_ge(s_rstd, b + 1)
                did(dv.tensor_tensor(msq[:, t], mv[:, t, 1], rstd[:, t], ALU.mult))
                settle()
                did(dv.tensor_tensor(msq[:, t], msq[:, t], rstd[:, t], ALU.mult), s_msq)
                normalise(0, b, X, H)
                dv.wait_ge(s_rr, b + 1)
                settle()
                for i in range(TB):
                    c = b * TB + i
                    did(dv.tensor_scalar(XN[:, c, :], H[:, c, :], rr[:, c:c + 1], None, ALU.mult),
                        s_xn if i == TB - 1 else None)
                dv.wait_ge(s_w0, 128)
                settle()
                did(dv.tensor_tensor(H[:, t, :], H[:, t, :], bc(bo_sb[:, :], TB), ALU.add))
            for b in range(B):
                for i in range(TB):
                    c = b * TB + i
                    dv.wait_ge(s_qkv, c + 1)
                    settle()
                    did(dv.tensor_tensor(VA[:, c, :, 0:HD0], bank(6 + i % 2)[:, 0:D].rearrange("p (h c) -> p h c", c=HD0),
                                         bqkv_sb[:, 2 * D:3 * D].rearrange("p (h c) -> p h c", c=HD0), ALU.add))
                    did(dv.tensor_tensor(QK[:, 0, :], bank(4 + i % 2), bqkv_sb[:, 0:2 * D], ALU.add), s_qkve)
                    settle()
                    pairs = QK[:, 0, :].rearrange("p (h f t) -> p h f t", f=ROT, t=2)
                    ra = RA[:, 0:D].rearrange("p (h f) -> p h f", f=ROT)
                    rb = RB[:, 0:D].rearrange("p (h f) -> p h f", f=ROT)
                    did(dv.tensor_tensor(ra, pairs[:, :, :, 0], bc(rope_sb[:, i, 0, :], 32), ALU.mult))
                    did(dv.tensor_tensor(rb, pairs[:, :, :, 1], bc(rope_sb[:, i, 1, :], 32), ALU.mult))
                    settle()
                    did(dv.tensor_tensor(ra, ra, rb, ALU.add))
                    settle()
                    if c >= 2:
                        dv.wait_ge(s_tps, tcount(0, 0, 0) * (c - 1))
                    qp = QP0[:, b, i, :].rearrange("p (h c) -> p h c", c=32)
                    kp = KP0[:, c % 2, :].rearrange("p (h c) -> p h c", c=32)
                    split_parts(dv, did, settle, qp, kp, ra[:, 0:16, :], ra[:, 16:32, :], ROT)
            for b in range(B):
                for n, (i, u) in enumerate(MUNITS):
                    cnt = b * len(MUNITS) + n
                    dv.wait_ge(s_mps, cnt + 1)
                    nh = MHEADS[i]
                    nk = (i + 1) * P
                    src = bank(2 * (cnt % 4), 2)
                    src = src[:, 0:nh * nk].rearrange("p (h k) -> p h k", h=nh) if i < 2 else \
                        src.rearrange("p (h k) -> p h k", h=2)[:, :, 0:nk]
                    did(dv.tensor_reduce(mx[:, b * TB + i, nh * u:nh * u + nh], src, AX.X, ALU.max), s_mrd)
                    if u == 16 // nh - 1:
                        c = b * TB + i
                        qp = QP0[:, b, i, :].rearrange("p (h c) -> p h c", c=32)
                        settle()
                        qp = qp.rearrange("p (g r) c -> p g r c", r=4)
                        m = mx[:, c, :].rearrange("p (r g) -> p g r", g=4)
                        did(dv.tensor_scalar(qp[:, :, :, 3 * ROT].bitcast(f32r), m, -1.0, None, ALU.mult))
                        settle()
                        did(dv.scalar_tensor_tensor(out=qp[:, :, :, 3 * ROT + 1], in0=m, scalar=-1.0,
                                                    in1=qp[:, :, :, 3 * ROT], op0=ALU.mult, op1=ALU.subtract), s_neg)
                for g in range(4):
                    if b and g == 0:
                        dv.wait_ge(s_otps, TB)
                    dv.wait_ge(s_pv, b * 4 + g + 1)
                    did(dv.tensor_copy(OT[:, g, :], bank(6 + g % 2)), s_pve)
                for i in range(TB):
                    c = b * TB + i
                    dv.wait_ge(s_otps, c + 1)
                    o = bank(i % 2).rearrange("p (h c) -> p h c", c=32)
                    settle()
                    did(dv.reciprocal(den[:, :], o[:, :, HD0]))
                    settle()
                    did(dv.tensor_tensor(XN[:, c, :].rearrange("p (h c) -> p h c", c=HD0), o[:, :, 0:HD0],
                                         den[:, :].unsqueeze(2).broadcast_to([P, HEADS0, HD0]), ALU.mult), s_on)
                    dv.wait_ge(s_wo, c + 1)
                    did(dv.tensor_tensor(H[:, c, :], H[:, c, :], bank(4 + i % 2)[:, 0:D], ALU.add), s_woe)
            settle()
            for b in range(B):
                stats(1, b, H)
            for b in range(B):
                add_norm(1, b)
                stats(2, b, X)
            for b in range(B):
                normalise(2, b, X, XN, s_xn)
            def choose(b, E, k, lg, bias):
                src = lgs[:, :, 0:E]
                did(dv.tensor_reduce(red[:, 0:TB], lg, AX.X, ALU.max))
                if bias is not None:
                    did(dv.tensor_tensor(src, lg, bias, ALU.add))
                else:
                    did(dv.tensor_copy(src, lg))
                settle()
                did(dv.tensor_tensor(shl[:, :, 0:E], lg, red[:, 0:TB].unsqueeze(2).broadcast_to([P, TB, E]), ALU.subtract))
                for i in range(TB):
                    did(dv.max(top[:, i, :], lgs[:, i, 0:E]))
                settle()
                for i in range(TB):
                    did(dv.max_index(idx[:, i, :], top[:, i, :], lgs[:, i, 0:E]))
                settle()
                did(dv.tensor_copy(idxf[:, :, :], idx[:, :, :]))
                for n in range(k):
                    settle()
                    did(dv.tensor_tensor((oh if n == 0 else oh2)[:, :, 0:E], bc(iota_f[:, 0:E], TB),
                                         idxf[:, :, n].unsqueeze(2).broadcast_to([P, TB, E]), ALU.is_equal))
                    if n:
                        settle()
                        did(dv.tensor_tensor(oh[:, :, 0:E], oh[:, :, 0:E], oh2[:, :, 0:E], ALU.add))

            dv.wait_ge(s_pool, 1)
            for b in range(B):
                dv.wait_ge(s_rd, b + 1)
                if b:
                    dv.wait_ge(s_up, b)
                lg = bank(4 + 2 * b)[:, 0:TB * E0].rearrange("p (i e) -> p i e", e=E0)
                settle()
                did(dv.tensor_copy(RA[:, :], bank(5 + 2 * b)))
                choose(b, E0, 2, lg, None)
                did(dv.memset(red[:, TB:2 * TB], 0.0), s_lmax)
                dv.wait_ge(s_ex, b + 1)
                settle()
                did(dv.tensor_reduce(red[:, 0:TB], exl[:, :, 0:E0], AX.X, ALU.add))
                did(dv.tensor_tensor(oh[:, :, 0:E0], oh[:, :, 0:E0], exl[:, :, 0:E0], ALU.mult))
                did(dv.tensor_scalar(RB[:, :], RB[:, :], 1.0, None, ALU.add))
                settle()
                did(dv.reciprocal(red[:, TB:2 * TB], red[:, 0:TB]))
                did(dv.reciprocal(RB[:, :], RB[:, :]))
                settle()
                did(dv.tensor_tensor(oh[:, :, 0:E0], oh[:, :, 0:E0],
                                     red[:, TB:2 * TB].unsqueeze(2).broadcast_to([P, TB, E0]), ALU.mult))
                did(dv.tensor_tensor(RB[:, :], RB[:, :], RA[:, :], ALU.mult))
                settle()
                for i in range(TB):
                    v = RB[:, i * P:(i + 1) * P].rearrange("p (e i) -> p e i", i=I0)
                    did(dv.tensor_tensor(v, v, oh[:, i, 0:E0].unsqueeze(2).broadcast_to([P, E0, I0]), ALU.mult),
                        s_aw if i == TB - 1 else None)
                dv.wait_ge(s_up, b + 1)
                did(dv.tensor_copy(H[:, b * TB:(b + 1) * TB, :].rearrange("p t c -> p (t c)"), bank(4 + 2 * b, 2)), s_upe)
            settle()
            for b in range(B):
                stats(3, b, H)
            for b in range(B):
                add_norm(3, b)
                stats(4, b, X)
            for b in range(B):
                normalise(4, b, X, XN, s_xn)
            did(dv.memset(QP0[:, :, :, :], 0.0))
            for b in range(B):
                for i in range(TB):
                    c = b * TB + i
                    dv.wait_ge(s_qkve1, c + 1)
                    settle()
                    q16 = QK[:, c % 2, :].rearrange("p (m d) -> p m d", d=HH)
                    did(dv.tensor_tensor(RA[:, :], QK[:, c % 2, :], QK[:, c % 2, :], ALU.mult))
                    settle()
                    did(dv.tensor_reduce(ss[:, c % 2, :], RA[:, :].rearrange("p (m d) -> p m d", d=HH), AX.X, ALU.add), s_ss)
                    dv.wait_ge(s_rs1, c + 1)
                    did(dv.tensor_tensor(q16, q16, rs1[:, c % 2, :].unsqueeze(2).broadcast_to([P, 32, HH]), ALU.mult))
                    settle()
                    if c >= 2:
                        dv.wait_ge(s_tps, 2 * NT + 4 * (c - 1))
                    qp = QKP1[:, c % 2, 1, :].rearrange("p (h c) -> p h c", c=64)
                    kp = QKP1[:, c % 2, 0, :].rearrange("p (h c) -> p h c", c=64)
                    split_parts(dv, did, settle, qp, kp, q16[:, 0:16, :], q16[:, 16:32, :], HH)
            for b in range(B):
                for q in range(4):
                    dv.wait_ge(s_pv, 8 + b * 4 + q + 1)
                    G, half = q // 2, q % 2
                    settle()
                    did(dv.reciprocal(NA[:, :], bank(7)))
                    settle()
                    if half == 0:
                        did(dv.tensor_tensor(XT[:, b, G, :], bank(6), NA[:, :], ALU.mult), s_pve)
                    else:
                        did(dv.scalar_tensor_tensor(out=NB[:, :], in0=bank(6), scalar=lam_sb[:, 1:2], in1=NA[:, :],
                                                    op0=ALU.mult, op1=ALU.mult))
                        settle()
                        did(dv.tensor_tensor(XT[:, b, G, :], XT[:, b, G, :], NB[:, :], ALU.add), s_pve)
            for b in range(B):
                dv.wait_ge(s_woe1, (b + 1) * TB)
                stats(5, b, H)
            for b in range(B):
                add_norm(5, b)
                stats(6, b, X)
            for b in range(B):
                normalise(6, b, X, XN, s_xn)
            for b in range(B):
                dv.wait_ge(s_rt, b + 1)
                if b:
                    dv.wait_ge(s_cps, b)
                lg = bank(4 + b)[:, 0:TB * E1].rearrange("p (i e) -> p i e", e=E1)
                settle()
                choose(b, E1, TOPK1, lg, bc(rb_sb[:, :], TB))
                did(dv.memset(red[:, TB:2 * TB], 0.0), s_rte)
                dv.wait_ge(s_rex, b + 1)
                settle()
                did(dv.tensor_tensor(oh[:, :, :], oh[:, :, :], exl[:, :, :], ALU.mult))
                settle()
                did(dv.tensor_reduce(red[:, 0:TB], oh[:, :, :], AX.X, ALU.add))
                settle()
                did(dv.reciprocal(red[:, TB:2 * TB], red[:, 0:TB]))
                settle()
                did(dv.tensor_tensor(exl[:, :, :], oh[:, :, :],
                                     red[:, TB:2 * TB].unsqueeze(2).broadcast_to([P, TB, E1]), ALU.mult), s_comb)
            did(dv.memset(H[:, 0:4, :], 1.0), s_ones)

            def gated(it, r):
                n = RING * it
                for h in range(2):
                    if h == 0:
                        dv.wait_ge(s_wr[r], 48 * it + 48)
                    dv.wait_ge(s_sg, 2 * (n + r) + h + 1)
                    dv.tensor_tensor(act2[:, h, :], act2[:, h, :], combB[:, r, h * S:(h + 1) * S], ALU.mult).then_inc(s_g1, 1)
                    dv.wait_ge(s_g1, 2 * (n + r) + h + 1)
                    if not (isinstance(n, int) and n + r == 0):
                        dv.wait_ge(s_dn, 2 * (n + r) + h - 1)
                    dv.tensor_tensor(act[:, h, :], act2[:, h, :], bank(2 * h + 1), ALU.mult).then_inc(s_gt, 1)

            for r in range(RING):
                gated(0, r)
            with dv.Fori(1, PAIRS // RING) as it:
                for r in range(RING):
                    gated(it, r)
            for c in range(0, NT, 2):
                dv.wait_ge(s_yps, c + 2)
                did(dv.tensor_copy(H[:, c:c + 2, :].rearrange("p t c -> p (t c)"), bank(c // 2)))
            settle()
            for b in range(B):
                stats(7, b, H)
            for b in range(B):
                normalise(7, b, H, H)
                settle()
                t = slice(b * TB, (b + 1) * TB)
                did(dv.tensor_tensor(X[:, t, :], X[:, t, :], H[:, t, :], ALU.add), s_fin)


_ORDER = ["x", "rms_w", "wqkv0", "bqkv0", "wo0", "bo0", "wrd0", "up0", "wqkv1", "wo1", "lvec", "router1", "rbias1",
          "wmoe", "rope", "ident_in", "mask_in"]


def constants():
    j = np.arange(ROT, dtype=np.float32)
    freqs = (10000.0 ** (j.astype(np.float64) * (-2.0 / HD0))).astype(np.float32)
    ang = (np.arange(S, dtype=np.float32)[:, None] * freqs[None, :]).astype(np.float64)
    cos, sin = np.cos(ang), np.sin(ang)
    even = (np.arange(ROT) % 2 == 0)[None, :]
    rope = np.stack([np.where(even, cos, sin), np.where(even, -sin, cos), cos, sin], axis=1).astype(np.float32)
    rope = np.ascontiguousarray(rope.reshape(TB, P, 4, ROT).transpose(1, 0, 2, 3))
    a = np.arange(P)
    keyq = np.where(a[None, :] >= a[:, None], 0.0, NEG).astype(np.float32)
    return {"rope": rope, "ident_in": np.eye(P, dtype=np.float32),
            "mask_in": np.ascontiguousarray(np.stack([keyq, keyq.T], axis=1))}


def layouts(a):
    c = np.ascontiguousarray
    wg, wu, wd = a["L1_ffn_wg"], a["L1_ffn_wu"], a["L1_ffn_wd"]

    def inner(w):
        return w.reshape(E1 // 2, 2, KT, P, F1).transpose(0, 3, 2, 1, 4).reshape(E1 // 2, P, KT * P)

    def shared(w):
        return w.reshape(SH, KT, P, HS // P, P).transpose(0, 3, 2, 1, 4).reshape(SH * HS // P, P, KT * P)

    gate = np.concatenate([inner(wg), shared(a["L1_ffn_swg"])])
    up = np.concatenate([inner(wu), shared(a["L1_ffn_swu"])])
    down = np.concatenate([wd.reshape(E1 // 2, P, D), a["L1_ffn_swd"].reshape(SH * HS // P, P, D)])
    return {
        "x": c(a["L0_attn_x"].reshape(TOK, D)),
        "rms_w": c(a["L0_attn_rms_w"].reshape(KT, P).T),
        "wqkv0": c(np.concatenate([a["L0_attn_wq"], a["L0_attn_wk"], a["L0_attn_wv"]], axis=1)),
        "bqkv0": c(np.concatenate([a["L0_attn_bq"], a["L0_attn_bk"], a["L0_attn_bv"]])),
        "wo0": c(a["L0_attn_wo"]), "bo0": c(a["L0_attn_bo"]),
        "wrd0": c(np.concatenate([a["L0_ffn_router_w"].T, a["L0_ffn_down_w"].reshape(E0 * I0, D).T], axis=1)),
        "up0": c(a["L0_ffn_up_w"].transpose(0, 2, 1).reshape(E0 * I0, D)),
        "wqkv1": c(np.concatenate([a["L1_attn_wq"].T, a["L1_attn_wk"].T, a["L1_attn_wv"].T], axis=1)),
        "wo1": c(a["L1_attn_wo"].T),
        "lvec": c(np.concatenate([a["L1_attn_lq1"], a["L1_attn_lk1"], a["L1_attn_lq2"], a["L1_attn_lk2"]])),
        "router1": c(a["L1_ffn_router_w"]), "rbias1": c(a["L1_ffn_router_bias"]),
        "wmoe": c(np.concatenate([gate, up, down], axis=2)),
    }


def kernel(**inputs):
    import concourse.bacc as bacc
    from concourse.bass_utils import run_bass_kernel_spmd

    arrays = {**layouts({k: np.asarray(v) for k, v in inputs.items()}), **constants()}
    nc = bacc.Bacc("TRN2", target_bir_lowering=False, num_devices=1)
    aps = [nc.dram_tensor(f"in_{n}", arrays[n].shape, mybir.dt.float32, kind="ExternalInput").ap() for n in _ORDER]
    out = nc.dram_tensor("out_x", (TOK, D), mybir.dt.float32, kind="ExternalOutput").ap()
    comb_dram = nc.dram_tensor("comb_rows", (2 * PAIRS, TOK), mybir.dt.float32).ap()
    build(nc, *aps, out, comb_dram)
    r = run_bass_kernel_spmd(nc, [{f"in_{n}": arrays[n] for n in _ORDER}], core_ids=[0])
    return r.results[0]["out_x"].reshape(B, S, D)
```

```python
import math
from contextlib import ExitStack

import numpy as np

import concourse.bass as bass
from concourse import mybir

P = 128
B, S, D = 2, 512, 256
TOK = B * S
NT = TOK // P
TB = S // P
KT = D // P
HEADS0, HD0 = 16, 16
ROT = HD0 // 2
MAPS = 16
HEADS1, HD1 = 8, 32
HH = HD1 // 2
E0, I0 = 8, 16
E1, F1, TOPK1 = 64, 64, 4
SH, HS = 2, 256
EPS = 1e-5
RMS_EPS1 = 1.1920929e-07
LAMBDA_INIT = 0.2
NEG = -1.0e30

SLOT = (32, 64)
DH = (ROT, HH)
GROUPS = (4, 8)
PCOL = [0, 512, 1024, 896]
PW = 1280
PSLOTS = 6
NSB = SH * HS // P
NTILE = -(-(TOK * TOPK1 + E1 * (P - 1)) // P // 8) * 8
U = 8
LAG_GU, LAG_TA, LAG_D = 1, 3, 5
NBODY = NTILE // U
MAGIC = 12582912.0


def build(nc, x, rms_w, wqkv0, bqkv0, wo0, bo0, wrd0, up0, wqkv1, wo1, lvec, router1, rbias1, wgu1, wd1,
          wsgu, wsd, rope, ident_in, mask_in, before_in, out, h_dram, y_dram):
    f32, f32r, bf16, f16 = mybir.dt.float32, mybir.dt.float32r, mybir.dt.bfloat16, mybir.dt.float16
    u32, i32 = mybir.dt.uint32, mybir.dt.int32
    ALU, ACT, AX = mybir.AluOpType, mybir.ActivationFunctionType, mybir.AxisListType

    ctx = ExitStack()
    with ctx:
        def sb(name, shape, dt=f32):
            return ctx.enter_context(nc.sbuf_tensor(name, shape, dt))

        def at(name, offset, shape, dt):
            return nc.alloc_sbuf_tensor_at(name, shape, dt, offset=offset)

        def sem(name):
            return ctx.enter_context(nc.semaphore(name))

        X = sb("X", [P, NT, D])
        H = sb("H", [P, NT, D])
        XN = sb("XN", [P, NT, D])
        XT = sb("XT", [P, B, KT, S])
        XTall = XT[:, :, :, :]
        QK = sb("QK", [P, 2, 2 * D])
        RA = sb("RA", [P, 2 * D])
        RB = sb("RB", [P, 2 * D])
        QP0 = sb("QP0", [P, B, TB, 2 * D])
        KP0 = sb("KP0", [P, 2, 2 * D])
        QKP1 = QP0[:, :, :, :].rearrange("p b t c -> p b (t c)").rearrange(
            "p r (a c) -> p r a c", a=2)
        arena = sb("arena", [P, 3 * 8192])
        base = nc.lookup_mloc(arena).addr
        QT = at("QT", base, [P, B, 8, S], f32r)
        KTr = at("KTr", base + 4 * 8192, [P, B, 8, S], f32r)
        PR = at("PR", base + 8 * 8192, [P, PSLOTS, PW], f32)
        WGU = arena[:, 0:E1 * KT * P]
        WD = arena[:, E1 * KT * P:E1 * KT * P + E1 // 2 * D]
        VA = sb("VA", [P, NT, HEADS0, 32])
        V1 = VA[:, :, :, :].rearrange("p t h c -> p t (h c)")[:, :, 0:D]
        OT = sb("OT", [P, 4, S])
        ones32 = sb("ones32", [P, 32])
        ident = sb("ident", [P, P])
        identb = sb("identb", [P, P], bf16)
        masksb = sb("masksb", [P, 2, P], bf16)
        rope_sb = sb("rope_sb", [P, TB, 4, ROT])
        wq_sb = sb("wq_sb", [P, KT, 3 * D])
        wo_sb = sb("wo_sb", [P, KT, D])
        bqkv_sb = sb("bqkv_sb", [P, 3 * D])
        bo_sb = sb("bo_sb", [P, D])
        rms_sb = sb("rms_sb", [P, KT])
        wrd_sb = sb("wrd_sb", [P, KT, E0 + E0 * I0])
        up_sb = sb("up_sb", [P, D])
        lv_sb = sb("lv_sb", [P, 4, HD1])
        lam_sb = sb("lam_sb", [P, 4])
        r1_sb = sb("r1_sb", [P, KT, E1])
        rb_sb = sb("rb_sb", [P, E1])
        iota_f = sb("iota_f", [P, E1])
        st = sb("st", [P, NT, 6])
        mv = sb("mv", [P, NT, 2])
        lnv = sb("lnv", [P, NT])
        rstd = sb("rstd", [P, NT])
        msq = sb("msq", [P, NT])
        rr = sb("rr", [P, NT])
        mx = sb("mx", [P, NT, HEADS0])
        ss = sb("ss", [P, 2, 32])
        rs1 = sb("rs1", [P, 2, 32])
        den = sb("den", [P, HEADS0])
        lgs = sb("lgs", [P, TB, E1])
        shl = sb("shl", [P, TB, E1])
        exl = sb("exl", [P, TB, E1])
        oh = sb("oh", [P, TB, E0])
        oh2 = sb("oh2", [P, TB, E0])
        top = sb("top", [P, TB, 8])
        idx = sb("idx", [P, TB, 8], u32)
        idxf = sb("idxf", [P, TB, 8])
        red = sb("red", [P, 2 * TB])
        eps_sb = sb("eps_sb", [P, 2])
        NA, NB = RA, RB
        q0 = QP0[:, :, :, :].rearrange("p b t c -> p (b t c)")
        XG = q0[:, 0:U * D].rearrange("p (r c) -> p r c", r=U)
        XGT = q0[:, U * D:U * D + 4 * D].rearrange("p (r c) -> p r c", r=4)
        Y = q0[:, U * D + 4 * D:U * D + 8 * D].rearrange("p (r c) -> p r c", r=4)
        kf = KP0[:, :, :].rearrange("p r c -> p (r c)")
        A = kf[:, 0:4 * P].rearrange("p (r c) -> p r c", r=4)
        AT = kf[:, 4 * P:8 * P].rearrange("p (r c) -> p r c", r=4)
        SG = up_sb[:, :].rearrange("p (r c) -> p r c", r=4)
        vf = VA[:, :, :, :].rearrange("p t h c -> p (t h c)")
        OH = vf[:, 0:NT * TOPK1 * E1].rearrange("p (t k e) -> p t k e", t=NT, k=TOPK1)
        PRD = vf[:, NT * TOPK1 * E1:2 * NT * TOPK1 * E1].rearrange("p (t k e) -> p t k e", t=NT, k=TOPK1)
        NC = NT * TOPK1
        LO1 = vf[:, NC * E1:2 * NC * E1].bitcast(f16).rearrange("p (n c) -> p n c", n=NC)
        HI1 = wq_sb[:, :, :].rearrange("p k c -> p (k c)").bitcast(f16).rearrange(
            "p (n c) -> p n c", n=NC)
        WSGU = H[:, :, :].rearrange("p t c -> p (t c)").rearrange("p (n c) -> p n c", n=NSB)
        WSD = QK[:, :, :].rearrange("p a c -> p (a c)").rearrange("p (n c) -> p n c", n=NSB)
        SACT = [OT[:, 2 * (n % 2):2 * (n % 2) + 2, :].rearrange("p a c -> p (a c)") if n < 2 else
                XN[:, 4 * (n % 2):4 * (n % 2) + 4, :].rearrange("p a c -> p (a c)") for n in range(NSB)]
        MKF = kf[:, 4 * P:8 * P].rearrange("p (t e) -> p t e", e=E1)
        MK = sb("MK", [P, NT, E1], bf16)
        before = sb("before", [P, P], bf16)
        onesb = sb("onesb", [P, P], bf16)
        ones64 = sb("ones64", [P, E1])
        iota16 = sb("iota16", [P, P], f16)
        iotaf = RA[:, P:2 * P]
        tokid = sb("tokid", [P, NT])
        tile_no = sb("tile_no", [P, 1])
        tcnt = bqkv_sb[:, 0:4 * E1].rearrange("p (a e) -> p a e", a=4)
        slotf = sb("slotf", [P, NC])
        hi = sb("hi", [P, NC])
        lo = sb("lo", [P, NC])
        wk = sb("wk", [P, NC])
        wsum = sb("wsum", [P, 2 * NT])
        slotu = sb("slotu", [P, NC], u32)
        tok_of = sb("tok_of", [P, NTILE], u32)
        ecol = sb("ecol", [P, 2])
        ediag = sb("ediag", [P, P], bf16)
        erow = bqkv_sb[:, 4 * E1:4 * E1 + 2 * NTILE].rearrange("p (a t) -> p a t", a=2)
        odd = sb("odd", [P, 2, NTILE])
        TABG = sb("TABG", [1, NTILE + 2 * U], i32)
        TABW = sb("TABW", [1, NTILE + 2 * U], i32)

        PSUM = ctx.enter_context(nc.psum_tensor("PSUM", [P, 8, 512], f32))

        def bank(n, k=1):
            return PSUM[:, n:n + k, :].rearrange("p a c -> p (a c)")

        s_ld = sem("s_ld")
        s_x = sem("s_x")
        s_w0 = sem("s_w0")
        s_w1 = sem("s_w1")
        s_w1o = sem("s_w1o")
        s_dv = sem("s_dv")
        s_ac = sem("s_ac")
        s_pool = sem("s_pool")
        s_const = sem("s_const")
        s_var = sem("s_var")
        s_rstd = sem("s_rstd")
        s_msq = sem("s_msq")
        s_rr = sem("s_rr")
        s_xn = sem("s_xn")
        s_xtps = sem("s_xtps")
        s_xt = sem("s_xt")
        s_qkv = sem("s_qkv")
        s_qkve = sem("s_qkve")
        s_ss = sem("s_ss")
        s_rs1 = sem("s_rs1")
        s_pad = sem("s_pad")
        s_tps = sem("s_tps")
        s_tev = sem("s_tev")
        s_mps = sem("s_mps")
        s_mrd = sem("s_mrd")
        s_neg = sem("s_neg")
        s_rqps = sem("s_rqps")
        s_rq = sem("s_rq")
        s_sc = sem("s_sc")
        s_p = sem("s_p")
        s_pv = sem("s_pv")
        s_pve = sem("s_pve")
        s_otps = sem("s_otps")
        s_on = sem("s_on")
        s_ontps = sem("s_ontps")
        s_ont = sem("s_ont")
        s_wo = sem("s_wo")
        s_woe = sem("s_woe")
        s_qkve1 = sem("s_qkve1")
        s_woe1 = sem("s_woe1")
        s_rd = sem("s_rd")
        s_lmax = sem("s_lmax")
        s_ex = sem("s_ex")
        s_aw = sem("s_aw")
        s_awps = sem("s_awps")
        s_awt = sem("s_awt")
        s_up = sem("s_up")
        s_upe = sem("s_upe")
        s_lamd = sem("s_lamd")
        s_lame = sem("s_lame")
        s_rt = sem("s_rt")
        s_rte = sem("s_rte")
        s_rex = sem("s_rex")
        s_oh = sem("s_oh")
        s_rank = sem("s_rank")
        s_ediag = sem("s_ediag")
        s_eps = sem("s_eps")
        s_hot = sem("s_hot")
        s_tok = sem("s_tok")
        s_idx = sem("s_idx")
        s_hd = sem("s_hd")
        s_wgu = sem("s_wgu")
        s_wd = sem("s_wd")
        s_ws = sem("s_ws")
        s_gu = sem("s_gu")
        s_sg = sem("s_sg")
        s_gt = sem("s_gt")
        s_gx = [sem(f"s_gx{r}") for r in range(U)]
        s_tx = sem("s_tx")
        s_xe = sem("s_xe")
        s_gup = sem("s_gup")
        s_sgs = sem("s_sgs")
        s_a = sem("s_a")
        s_ta = sem("s_ta")
        s_ate = sem("s_ate")
        s_d = sem("s_d")
        s_ye = sem("s_ye")
        s_st = [sem(f"s_st{r}") for r in range(4)]
        s_yg = [sem(f"s_yg{r}") for r in range(U)]
        s_sd = sem("s_sd")
        s_mx = sem("s_mx")
        s_fin = sem("s_fin")
        s_out = sem("s_out")

        block = ctx.enter_context(nc.Block())

        def slot(l, m):
            per = P // SLOT[l]
            return m // per, SLOT[l] * (m % per)

        def tunits(l):
            return [(a, 4 * n) for a in (0, 1) for n in range(GROUPS[l] // 4)]

        MUNITS = [(i, u) for i in range(TB) for u in range((2, 4, 8, 8)[i])]
        MHEADS = (8, 4, 2, 2)
        NTU = 2

        def tcount(l, b, i):
            n = b * TB + i + 1
            return 2 * n if l == 0 else 2 * NT + 4 * n

        def split_parts(dv, did, settle, qp, kp, rq, rk, d):
            did(dv.tensor_copy(qp[:, :, 0:d].bitcast(f32r), rq))
            did(dv.tensor_copy(kp[:, :, 0:d].bitcast(f32r), rk))
            settle()
            did(dv.tensor_copy(qp[:, :, d:2 * d], qp[:, :, 0:d]))
            did(dv.tensor_copy(kp[:, :, 2 * d:3 * d], kp[:, :, 0:d]))
            did(dv.tensor_tensor(qp[:, :, 2 * d:3 * d], rq, qp[:, :, 0:d], ALU.subtract))
            did(dv.tensor_tensor(kp[:, :, d:2 * d], rk, kp[:, :, 0:d], ALU.subtract), s_pad)

        @block.sync
        def _(sp):
            sp.dma_start(X[:, 0:TB, :], x[0:S, :].rearrange("(t p) d -> p t d", p=P)).then_inc(s_x, 16)
            sp.dma_start(ident[:, :], ident_in).then_inc(s_ld, 16)
            sp.dma_start(RB[:, 0:2 * P].rearrange("p (a c) -> p a c", a=2), mask_in).then_inc(s_ld, 16)
            sp.dma_start(RA[:, 0:P], before_in).then_inc(s_ld, 16)
            sp.dma_start(X[:, TB:NT, :], x[S:TOK, :].rearrange("(t p) d -> p t d", p=P)).then_inc(s_x, 16)
            sp.dma_start(rms_sb[:, :], rms_w).then_inc(s_w0, 16)
            sp.dma_start(wq_sb[:, :, :], wqkv0.rearrange("(k p) n -> p k n", p=P)).then_inc(s_w0, 16)
            sp.dma_start(bqkv_sb[:, :], bqkv0.partition_broadcast(P)).then_inc(s_w0, 16)
            sp.dma_start(rope_sb[:, :, :, :], rope).then_inc(s_w0, 16)
            sp.dma_start(bo_sb[:, :], bo0.partition_broadcast(P)).then_inc(s_w0, 16)
            sp.dma_start(wo_sb[:, :, :], wo0.rearrange("(k p) n -> p k n", p=P)).then_inc(s_w0, 16)
            sp.dma_start(wrd_sb[:, :, :], wrd0.rearrange("(k p) n -> p k n", p=P)).then_inc(s_w0, 16)
            sp.dma_start(up_sb[:, :], up0).then_inc(s_w0, 16)
            sp.dma_start(lv_sb[:, :, :].rearrange("p a c -> p (a c)"), lvec.partition_broadcast(P)).then_inc(s_ld, 16)
            sp.dma_start(r1_sb[:, :, :], router1.rearrange("(k p) n -> p k n", p=P)).then_inc(s_ld, 16)
            sp.dma_start(rb_sb[:, :], rbias1.partition_broadcast(P)).then_inc(s_ld, 16)
            sp.wait_ge(s_qkv, NT)
            sp.dma_start(wq_sb[:, :, :], wqkv1.rearrange("(k p) n -> p k n", p=P)).then_inc(s_w1, 16)
            sp.wait_ge(s_wo, NT)
            sp.dma_start(wo_sb[:, :, :], wo1.rearrange("(k p) n -> p k n", p=P)).then_inc(s_w1o, 16)
            sp.wait_ge(s_pv, 16)
            for n in range(4):
                e = slice(16 * n, 16 * (n + 1))
                sp.dma_start(WGU[:, n * 4096:(n + 1) * 4096].rearrange("p (e c) -> p e c", e=16),
                             wgu1[e, :, :].rearrange("e p c -> p e c")).then_inc(s_wgu, 16)
            sp.wait_ge(s_xn, 7)
            sp.dma_start(h_dram[0:S, :].rearrange("(t p) d -> p t d", p=P), XN[:, 0:TB, :]).then_inc(s_hd, 16)
            sp.wait_ge(s_xn, 8)
            sp.dma_start(WSGU, wsgu.rearrange("n p c -> p n c")).then_inc(s_ws, 16)
            sp.dma_start(WSD, wsd.rearrange("n p c -> p n c")).then_inc(s_ws, 16)
            sp.dma_start(h_dram[S:TOK, :].rearrange("(t p) d -> p t d", p=P), XN[:, TB:NT, :]).then_inc(s_hd, 16)
            for n in range(2):
                sp.dma_start(WD[:, n * 4096:(n + 1) * 4096].rearrange("p (e c) -> p e c", e=16),
                             wd1[16 * n:16 * (n + 1), :, :].rearrange("e p c -> p e c")).then_inc(s_wd, 16)

            def store(i, m, row):
                sp.wait_ge(s_ye, i + 1)
                sp.dma_start(row, Y[:, m % 4, :]).then_inc(s_st[m % 4], 16)

            y_rows = y_dram.rearrange("(j m p) d -> j m p d", m=U, p=P)
            with sp.Fori(0, NBODY) as j:
                for m in range(U):
                    store(U * j + m, m, y_rows[bass.ds(j, 1), m].rearrange("a p d -> (a p) d"))
            sp.wait_ge(s_fin, 1)
            sp.dma_start(out[0:S, :].rearrange("(t p) d -> p t d", p=P), X[:, 0:TB, :]).then_inc(s_out, 16)
            sp.wait_ge(s_fin, 2)
            sp.dma_start(out[S:TOK, :].rearrange("(t p) d -> p t d", p=P), X[:, TB:NT, :]).then_inc(s_out, 16)
            sp.wait_ge(s_out, 32)

        @block.gpsimd
        def _(pool):
            pool.iota(iota_f[:, :], [[1, E1]], base=0, channel_multiplier=0,
                      allow_small_or_imprecise_dtypes=True).then_inc(s_pool, 1)
            pool.iota(iotaf[:, :], [[1, P]], base=0, channel_multiplier=0,
                      allow_small_or_imprecise_dtypes=True).then_inc(s_pool, 1)
            pool.iota(tokid[:, :], [[P, NT]], base=0, channel_multiplier=1,
                      allow_small_or_imprecise_dtypes=True).then_inc(s_pool, 1)
            pool.iota(tile_no[:, :], [[1, 1]], base=0, channel_multiplier=1,
                      allow_small_or_imprecise_dtypes=True).then_inc(s_pool, 1)
            def shared_gate(n):
                for h in range(2):
                    pool.wait_ge(s_sg, 2 * n + h + 1)
                    sact = SACT[n][:, h * S:(h + 1) * S]
                    pool.tensor_tensor(sact, sact, (RA, RB)[h][:, :], ALU.mult).then_inc(s_gt, 1)

            for n in range(NSB - 1):
                shared_gate(n)
            pool.wait_ge(s_hd, 32)
            pool.wait_ge(s_idx, 1)
            for i in range(NTILE):
                if i == U:
                    shared_gate(NSB - 1)
                if i >= U:
                    pool.wait_ge(s_tx, i - U + 1)
                pool.indirect_dma_start(out=XG[:, i % U, :], out_offset=None, in_=h_dram,
                                        in_offset=bass.IndirectOffsetOnAxis(ap=tok_of[:, i:i + 1], axis=0)
                                        ).then_inc(s_gx[i % U], 16)
            pool.wait_ge(s_tx, NTILE)
            for r in range(4):
                pool.wait_ge(s_st[r], 16 * NTILE // 4)
            for n in range(NC):
                if n >= U:
                    pool.wait_ge(s_mx, n - U + 1)
                pool.indirect_dma_start(out=XG[:, n % U, :], out_offset=None, in_=y_dram,
                                        in_offset=bass.IndirectOffsetOnAxis(ap=slotu[:, n:n + 1], axis=0)
                                        ).then_inc(s_yg[n % U], 16)

        @block.tensor
        def _(pe):
            def turn_tokens(k, b):
                pe.wait_ge(s_xn, 2 * k + b + 1)
                for kt in range(KT):
                    for i in range(TB):
                        mm = pe.transpose(bank(2 * b + kt)[:, i * P:(i + 1) * P],
                                          XN[:, b * TB + i, kt * P:(kt + 1) * P], ident[:, :])
                mm.then_inc(s_xtps, 1)

            def project(l, b, i):
                c = b * TB + i
                if c >= 2:
                    pe.wait_ge((s_qkve, s_qkve1)[l], c - 1)
                for kt in range(KT):
                    pe.matmul(bank(4 + i % 2), XT[:, b, kt, i * P:(i + 1) * P], wq_sb[:, kt, 0:2 * D],
                              start=(kt == 0), stop=(kt == KT - 1))
                for kt in range(KT):
                    mm = pe.matmul(bank(6 + i % 2)[:, 0:D], XT[:, b, kt, i * P:(i + 1) * P],
                                   wq_sb[:, kt, 2 * D:3 * D], start=(kt == 0), stop=(kt == KT - 1))
                mm.then_inc(s_qkv, 1)

            def turn_padded(l, b, i):
                c = b * TB + i
                pe.wait_ge(s_pad, l * NT + c + 1)
                for n, (q, g0) in enumerate(tunits(l)):
                    u = tcount(l, b, i) - len(tunits(l)) + n
                    if u >= 4:
                        pe.wait_ge(s_tev, u - 3)
                    for g in range(4):
                        if l == 0:
                            src = (QP0[:, b, i, :] if q else KP0[:, c % 2, :])
                        else:
                            src = QKP1[:, c % 2, q, :]
                        mm = pe.transpose(bank(u % 4)[:, g * P:(g + 1) * P],
                                          src[:, (g0 + g) * P:(g0 + g + 1) * P], ident[:, :])
                    mm.then_inc(s_tps, 1)

            def prepare(l, b):
                pe.wait_ge(s_xt, 4 * l + 2)
                for i in range(TB):
                    project(l, b, i)
                    if i >= 1:
                        turn_padded(l, b, i - 1)
                turn_padded(l, b, TB - 1)

            def maxima(b):
                for m, (i, u) in enumerate(MUNITS):
                    cnt = b * len(MUNITS) + m
                    if cnt >= 4:
                        pe.wait_ge(s_mrd, cnt - 3)
                    nk = (i + 1) * P
                    for k in range(MHEADS[i]):
                        n = MHEADS[i] * u + k
                        g, row = n % 4, 32 * (n // 4)
                        off = k * nk if i < 2 else k * 512
                        o = bank(2 * (cnt % 4), 2)[:, off:off + nk]
                        pe.matmul(o, QT[row:row + 32, b, g, i * P:(i + 1) * P], KTr[row:row + 32, b, g, 0:nk],
                                  start=True, stop=False)
                        mm = pe.matmul(o[:, i * P:nk], identb[:, :], masksb[:, 1, :], start=False, stop=True)
                    mm.then_inc(s_mps, 1)

            def turn_again(b, i):
                pe.wait_ge(s_neg, b * TB + i + 1)
                pe.wait_ge(s_mrd, (b + 1) * len(MUNITS))
                for g in range(4):
                    mm = pe.transpose(bank(i)[:, g * P:(g + 1) * P], QP0[:, b, i, g * P:(g + 1) * P], ident[:, :])
                mm.then_inc(s_rqps, 1)

            def order1(n):
                G, half, c = n // 8, n // 4 % 2, n % 4
                return 2 * (4 * G + c) + half

            def weigh0(b, g):
                pe.wait_ge(s_p, b * MAPS + 4 * g + 4)
                c = b * 4 + g
                if c >= 2:
                    pe.wait_ge(s_pve, c - 1)
                for j in range(TB):
                    for k in range(4):
                        mm = pe.matmul(bank(6 + g % 2)[32 * k:32 * k + 32, j * P:S], VA[:, b * TB + j, 4 * g + k, :],
                                       PR[:, (b * MAPS + 4 * g + k) % PSLOTS, PCOL[j]:PCOL[j] + S - j * P],
                                       start=(j == 0), stop=(j == TB - 1), tile_position=(0, 32 * k))
                mm.then_inc(s_pv, 1)

            def weigh1(b, q):
                base = (2 + b) * MAPS + 4 * q
                pe.wait_ge(s_p, base + 4)
                c = 8 + b * 4 + q
                pe.wait_ge(s_pve, c)
                G = q // 2
                for j in range(TB):
                    for k in range(4):
                        pr = PR[:, (base + k) % PSLOTS, PCOL[j]:PCOL[j] + S - j * P]
                        pe.matmul(bank(6)[32 * k:32 * k + 32, j * P:S], V1[:, b * TB + j, (4 * G + k) * 32:(4 * G + k + 1) * 32],
                                  pr, start=(j == 0), stop=(j == TB - 1), tile_position=(0, 32 * k))
                    for k in range(4):
                        pr = PR[:, (base + k) % PSLOTS, PCOL[j]:PCOL[j] + S - j * P]
                        mm = pe.matmul(bank(7)[32 * k:32 * k + 32, j * P:S], ones32[:, :], pr,
                                       start=(j == 0), stop=(j == TB - 1), tile_position=(0, 32 * k))
                mm.then_inc(s_pv, 1)

            def attend(l, b):
                for n in range(MAPS):
                    scores_n(l, b, n)
                    if n >= 5 and n % 4 == 1:
                        (weigh0 if l == 0 else weigh1)(b, n // 4 - 1)
                (weigh0 if l == 0 else weigh1)(b, 3)

            def scores_n(l, b, n):
                c = (2 * l + b) * MAPS + n
                if c >= 2:
                    pe.wait_ge(s_p, c - 1)
                m = n if l == 0 else order1(n)
                g, row = slot(l, m)
                o = bank(3 * (n % 2), 3)
                for j in (0, 1, 3, 2):
                    w = S - j * P
                    blk = o[:, PCOL[j]:PCOL[j] + w]
                    pe.matmul(blk, KTr[row:row + SLOT[l], b, g, j * P:(j + 1) * P],
                              QT[row:row + SLOT[l], b, g, j * P:S], start=True, stop=False)
                    mm = pe.matmul(blk[:, 0:P], identb[:, :], masksb[:, 0, :], start=False, stop=True)
                mm.then_inc(s_sc, 1)

            def out_proj(l, b, i, lhs):
                c = b * TB + i
                if c >= 2:
                    pe.wait_ge((s_woe, s_woe1)[l], c - 1)
                for kt in range(KT):
                    mm = pe.matmul(bank(4 + i % 2)[:, 0:D], lhs(kt), wo_sb[:, kt, :],
                                   start=(kt == 0), stop=(kt == KT - 1))
                mm.then_inc(s_wo, 1)

            pe.wait_ge(s_ld, 96)
            pe.wait_ge(s_w0, 128)
            pe.wait_ge(s_const, 1)
            for b in range(B):
                turn_tokens(0, b)
            for b in range(B):
                prepare(0, b)
            for b in range(B):
                pe.wait_ge(s_tev, tcount(0, B - 1, TB - 1))
                pe.wait_ge(s_qkve, NT)
                if b:
                    pe.wait_ge(s_p, MAPS)
                    pe.wait_ge(s_pve, 4)
                    pe.wait_ge(s_ont, TB)
                    pe.wait_ge(s_woe, TB)
                maxima(b)
                for i in range(TB):
                    turn_again(b, i)
                pe.wait_ge(s_rq, (b + 1) * TB)
                attend(0, b)
                pe.wait_ge(s_pve, 4 * (b + 1))
                pe.wait_ge(s_p, MAPS * (b + 1))
                for i in range(TB):
                    c = b * TB + i
                    if c >= 2:
                        pe.wait_ge(s_on, c - 1)
                    for g in range(4):
                        mm = pe.transpose(bank(i % 2)[:, g * P:(g + 1) * P], OT[:, g, i * P:(i + 1) * P], ident[:, :])
                    mm.then_inc(s_otps, 1)
                    pe.wait_ge(s_on, c + 1)
                    if c >= 2:
                        pe.wait_ge(s_ont, c - 1)
                    for kt in range(KT):
                        mm = pe.transpose(bank(2 + i % 2)[:, kt * P:(kt + 1) * P],
                                          XN[:, c, kt * P:(kt + 1) * P], ident[:, :])
                    mm.then_inc(s_ontps, 1)
                    pe.wait_ge(s_ont, c + 1)
                    out_proj(0, b, i, lambda kt: XT[:, b, kt, i * P:(i + 1) * P])

            pe.wait_ge(s_woe, NT)
            for b in range(B):
                turn_tokens(1, b)
            for b in range(B):
                pe.wait_ge(s_xt, 2 + b + 1)
                for i in range(TB):
                    xt = [XT[:, b, kt, i * P:(i + 1) * P] for kt in range(KT)]
                    for kt in range(KT):
                        pe.matmul(bank(4 + 2 * b)[:, i * E0:(i + 1) * E0], xt[kt], wrd_sb[:, kt, 0:E0],
                                  start=(kt == 0), stop=(kt == KT - 1))
                    for kt in range(KT):
                        mm = pe.matmul(bank(5 + 2 * b)[:, i * P:(i + 1) * P], xt[kt], wrd_sb[:, kt, E0:E0 + E0 * I0],
                                       start=(kt == 0), stop=(kt == KT - 1))
                mm.then_inc(s_rd, 1)
            for b in range(B):
                pe.wait_ge(s_aw, b + 1)
                for i in range(TB):
                    mm = pe.transpose(bank(2 * b)[:, i * P:(i + 1) * P], RB[:, i * P:(i + 1) * P], ident[:, :])
                mm.then_inc(s_awps, 1)
                pe.wait_ge(s_awt, b + 1)
                for i in range(TB):
                    mm = pe.matmul(bank(4 + 2 * b + i // 2)[:, i % 2 * D:(i % 2 + 1) * D], RA[:, i * P:(i + 1) * P],
                                   up_sb[:, :], start=True, stop=True)
                mm.then_inc(s_up, 1)

            pe.wait_ge(s_upe, B)
            for b in range(B):
                turn_tokens(2, b)
            pe.wait_ge(s_w1, 16)
            for b in range(B):
                prepare(1, b)
            pe.wait_ge(s_tev, tcount(1, B - 1, TB - 1))
            pe.wait_ge(s_qkve1, NT)
            pe.wait_ge(s_w1o, 16)
            for b in range(B):
                attend(1, b)
            pe.wait_ge(s_pve, 16)
            pe.wait_ge(s_p, 4 * MAPS)
            for b in range(B):
                for i in range(TB):
                    out_proj(1, b, i, lambda kt: XT[:, b, kt, i * P:(i + 1) * P])

            pe.wait_ge(s_woe1, NT)
            for b in range(B):
                turn_tokens(3, b)
            for b in range(B):
                pe.wait_ge(s_xt, 6 + b + 1)
                for i in range(TB):
                    for kt in range(KT):
                        mm = pe.matmul(bank(4 + b)[:, i * E1:(i + 1) * E1], XT[:, b, kt, i * P:(i + 1) * P],
                                       r1_sb[:, kt, :], start=(kt == 0), stop=(kt == KT - 1))
                mm.then_inc(s_rt, 1)

            def shared_up(n):
                if n == 0:
                    pe.wait_ge(s_ws, 32)
                for h in range(2):
                    if n:
                        pe.wait_ge(s_sg, 2 * n + h - 1)
                    for part in range(2):
                        for kt in range(KT):
                            w0 = (part * KT + kt) * P
                            mm = pe.matmul(bank(2 * h + part), WSGU[:, n, w0:w0 + P], XT[:, h, kt, :],
                                           start=(kt == 0), stop=(kt == KT - 1))
                    mm.then_inc(s_gu, 1)

            shared_up(0)
            pe.wait_ge(s_oh, B)
            for c in range(NT):
                o = bank(6)[:, c * E1:(c + 1) * E1]
                pe.matmul(o, before[:, :], MK[:, c, :], start=True, stop=(c == 0))
                for c2 in range(c):
                    pe.matmul(o, onesb[:, :], MK[:, c2, :], start=False, stop=(c2 == c - 1))
            for c in range(NT):
                mm = pe.matmul(bank(7)[:, 0:E1], onesb[:, :], MK[:, c, :], start=(c == 0), stop=(c == NT - 1))
            mm.then_inc(s_rank, 1)
            shared_up(1)
            pe.wait_ge(s_ediag, 1)
            pe.matmul(bank(7)[:, 0:P], onesb[:, :], ediag[:, :], start=True, stop=True).then_inc(s_eps, 1)
            shared_up(2)
            for n in range(NC):
                if n % (NC // 2) == 0:
                    pe.wait_ge(s_hot, n // (NC // 2) + 1)
                mm = pe.matmul(bank(5)[:, 0:NTILE], LO1[:, n, :], HI1[:, n, 0:NTILE], start=(n == 0), stop=(n == NC - 1))
            mm.then_inc(s_tok, 1)
            shared_up(3)

            def loads(j):
                vals = []
                for tab, top in ((TABG, (E1 - 1) * KT * P), (TABW, (E1 // 2 - 1) * D)):
                    for q in range(U // 4):
                        _, v = nc.values_load_multi_w_load_instructions(
                            tab[0:1, bass.ds(U * j + 4 * q, 4)], engines=[mybir.EngineType.PE], min_val=0, max_val=top,
                            skip_runtime_bounds_check_because="the expert is at most 63")
                        vals += v
                return vals[0:U], vals[U:2 * U]

            def step(i, m, gu, wd):
                fixed = isinstance(i, int)

                def has(lag):
                    return not fixed or 0 <= i - lag < NTILE

                def wait(s, value):
                    if not fixed or value > 0:
                        pe.wait_ge(s, value)

                if has(0):
                    pe.wait_ge(s_gx[m], 2 * i - 2 * m + 16)
                    wait(s_xe, i - 1)
                    for kt in range(KT):
                        mm = pe.transpose(bank(m % 2)[:, kt * P:(kt + 1) * P], XG[:, m, kt * P:(kt + 1) * P], ident[:, :])
                    mm.then_inc(s_tx, 1)
                if has(LAG_D):
                    t, r = i - LAG_D, (m - LAG_D) % 4
                    pe.wait_ge(s_ate, t + 1)
                    wait(s_ye, t - 1)
                    pe.matmul(bank(6 + r % 2)[:, 0:D], AT[:, r, :], WD[:, bass.ds(wd[m], D)],
                              start=True, stop=True).then_inc(s_d, 1)
                if has(LAG_GU):
                    t, r = i - LAG_GU, (m - LAG_GU) % 4
                    pe.wait_ge(s_xe, t + 1)
                    wait(s_a, t - 1)
                    for kt in range(KT):
                        mm = pe.matmul(bank(2 + r % 2)[:, 0:P], XGT[:, r, kt * P:(kt + 1) * P],
                                       WGU[:, bass.ds(gu[m] + kt * P, P)], start=(kt == 0), stop=(kt == KT - 1))
                    mm.then_inc(s_gup, 1)
                if has(LAG_TA):
                    t, r = i - LAG_TA, (m - LAG_TA) % 4
                    pe.wait_ge(s_a, t + 1)
                    wait(s_ate, t - 1)
                    pe.transpose(bank(4 + r % 2)[:, 0:P], A[:, r, :], ident[:, :]).then_inc(s_ta, 1)

            pe.wait_ge(s_wgu, 64)
            pe.wait_ge(s_wd, 32)
            pe.wait_ge(s_idx, 1)
            pe.wait_ge(s_sg, 2 * NSB)
            gu, wd = loads(0)
            for m in range(U):
                step(m, m, gu, wd)
            with pe.Fori(1, NBODY) as j:
                gu, wd = loads(j)
                for m in range(U):
                    step(U * j + m, m, gu, wd)
            gu, wd = loads(NBODY)
            for m in range(LAG_D):
                step(NTILE + m, m, gu, wd)

            pe.wait_ge(s_ye, NTILE)
            pe.wait_ge(s_gt, 2 * NSB)
            for c in range(NT):
                for n in range(NSB):
                    mm = pe.matmul(bank(c // 2)[:, c % 2 * D:(c % 2 + 1) * D], SACT[n][:, c * P:(c + 1) * P], WSD[:, n, :],
                                   start=(n == 0), stop=(n == NSB - 1))
                if c % 2:
                    mm.then_inc(s_sd, 1)

        @block.scalar
        def _(sc):
            last = [None, 0]
            counts = {}

            def did(ins, s=None):
                s = s or s_ac
                ins.then_inc(s, 1)
                counts[id(s)] = counts.get(id(s), 0) + 1
                last[:] = [s, counts[id(s)]]

            def settle():
                sc.wait_ge(last[0], last[1])

            def root(src, dst, bias, s):
                did(sc.activation(dst, src, ACT.Ln, bias=bias, scale=1.0))
                settle()
                did(sc.activation(dst, dst, ACT.Exp, scale=-0.5), s)

            def rstd_of(k, b):
                sc.wait_ge(s_var, 2 * k + b + 1)
                t = slice(b * TB, (b + 1) * TB)
                root(mv[:, t, 1], rstd[:, t], eps_sb[:, 0:1], s_rstd)

            def store_xt(k, b):
                sc.wait_ge(s_xtps, 2 * k + b + 1)
                for kt in range(KT):
                    ins = sc.activation(XT[:, b, kt, :], bank(2 * b + kt), ACT.Copy,
                                        scale=rms_sb[:, kt:kt + 1] if k == 0 else 1.0)
                    did(ins, s_xt if kt == KT - 1 else None)

            def store_padded(l, b, i):
                for n, (q, g0) in enumerate(tunits(l)):
                    u = tcount(l, b, i) - len(tunits(l)) + n
                    sc.wait_ge(s_tps, u + 1)
                    dst = (QT if q else KTr)[:, b, g0:g0 + 4, i * P:(i + 1) * P]
                    did(sc.activation(dst, bank(u % 4).rearrange("p (g c) -> p g c", g=4), ACT.Copy), s_tev)

            def exps(l, b):
                for n in range(MAPS):
                    c = (2 * l + b) * MAPS + n
                    sc.wait_ge(s_sc, c + 1)
                    if c >= PSLOTS:
                        sc.wait_ge(s_pv, (c - PSLOTS) // 4 + 1)
                    did(sc.activation(PR[:, c % PSLOTS, :], bank(3 * (n % 2), 3)[:, 0:PW], ACT.Exp,
                                      scale=0.5 if l == 0 else 4.0), s_p)

            sc.preload_act_table_set("natural_log_exp_and_others")
            sc.wait_ge(s_const, 1)
            sc.wait_ge(s_lamd, 1)
            did(sc.activation(lam_sb[:, 2:4], lam_sb[:, 0:2], ACT.Exp), s_lame)
            for b in range(B):
                rstd_of(0, b)
                sc.wait_ge(s_msq, b + 1)
                root(msq[:, b * TB:(b + 1) * TB], rr[:, b * TB:(b + 1) * TB], eps_sb[:, 0:1], s_rr)
            sc.wait_ge(s_w0, 128)
            for b in range(B):
                store_xt(0, b)
            for b in range(B):
                for i in range(TB):
                    store_padded(0, b, i)
            for b in range(B):
                for i in range(TB):
                    sc.wait_ge(s_rqps, b * TB + i + 1)
                    did(sc.activation(QT[:, b, 0:4, i * P:(i + 1) * P],
                                      bank(i).rearrange("p (g c) -> p g c", g=4), ACT.Copy), s_rq)
                exps(0, b)
                for i in range(TB):
                    c = b * TB + i
                    sc.wait_ge(s_ontps, c + 1)
                    did(sc.activation(XT[:, b, :, i * P:(i + 1) * P],
                                      bank(2 + i % 2)[:, 0:D].rearrange("p (k c) -> p k c", k=KT), ACT.Copy), s_ont)
            for b in range(B):
                rstd_of(1, b)
            for b in range(B):
                rstd_of(2, b)
            for b in range(B):
                store_xt(1, b)
            for b in range(B):
                sc.wait_ge(s_lmax, b + 1)
                did(sc.activation(exl[:, :, 0:E0], shl[:, :, 0:E0], ACT.Exp))
                did(sc.activation(RB[:, :], RA[:, :], ACT.Exp, scale=-1.0), s_ex)
                sc.wait_ge(s_awps, b + 1)
                did(sc.activation(RA[:, :], bank(2 * b), ACT.Copy), s_awt)
            for b in range(B):
                rstd_of(3, b)
            for b in range(B):
                rstd_of(4, b)
            for b in range(B):
                store_xt(2, b)
            for b in range(B):
                for i in range(TB):
                    c = b * TB + i
                    sc.wait_ge(s_qkv, NT + c + 1)
                    if c >= 2:
                        sc.wait_ge(s_pad, NT + c - 1)
                    did(sc.activation(QK[:, c % 2, :], bank(4 + i % 2), ACT.Copy))
                    did(sc.activation(V1[:, c, :], bank(6 + i % 2)[:, 0:D], ACT.Copy), s_qkve1)
                    sc.wait_ge(s_ss, c + 1)
                    root(ss[:, c % 2, :], rs1[:, c % 2, :], eps_sb[:, 1:2], s_rs1)
                    store_padded(1, b, i)
            for b in range(B):
                exps(1, b)
            for b in range(B):
                for i in range(TB):
                    c = b * TB + i
                    sc.wait_ge(s_wo, NT + c + 1)
                    did(sc.activation(H[:, c, :], bank(4 + i % 2)[:, 0:D], ACT.Copy, scale=1.0 - LAMBDA_INIT), s_woe1)
            for b in range(B):
                rstd_of(5, b)
            for b in range(B):
                rstd_of(6, b)
            for b in range(B):
                store_xt(3, b)
            for g in range(B):
                sc.wait_ge(s_rte, g + 1)
                did(sc.activation(exl[:, :, :], shl[:, :, :], ACT.Exp), s_rex)

            for n in range(NSB):
                for h in range(2):
                    sc.wait_ge(s_gu, 2 * n + h + 1)
                    if n:
                        sc.wait_ge(s_gt, 2 * n + h - 1)
                    did(sc.activation((RA, RB)[h][:, :], bank(2 * h), ACT.Silu))
                    if n == 2 and h == 0:
                        sc.wait_ge(s_hd, 32)
                    did(sc.activation(SACT[n][:, h * S:(h + 1) * S], bank(2 * h + 1), ACT.Copy), s_sg)

            def step(i, m):
                fixed = isinstance(i, int)

                def wait(s, value):
                    if not fixed or value > 0:
                        sc.wait_ge(s, value)

                if not fixed or i < NTILE:
                    sc.wait_ge(s_tx, i + 1)
                    wait(s_gup, i - 3)
                    sc.activation(XGT[:, m % 4, :], bank(m % 2)[:, 0:D], ACT.Copy).then_inc(s_xe, 1)
                if not fixed or i >= 1:
                    r = (m - 1) % 4
                    sc.wait_ge(s_gup, i)
                    wait(s_a, i - 4)
                    sc.activation(SG[:, r, :], bank(2 + r % 2)[:, 0:F1], ACT.Silu).then_inc(s_sgs, 1)

            for m in range(U):
                step(m, m)
            with sc.Fori(1, NBODY) as j:
                for m in range(U):
                    step(U * j + m, m)
            step(NTILE, 0)
            for b in range(B):
                rstd_of(7, b)

        @block.vector
        def _(dv):
            last = [None, 0]
            counts = {}

            def did(ins, s=None):
                s = s or s_dv
                ins.then_inc(s, 1)
                counts[id(s)] = counts.get(id(s), 0) + 1
                last[:] = [s, counts[id(s)]]

            def settle():
                dv.wait_ge(last[0], last[1])

            def stats(k, b, src):
                for i in range(TB):
                    did(dv.bn_stats(st[:, b * TB + i, :], src[:, b * TB + i, :]))
                settle()
                for i in range(TB):
                    t = b * TB + i
                    did(dv.bn_aggr(mv[:, t, :], st[:, t, :]), s_var if i == TB - 1 else None)

            def normalise(k, b, src, dst, s=None):
                dv.wait_ge(s_rstd, 2 * k + b + 1)
                for i in range(TB):
                    t = b * TB + i
                    did(dv.tensor_scalar(dst[:, t, :], src[:, t, :], mv[:, t, 0:1], rstd[:, t:t + 1],
                                         ALU.subtract, ALU.mult), s if i == TB - 1 else None)

            def add_norm(k, b):
                normalise(k, b, H, H)
                settle()
                t = slice(b * TB, (b + 1) * TB)
                did(dv.tensor_tensor(X[:, t, :], X[:, t, :], H[:, t, :], ALU.add))
                settle()

            def bc(ap, n):
                return ap.unsqueeze(1).broadcast_to([P, n, ap.shape[-1]])

            dv.wait_ge(s_ld, 96)
            did(dv.tensor_copy(identb[:, :], ident[:, :]))
            did(dv.tensor_copy(masksb[:, :, :], RB[:, 0:2 * P].rearrange("p (a c) -> p a c", a=2)))
            did(dv.tensor_copy(before[:, :], RA[:, 0:P]))
            did(dv.memset(ones32[:, :], 1.0))
            did(dv.memset(onesb[:, :], 1.0))
            did(dv.memset(ones64[:, :], 1.0))
            did(dv.memset(TABG[:, :], 0))
            did(dv.memset(TABW[:, :], 0))
            dv.wait_ge(s_pool, 4)
            did(dv.tensor_copy(iota16[:, :], iotaf[:, :]))
            did(dv.memset(eps_sb[:, 0:1], EPS))
            did(dv.memset(eps_sb[:, 1:2], HH * RMS_EPS1))
            did(dv.memset(QP0[:, :, :, :], 0.0))
            did(dv.memset(KP0[:, :, :], 0.0))
            did(dv.memset(VA[:, :, :, :], 0.0))
            settle()
            did(dv.memset(VA[:, :, :, HD0:HD0 + 1], 1.0))
            did(dv.memset(KP0[:, :, :].rearrange("p r (h c) -> p r h c", c=32)[:, :, :, 3 * ROT:3 * ROT + 2], 1.0), s_const)
            did(dv.tensor_tensor(lv_sb[:, 0:4:2, :], lv_sb[:, 0:4:2, :], lv_sb[:, 1:4:2, :], ALU.mult))
            settle()
            did(dv.tensor_reduce(lam_sb[:, 0:2], lv_sb[:, 0:4:2, :], AX.X, ALU.add), s_lamd)
            dv.wait_ge(s_lame, 1)
            did(dv.tensor_tensor(lam_sb[:, 0:1], lam_sb[:, 3:4], lam_sb[:, 2:3], ALU.subtract))
            settle()
            did(dv.tensor_scalar(lam_sb[:, 1:2], lam_sb[:, 0:1], -LAMBDA_INIT, None, ALU.add))

            dv.wait_ge(s_x, 32)
            for b in range(B):
                stats(0, b, X)
            for b in range(B):
                t = slice(b * TB, (b + 1) * TB)
                dv.wait_ge(s_rstd, b + 1)
                did(dv.tensor_tensor(msq[:, t], mv[:, t, 1], rstd[:, t], ALU.mult))
                settle()
                did(dv.tensor_tensor(msq[:, t], msq[:, t], rstd[:, t], ALU.mult), s_msq)
                normalise(0, b, X, H)
                dv.wait_ge(s_rr, b + 1)
                settle()
                for i in range(TB):
                    c = b * TB + i
                    did(dv.tensor_scalar(XN[:, c, :], H[:, c, :], rr[:, c:c + 1], None, ALU.mult),
                        s_xn if i == TB - 1 else None)
                dv.wait_ge(s_w0, 128)
                settle()
                did(dv.tensor_tensor(H[:, t, :], H[:, t, :], bc(bo_sb[:, :], TB), ALU.add))
            for b in range(B):
                for i in range(TB):
                    c = b * TB + i
                    dv.wait_ge(s_qkv, c + 1)
                    settle()
                    did(dv.tensor_tensor(VA[:, c, :, 0:HD0], bank(6 + i % 2)[:, 0:D].rearrange("p (h c) -> p h c", c=HD0),
                                         bqkv_sb[:, 2 * D:3 * D].rearrange("p (h c) -> p h c", c=HD0), ALU.add))
                    did(dv.tensor_tensor(QK[:, 0, :], bank(4 + i % 2), bqkv_sb[:, 0:2 * D], ALU.add), s_qkve)
                    settle()
                    pairs = QK[:, 0, :].rearrange("p (h f t) -> p h f t", f=ROT, t=2)
                    ra = RA[:, 0:D].rearrange("p (h f) -> p h f", f=ROT)
                    rb = RB[:, 0:D].rearrange("p (h f) -> p h f", f=ROT)
                    did(dv.tensor_tensor(ra, pairs[:, :, :, 0], bc(rope_sb[:, i, 0, :], 32), ALU.mult))
                    did(dv.tensor_tensor(rb, pairs[:, :, :, 1], bc(rope_sb[:, i, 1, :], 32), ALU.mult))
                    settle()
                    did(dv.tensor_tensor(ra, ra, rb, ALU.add))
                    settle()
                    if c >= 2:
                        dv.wait_ge(s_tps, tcount(0, 0, 0) * (c - 1))
                    qp = QP0[:, b, i, :].rearrange("p (h c) -> p h c", c=32)
                    kp = KP0[:, c % 2, :].rearrange("p (h c) -> p h c", c=32)
                    split_parts(dv, did, settle, qp, kp, ra[:, 0:16, :], ra[:, 16:32, :], ROT)
            for b in range(B):
                for n, (i, u) in enumerate(MUNITS):
                    cnt = b * len(MUNITS) + n
                    dv.wait_ge(s_mps, cnt + 1)
                    nh = MHEADS[i]
                    nk = (i + 1) * P
                    src = bank(2 * (cnt % 4), 2)
                    src = src[:, 0:nh * nk].rearrange("p (h k) -> p h k", h=nh) if i < 2 else \
                        src.rearrange("p (h k) -> p h k", h=2)[:, :, 0:nk]
                    did(dv.tensor_reduce(mx[:, b * TB + i, nh * u:nh * u + nh], src, AX.X, ALU.max), s_mrd)
                    if u == 16 // nh - 1:
                        c = b * TB + i
                        qp = QP0[:, b, i, :].rearrange("p (h c) -> p h c", c=32)
                        settle()
                        qp = qp.rearrange("p (g r) c -> p g r c", r=4)
                        m = mx[:, c, :].rearrange("p (r g) -> p g r", g=4)
                        did(dv.tensor_scalar(qp[:, :, :, 3 * ROT].bitcast(f32r), m, -1.0, None, ALU.mult))
                        settle()
                        did(dv.scalar_tensor_tensor(out=qp[:, :, :, 3 * ROT + 1], in0=m, scalar=-1.0,
                                                    in1=qp[:, :, :, 3 * ROT], op0=ALU.mult, op1=ALU.subtract), s_neg)
                for g in range(4):
                    if b and g == 0:
                        dv.wait_ge(s_otps, TB)
                    dv.wait_ge(s_pv, b * 4 + g + 1)
                    did(dv.tensor_copy(OT[:, g, :], bank(6 + g % 2)), s_pve)
                for i in range(TB):
                    c = b * TB + i
                    dv.wait_ge(s_otps, c + 1)
                    o = bank(i % 2).rearrange("p (h c) -> p h c", c=32)
                    settle()
                    did(dv.reciprocal(den[:, :], o[:, :, HD0]))
                    settle()
                    did(dv.tensor_tensor(XN[:, c, :].rearrange("p (h c) -> p h c", c=HD0), o[:, :, 0:HD0],
                                         den[:, :].unsqueeze(2).broadcast_to([P, HEADS0, HD0]), ALU.mult), s_on)
                    dv.wait_ge(s_wo, c + 1)
                    did(dv.tensor_tensor(H[:, c, :], H[:, c, :], bank(4 + i % 2)[:, 0:D], ALU.add), s_woe)
            settle()
            for b in range(B):
                stats(1, b, H)
            for b in range(B):
                add_norm(1, b)
                stats(2, b, X)
            for b in range(B):
                normalise(2, b, X, XN, s_xn)
            def choose(b, E, k, lg, bias):
                src = lgs[:, :, 0:E]
                did(dv.tensor_reduce(red[:, 0:TB], lg, AX.X, ALU.max))
                if bias is not None:
                    did(dv.tensor_tensor(src, lg, bias, ALU.add))
                else:
                    did(dv.tensor_copy(src, lg))
                settle()
                did(dv.tensor_tensor(shl[:, :, 0:E], lg, red[:, 0:TB].unsqueeze(2).broadcast_to([P, TB, E]), ALU.subtract))
                for i in range(TB):
                    did(dv.max(top[:, i, :], lgs[:, i, 0:E]))
                settle()
                for i in range(TB):
                    did(dv.max_index(idx[:, i, :], top[:, i, :], lgs[:, i, 0:E]))
                settle()
                did(dv.tensor_copy(idxf[:, :, :], idx[:, :, :]))
                for n in range(k):
                    settle()
                    did(dv.tensor_tensor((oh if n == 0 else oh2)[:, :, 0:E], bc(iota_f[:, 0:E], TB),
                                         idxf[:, :, n].unsqueeze(2).broadcast_to([P, TB, E]), ALU.is_equal))
                    if n:
                        settle()
                        did(dv.tensor_tensor(oh[:, :, 0:E], oh[:, :, 0:E], oh2[:, :, 0:E], ALU.add))

            dv.wait_ge(s_pool, 1)
            for b in range(B):
                dv.wait_ge(s_rd, b + 1)
                if b:
                    dv.wait_ge(s_up, b)
                lg = bank(4 + 2 * b)[:, 0:TB * E0].rearrange("p (i e) -> p i e", e=E0)
                settle()
                did(dv.tensor_copy(RA[:, :], bank(5 + 2 * b)))
                choose(b, E0, 2, lg, None)
                did(dv.memset(red[:, TB:2 * TB], 0.0), s_lmax)
                dv.wait_ge(s_ex, b + 1)
                settle()
                did(dv.tensor_reduce(red[:, 0:TB], exl[:, :, 0:E0], AX.X, ALU.add))
                did(dv.tensor_tensor(oh[:, :, 0:E0], oh[:, :, 0:E0], exl[:, :, 0:E0], ALU.mult))
                did(dv.tensor_scalar(RB[:, :], RB[:, :], 1.0, None, ALU.add))
                settle()
                did(dv.reciprocal(red[:, TB:2 * TB], red[:, 0:TB]))
                did(dv.reciprocal(RB[:, :], RB[:, :]))
                settle()
                did(dv.tensor_tensor(oh[:, :, 0:E0], oh[:, :, 0:E0],
                                     red[:, TB:2 * TB].unsqueeze(2).broadcast_to([P, TB, E0]), ALU.mult))
                did(dv.tensor_tensor(RB[:, :], RB[:, :], RA[:, :], ALU.mult))
                settle()
                for i in range(TB):
                    v = RB[:, i * P:(i + 1) * P].rearrange("p (e i) -> p e i", i=I0)
                    did(dv.tensor_tensor(v, v, oh[:, i, 0:E0].unsqueeze(2).broadcast_to([P, E0, I0]), ALU.mult),
                        s_aw if i == TB - 1 else None)
                dv.wait_ge(s_up, b + 1)
                did(dv.tensor_copy(H[:, b * TB:(b + 1) * TB, :].rearrange("p t c -> p (t c)"), bank(4 + 2 * b, 2)), s_upe)
            settle()
            for b in range(B):
                stats(3, b, H)
            for b in range(B):
                add_norm(3, b)
                stats(4, b, X)
            for b in range(B):
                normalise(4, b, X, XN, s_xn)
            did(dv.memset(QP0[:, :, :, :], 0.0))
            for b in range(B):
                for i in range(TB):
                    c = b * TB + i
                    dv.wait_ge(s_qkve1, c + 1)
                    settle()
                    q16 = QK[:, c % 2, :].rearrange("p (m d) -> p m d", d=HH)
                    did(dv.tensor_tensor(RA[:, :], QK[:, c % 2, :], QK[:, c % 2, :], ALU.mult))
                    settle()
                    did(dv.tensor_reduce(ss[:, c % 2, :], RA[:, :].rearrange("p (m d) -> p m d", d=HH), AX.X, ALU.add), s_ss)
                    dv.wait_ge(s_rs1, c + 1)
                    did(dv.tensor_tensor(q16, q16, rs1[:, c % 2, :].unsqueeze(2).broadcast_to([P, 32, HH]), ALU.mult))
                    settle()
                    if c >= 2:
                        dv.wait_ge(s_tps, 2 * NT + 4 * (c - 1))
                    qp = QKP1[:, c % 2, 1, :].rearrange("p (h c) -> p h c", c=64)
                    kp = QKP1[:, c % 2, 0, :].rearrange("p (h c) -> p h c", c=64)
                    split_parts(dv, did, settle, qp, kp, q16[:, 0:16, :], q16[:, 16:32, :], HH)
            for b in range(B):
                for q in range(4):
                    dv.wait_ge(s_pv, 8 + b * 4 + q + 1)
                    G, half = q // 2, q % 2
                    settle()
                    did(dv.reciprocal(NA[:, :], bank(7)))
                    settle()
                    if half == 0:
                        did(dv.tensor_tensor(XT[:, b, G, :], bank(6), NA[:, :], ALU.mult), s_pve)
                    else:
                        did(dv.scalar_tensor_tensor(out=NB[:, :], in0=bank(6), scalar=lam_sb[:, 1:2], in1=NA[:, :],
                                                    op0=ALU.mult, op1=ALU.mult))
                        settle()
                        did(dv.tensor_tensor(XT[:, b, G, :], XT[:, b, G, :], NB[:, :], ALU.add), s_pve)
            for b in range(B):
                dv.wait_ge(s_woe1, (b + 1) * TB)
                stats(5, b, H)
            for b in range(B):
                add_norm(5, b)
                stats(6, b, X)
            for b in range(B):
                normalise(6, b, X, XN, s_xn)
            for b in range(B):
                t = slice(b * TB, (b + 1) * TB)
                dv.wait_ge(s_rt, b + 1)
                lg = bank(4 + b)[:, 0:TB * E1].rearrange("p (i e) -> p i e", e=E1)
                if b:
                    dv.wait_ge(s_rex, b)
                settle()
                choose(b, E1, 0, lg, bc(rb_sb[:, :], TB))
                settle()
                did(dv.tensor_tensor(OH[:, t, :, :], iota_f[:, :].unsqueeze(1).unsqueeze(1).broadcast_to([P, TB, TOPK1, E1]),
                                     idxf[:, :, 0:TOPK1].unsqueeze(3).broadcast_to([P, TB, TOPK1, E1]), ALU.is_equal), s_rte)
                settle()
                with nc.allow_low_precision(reason="zeros and ones"):
                    did(dv.tensor_reduce(MK[:, t, :], OH[:, t, :, :].rearrange("p t k e -> p t e k"), AX.X, ALU.add), s_oh)
                dv.wait_ge(s_rex, b + 1)
                settle()
                did(dv.tensor_tensor(PRD[:, t, :, :], OH[:, t, :, :],
                                     exl[:, :, :].unsqueeze(2).broadcast_to([P, TB, TOPK1, E1]), ALU.mult))
                settle()
                did(dv.tensor_reduce(wk[:, b * TB * TOPK1:(b + 1) * TB * TOPK1].rearrange("p (t k) -> p t k", k=TOPK1),
                                     PRD[:, t, :, :], AX.X, ALU.add))
            dv.wait_ge(s_rank, 1)
            did(dv.tensor_scalar(tcnt[:, 0, :], bank(7)[:, 0:E1], (P - 1) / 2, 1.0 / P, ALU.add, ALU.mult))
            settle()
            did(dv.tensor_scalar(tcnt[:, 0, :], tcnt[:, 0, :], MAGIC, None, ALU.add))
            settle()
            did(dv.tensor_scalar(tcnt[:, 0, :], tcnt[:, 0, :], -MAGIC, None, ALU.add))
            settle()
            did(dv.tensor_tensor_scan(tcnt[:, 1, :], ones64[:, :], tcnt[:, 0, :], 0.0, ALU.mult, ALU.add))
            settle()
            did(dv.tensor_tensor(tcnt[:, 2, :], tcnt[:, 1, :], tcnt[:, 0, :], ALU.subtract))
            did(dv.tensor_scalar(tcnt[:, 3, :], tcnt[:, 1, :], tile_no[:, 0:1], None, ALU.is_le))
            settle()
            did(dv.tensor_reduce(ecol[:, 0:1], tcnt[:, 3, :], AX.X, ALU.add))
            did(dv.tensor_scalar(tcnt[:, 2, :], tcnt[:, 2, :], float(P), None, ALU.mult))
            settle()
            did(dv.tensor_scalar(ecol[:, 1:2], ecol[:, 0:1], float(E1 - 1), None, ALU.min))
            settle()
            did(dv.tensor_scalar(ediag[:, :], ident[:, :], ecol[:, 1:2], None, ALU.mult), s_ediag)
            rank = bank(6).rearrange("p (t e) -> p t e", e=E1)
            did(dv.tensor_tensor(MKF, rank, bc(tcnt[:, 2, :], NT), ALU.add))
            settle()
            did(dv.tensor_tensor(PRD, OH, MKF.unsqueeze(2).broadcast_to([P, NT, TOPK1, E1]), ALU.mult))
            settle()
            did(dv.tensor_reduce(slotf[:, :].rearrange("p (t k) -> p t k", k=TOPK1), PRD, AX.X, ALU.add))
            settle()
            did(dv.tensor_scalar(hi[:, :], slotf[:, :], -(P - 1) / 2, 1.0 / P, ALU.add, ALU.mult))
            settle()
            did(dv.tensor_scalar(hi[:, :], hi[:, :], MAGIC, None, ALU.add))
            settle()
            did(dv.tensor_scalar(hi[:, :], hi[:, :], -MAGIC, None, ALU.add))
            settle()
            did(dv.scalar_tensor_tensor(out=lo[:, :], in0=hi[:, :], scalar=-float(P), in1=slotf[:, :],
                                        op0=ALU.mult, op1=ALU.add))
            did(dv.tensor_copy(slotu[:, :], slotf[:, :]))
            settle()
            for n in range(NC):
                did(dv.tensor_scalar(LO1[:, n, :], iota16[:, :], lo[:, n:n + 1], None, ALU.is_equal))
                did(dv.tensor_scalar(HI1[:, n, 0:NTILE], iota16[:, 0:NTILE], hi[:, n:n + 1],
                                     tokid[:, n // TOPK1:n // TOPK1 + 1], ALU.is_equal, ALU.mult),
                    s_hot if n % (NC // 2) == NC // 2 - 1 else None)
            dv.wait_ge(s_eps, 1)
            did(dv.tensor_copy(erow[:, 0, :], bank(7)[:, 0:NTILE]))
            settle()
            did(dv.tensor_scalar(erow[:, 1, :], erow[:, 0, :], -0.5, 0.5, ALU.add, ALU.mult))
            settle()
            did(dv.tensor_scalar(erow[:, 1, :], erow[:, 1, :], MAGIC, None, ALU.add))
            settle()
            did(dv.tensor_scalar(erow[:, 1, :], erow[:, 1, :], -MAGIC, None, ALU.add))
            settle()
            did(dv.scalar_tensor_tensor(out=odd[:, 1, :], in0=erow[:, 1, :], scalar=-2.0, in1=erow[:, 0, :],
                                        op0=ALU.mult, op1=ALU.add))
            did(dv.tensor_scalar(TABG[:, LAG_GU:LAG_GU + NTILE], erow[0:1, 0, :], float(KT * P), None, ALU.mult))
            did(dv.tensor_scalar(TABW[:, LAG_D:LAG_D + NTILE], erow[0:1, 1, :], float(D), None, ALU.mult))
            settle()
            did(dv.tensor_scalar(odd[:, 0, :], odd[:, 1, :], -1.0, 1.0, ALU.mult, ALU.add))
            dv.wait_ge(s_tok, 1)
            did(dv.tensor_copy(tok_of[:, :], bank(5)[:, 0:NTILE]), s_idx)
            did(dv.tensor_reduce(wsum[:, 0:NT], wk[:, :].rearrange("p (t k) -> p t k", k=TOPK1), AX.X, ALU.add))
            settle()
            did(dv.reciprocal(wsum[:, NT:2 * NT], wsum[:, 0:NT]))
            settle()
            w3 = wk[:, :].rearrange("p (t k) -> p t k", k=TOPK1)
            did(dv.tensor_tensor(w3, w3, wsum[:, NT:2 * NT].unsqueeze(2).broadcast_to([P, NT, TOPK1]), ALU.mult))

            def step(i, m):
                fixed = isinstance(i, int)

                def has(lag):
                    return not fixed or 0 <= i - lag < NTILE

                def wait(s, value):
                    if not fixed or value > 0:
                        dv.wait_ge(s, value)

                if has(LAG_D):
                    t, r = i - LAG_D, (m - LAG_D) % 4
                    dv.wait_ge(s_d, t + 1)
                    if m:
                        wait(s_st[r], 4 * (i - m) + 16 * ((m - LAG_D) // 4))
                    if m == U - 1:
                        wait(s_st[(U - LAG_D) % 4], 4 * (i - m) + 16 * ((U - LAG_D) // 4))
                    dv.tensor_copy(Y[:, r, :], bank(6 + r % 2)[:, 0:D]).then_inc(s_ye, 1)
                if has(LAG_TA):
                    t, r = i - LAG_TA, (m - LAG_TA) % 4
                    dv.wait_ge(s_ta, t + 1)
                    wait(s_d, t - 3)
                    dv.tensor_copy(AT[:, r, :], bank(4 + r % 2)[:, 0:P]).then_inc(s_ate, 1)
                if has(LAG_GU):
                    t, r = i - LAG_GU, (m - LAG_GU) % 4
                    dv.wait_ge(s_sgs, t + 1)
                    wait(s_ta, t - 3)
                    for half in range(2):
                        par = odd[:, half, t:t + 1] if fixed else odd[:, half, bass.ds(t, 1)]
                        ins = dv.scalar_tensor_tensor(out=A[:, r, half * F1:(half + 1) * F1], in0=SG[:, r, :], scalar=par,
                                                      in1=bank(2 + r % 2)[:, F1:2 * F1], op0=ALU.mult, op1=ALU.mult)
                    ins.then_inc(s_a, 1)

            for m in range(U):
                step(m, m)
            with dv.Fori(1, NBODY) as j:
                for m in range(U):
                    step(U * j + m, m)
            for m in range(LAG_D):
                step(NTILE + m, m)
            for n in range(NC):
                c = n // TOPK1
                dv.wait_ge(s_yg[n % U], 16 * (n // U + 1))
                if n % TOPK1 == 0:
                    dv.wait_ge(s_sd, c // 2 + 1)
                settle()
                did(dv.scalar_tensor_tensor(out=H[:, c, :], in0=XG[:, n % U, :], scalar=wk[:, n:n + 1],
                                            in1=bank(c // 2)[:, c % 2 * D:(c % 2 + 1) * D] if n % TOPK1 == 0 else H[:, c, :],
                                            op0=ALU.mult, op1=ALU.add), s_mx)
            settle()
            for b in range(B):
                stats(7, b, H)
            for b in range(B):
                normalise(7, b, H, H)
                settle()
                t = slice(b * TB, (b + 1) * TB)
                did(dv.tensor_tensor(X[:, t, :], X[:, t, :], H[:, t, :], ALU.add), s_fin)


_ORDER = ["x", "rms_w", "wqkv0", "bqkv0", "wo0", "bo0", "wrd0", "up0", "wqkv1", "wo1", "lvec", "router1", "rbias1",
          "wgu1", "wd1", "wsgu", "wsd", "rope", "ident_in", "mask_in", "before_in"]


def constants():
    j = np.arange(ROT, dtype=np.float32)
    freqs = (10000.0 ** (j.astype(np.float64) * (-2.0 / HD0))).astype(np.float32)
    ang = (np.arange(S, dtype=np.float32)[:, None] * freqs[None, :]).astype(np.float64)
    cos, sin = np.cos(ang), np.sin(ang)
    even = (np.arange(ROT) % 2 == 0)[None, :]
    rope = np.stack([np.where(even, cos, sin), np.where(even, -sin, cos), cos, sin], axis=1).astype(np.float32)
    rope = np.ascontiguousarray(rope.reshape(TB, P, 4, ROT).transpose(1, 0, 2, 3))
    a = np.arange(P)
    keyq = np.where(a[None, :] >= a[:, None], 0.0, NEG).astype(np.float32)
    return {"rope": rope, "ident_in": np.eye(P, dtype=np.float32),
            "before_in": (a[:, None] < a[None, :]).astype(np.float32),
            "mask_in": np.ascontiguousarray(np.stack([keyq, keyq.T], axis=1))}


def layouts(a):
    c = np.ascontiguousarray
    wg, wu, wd = a["L1_ffn_wg"], a["L1_ffn_wu"], a["L1_ffn_wd"]

    def experts(w):
        return w.reshape(E1, KT, P, F1).transpose(0, 2, 1, 3)

    def shared(w):
        return w.reshape(SH, KT, P, HS // P, P).transpose(0, 3, 2, 1, 4).reshape(NSB, P, KT * P)

    return {
        "x": c(a["L0_attn_x"].reshape(TOK, D)),
        "rms_w": c(a["L0_attn_rms_w"].reshape(KT, P).T),
        "wqkv0": c(np.concatenate([a["L0_attn_wq"], a["L0_attn_wk"], a["L0_attn_wv"]], axis=1)),
        "bqkv0": c(np.concatenate([a["L0_attn_bq"], a["L0_attn_bk"], a["L0_attn_bv"]])),
        "wo0": c(a["L0_attn_wo"]), "bo0": c(a["L0_attn_bo"]),
        "wrd0": c(np.concatenate([a["L0_ffn_router_w"].T, a["L0_ffn_down_w"].reshape(E0 * I0, D).T], axis=1)),
        "up0": c(a["L0_ffn_up_w"].transpose(0, 2, 1).reshape(E0 * I0, D)),
        "wqkv1": c(np.concatenate([a["L1_attn_wq"].T, a["L1_attn_wk"].T, a["L1_attn_wv"].T], axis=1)),
        "wo1": c(a["L1_attn_wo"].T),
        "lvec": c(np.concatenate([a["L1_attn_lq1"], a["L1_attn_lk1"], a["L1_attn_lq2"], a["L1_attn_lk2"]])),
        "router1": c(a["L1_ffn_router_w"]), "rbias1": c(a["L1_ffn_router_bias"]),
        "wgu1": c(np.concatenate([experts(wg), experts(wu)], axis=3).reshape(E1, P, KT * P)),
        "wd1": c(wd.reshape(E1 // 2, P, D)),
        "wsgu": c(np.concatenate([shared(a["L1_ffn_swg"]), shared(a["L1_ffn_swu"])], axis=2)),
        "wsd": c(a["L1_ffn_swd"].reshape(NSB, P, D)),
    }


def kernel(**inputs):
    import concourse.bacc as bacc
    from concourse.bass_utils import run_bass_kernel_spmd

    arrays = {**layouts({k: np.asarray(v) for k, v in inputs.items()}), **constants()}
    nc = bacc.Bacc("TRN2", target_bir_lowering=False, num_devices=1)
    aps = [nc.dram_tensor(f"in_{n}", arrays[n].shape, mybir.dt.float32, kind="ExternalInput").ap() for n in _ORDER]
    out = nc.dram_tensor("out_x", (TOK, D), mybir.dt.float32, kind="ExternalOutput").ap()
    h_dram = nc.dram_tensor("tokens", (TOK, D), mybir.dt.float32).ap()
    y_dram = nc.dram_tensor("expert_outputs", (NTILE * P, D), mybir.dt.float32).ap()
    build(nc, *aps, out, h_dram, y_dram)
    r = run_bass_kernel_spmd(nc, [{f"in_{n}": arrays[n] for n in _ORDER}], core_ids=[0])
    return r.results[0]["out_x"].reshape(B, S, D)
```

```python
from contextlib import ExitStack

import numpy as np

import concourse.bass as bass
from concourse import mybir

P = 128
B, S, D = 2, 512, 256
TOK = B * S
NT = TOK // P
TB = S // P
KT = D // P
HEADS0, HD0 = 16, 16
ROT = HD0 // 2
MAPS = 16
HEADS1, HD1 = 8, 32
HH = HD1 // 2
E0, I0 = 8, 16
E1, F1, TOPK1 = 64, 64, 4
SH, HS = 2, 256
EPS = 1e-5
RMS_EPS1 = 1.1920929e-07
LAMBDA_INIT = 0.2
NEG = -1.0e30

SLOT = (32, 64)
GROUPS = (4, 8)
UNITS = [[(0, 0)], [(0, 1), (0, 3)], [(0, 2), (1, 2)], [(1, 0)], [(1, 1), (1, 3)]]
PCOL = {mj: S * u + sum(S - P * j for _, j in unit[:n]) for u, unit in enumerate(UNITS) for n, mj in enumerate(unit)}
PW = len(UNITS) * S
PSLOTS = 3
STEPS = MAPS // 2 * len(UNITS)
NORMS = [(0, 0), (0, 1)] + [(k, b) for b in (0, 1) for k in (1, 2, 3, 4)] + \
        [(k, b) for b in (0, 1) for k in (5, 6)] + [(7, 0), (7, 1)]
TURNS = [(0, 0), (0, 1)] + [(k, b) for b in (0, 1) for k in (1, 2)] + [(3, 0), (3, 1)]
WEIGH_AT, SPREAD = (3, 2, 2, 2), (False, False, False, True)
TURN_LATER, MAX_STEPS = 3, STEPS + 1
OUT0, LN1, ADD1, NORM2, TURN1, INNER, EXPS, GATED, UP = 0, 6, 6, 11, 13, 17, 19, 22, 27
LN3, ADD3, NORM4, TURN2, PREP = 28, 30, 33, 39, 41
AFTER0 = PREP + TB + 2
OUT1, LN5, ADD5, NORM6, TURN3, ROUTE, ROUTED_EXP = 0, 3, 8, 14, 15, 16, 19
AFTER1 = ROUTED_EXP + 1
SHARED_AT = {OUT1 + TB: (0, 1), ROUTE + 1: (2, 3)}
SILU_AT = {NORM6: (0, 1), ROUTED_EXP: (2, 3)}
LATE = 7
NSB = SH * HS // P
NTILE = -(-(TOK * TOPK1 + E1 * (P - 1)) // P // 8) * 8
U = 8
LAG_GU, LAG_TA, LAG_D = 1, 3, 5
NBODY = NTILE // U
MAGIC = 12582912.0


def build(nc, x, rms_w, wqkv0, bqkv0, wo0, bo0, wrd0, up0, wqkv1, wo1, lvec, router1, rbias1, wgu1, wd1,
          wsgu, wsd, rope, ident_in, mask_in, before_in, out, h_dram, y_dram):
    f32, f32r, bf16, f16 = mybir.dt.float32, mybir.dt.float32r, mybir.dt.bfloat16, mybir.dt.float16
    u32, i32 = mybir.dt.uint32, mybir.dt.int32
    ALU, ACT, AX = mybir.AluOpType, mybir.ActivationFunctionType, mybir.AxisListType

    ctx = ExitStack()
    with ctx:
        def sb(name, shape, dt=f32):
            return ctx.enter_context(nc.sbuf_tensor(name, shape, dt))

        def at(name, offset, shape, dt):
            return nc.alloc_sbuf_tensor_at(name, shape, dt, offset=offset)

        def sem(name):
            return ctx.enter_context(nc.semaphore(name))

        X = sb("X", [P, NT, D])
        H = sb("H", [P, NT, D])
        XN = sb("XN", [P, NT, D])
        XT = sb("XT", [P, B, KT, S])
        QK = sb("QK", [P, 2, 2 * D])
        RA = sb("RA", [P, 2 * D])
        RB = sb("RB", [P, 2 * D])
        QP0 = sb("QP0", [P, B, TB, 2 * D])
        KP0 = sb("KP0", [P, 2, 2 * D])
        QKP1 = QP0[:, :, :, :].rearrange("p b t c -> p b (t c)").rearrange(
            "p r (a c) -> p r a c", a=2)
        arena = sb("arena", [P, 3 * 8192])
        base = nc.lookup_mloc(arena).addr
        QT = at("QT", base, [P, B, 8, S], f32r)
        KTr = at("KTr", base + 4 * 8192, [P, B, 8, S], f32r)
        PR = at("PR", base + 8 * 8192, [P, PSLOTS, PW], f32)
        RT = arena[:, 4 * 4096:4 * 4096 + D]
        WGU = arena[:, 0:E1 * KT * P]
        WD = arena[:, E1 * KT * P:E1 * KT * P + E1 // 2 * D]
        VA = sb("VA", [P, NT, HEADS0, 32])
        V1 = VA[:, :, :, :].rearrange("p t h c -> p t (h c)")[:, :, 0:D]
        OT = sb("OT", [P, 4, S])
        ones32 = sb("ones32", [P, 32])
        ident = sb("ident", [P, P])
        identb = sb("identb", [P, P], bf16)
        masksb = sb("masksb", [P, 2, P], bf16)
        rope_sb = sb("rope_sb", [P, TB, 4, ROT])
        wq_sb = sb("wq_sb", [P, KT, 3 * D])
        wo_sb = sb("wo_sb", [P, KT, D])
        bqkv_sb = sb("bqkv_sb", [P, 3 * D])
        bo_sb = sb("bo_sb", [P, D])
        rms_sb = sb("rms_sb", [P, KT])
        wrd_sb = sb("wrd_sb", [P, KT, E0 + E0 * I0])
        up_sb = sb("up_sb", [P, D])
        lv_sb = sb("lv_sb", [P, 4, HD1])
        lam_sb = sb("lam_sb", [P, 4])
        r1_sb = sb("r1_sb", [P, KT, E1])
        rb_sb = sb("rb_sb", [P, E1])
        iota_f = sb("iota_f", [P, E1])
        st = sb("st", [P, NT, 6])
        mv = sb("mv", [P, NT, 2])
        rstd = sb("rstd", [P, NT])
        msq = sb("msq", [P, NT])
        rr = sb("rr", [P, NT])
        mx = sb("mx", [P, NT, HEADS0])
        ss = sb("ss", [P, 2, 32])
        rs1 = sb("rs1", [P, 2, 32])
        den = sb("den", [P, 2, HEADS0])
        lgs = sb("lgs", [P, TB, E1])
        shl = sb("shl", [P, TB, E1])
        exl = sb("exl", [P, TB, E1])
        oh = sb("oh", [P, TB, E0])
        oh2 = sb("oh2", [P, TB, E0])
        top = sb("top", [P, TB, 8])
        idx = sb("idx", [P, TB, 8], u32)
        idxf = sb("idxf", [P, TB, 8])
        red = sb("red", [P, 2 * TB])
        eps_sb = sb("eps_sb", [P, 3])
        NA, NB = KP0[:, 0, :], KP0[:, 1, :]
        q0 = QP0[:, :, :, :].rearrange("p b t c -> p (b t c)")
        XG = q0[:, 0:U * D].rearrange("p (r c) -> p r c", r=U)
        XGT = q0[:, U * D:U * D + 4 * D].rearrange("p (r c) -> p r c", r=4)
        Y = q0[:, U * D + 4 * D:U * D + 8 * D].rearrange("p (r c) -> p r c", r=4)
        kf = KP0[:, :, :].rearrange("p r c -> p (r c)")
        A = kf[:, 0:4 * P].rearrange("p (r c) -> p r c", r=4)
        AT = kf[:, 4 * P:8 * P].rearrange("p (r c) -> p r c", r=4)
        SG = up_sb[:, :].rearrange("p (r c) -> p r c", r=4)
        vf = VA[:, :, :, :].rearrange("p t h c -> p (t h c)")
        halfv = NT * TOPK1 * E1 // 2
        OHB = [vf[:, 2 * b * halfv:(2 * b + 1) * halfv].rearrange("p (t k e) -> p t k e", t=TB, k=TOPK1)
               for b in range(B)]
        PRDB = [vf[:, (2 * b + 1) * halfv:(2 * b + 2) * halfv].rearrange("p (t k e) -> p t k e", t=TB, k=TOPK1)
                for b in range(B)]
        NC = NT * TOPK1
        LO1 = [vf[:, (2 * b + 1) * halfv:(2 * b + 2) * halfv].bitcast(f16).rearrange("p (n c) -> p n c", n=NC // 2)
               for b in range(B)]
        HI1 = wq_sb[:, :, :].rearrange("p k c -> p (k c)").bitcast(f16).rearrange(
            "p (n c) -> p n c", n=NC)
        WSGU = q0[:, U * D:U * D + 8 * D].rearrange("p (n c) -> p n c", n=NSB)
        WSD = QK[:, :, :].rearrange("p a c -> p (a c)").rearrange("p (n c) -> p n c", n=NSB)
        WSG2 = H[:, TB:TB + 2 * (2 * NSB - LATE), :].rearrange("p (n a) c -> p n (a c)", a=2)
        SACT = [[OT[:, 2 * n + h, :] if n < 2 else
                 XN[:, 4 * h + 2 * (n - 2):4 * h + 2 * (n - 1), :].rearrange("p a c -> p (a c)") for h in range(B)]
                for n in range(NSB)]
        MKF = kf[:, 4 * P:8 * P].rearrange("p (t e) -> p t e", e=E1)
        MK = sb("MK", [P, NT, E1], bf16)
        before = sb("before", [P, P], bf16)
        onesb = sb("onesb", [P, P], bf16)
        ones64 = sb("ones64", [P, E1])
        iota16 = sb("iota16", [P, P], f16)
        iotaf = RA[:, P:2 * P]
        tokid = sb("tokid", [P, NT])
        tile_no = sb("tile_no", [P, 1])
        tcnt = bqkv_sb[:, 0:4 * E1].rearrange("p (a e) -> p a e", a=4)
        slotf = sb("slotf", [P, NC])
        hi = sb("hi", [P, NC])
        lo = sb("lo", [P, NC])
        wk = sb("wk", [P, NC])
        wsum = sb("wsum", [P, 2 * NT])
        slotu = sb("slotu", [P, NC], u32)
        tok_of = sb("tok_of", [P, NTILE], u32)
        ecol = sb("ecol", [P, 2])
        ediag = sb("ediag", [P, P], bf16)
        erow = bqkv_sb[:, 4 * E1:4 * E1 + 2 * NTILE].rearrange("p (a t) -> p a t", a=2)
        odd = sb("odd", [P, 2, NTILE])
        TABG = sb("TABG", [1, NTILE + 2 * U], i32)
        TABW = sb("TABW", [1, NTILE + 2 * U], i32)

        PSUM = ctx.enter_context(nc.psum_tensor("PSUM", [P, 8, 512], f32))

        def bank(n, k=1):
            return PSUM[:, n:n + k, :].rearrange("p a c -> p (a c)")

        s_ld = sem("s_ld")
        s_x0 = sem("s_x0")
        s_x = sem("s_x")
        s_id = sem("s_id")
        s_wc = sem("s_wc")
        s_w0 = sem("s_w0")
        s_w1 = sem("s_w1")
        s_w1o = sem("s_w1o")
        s_dv = sem("s_dv")
        s_ac = sem("s_ac")
        s_fill = sem("s_fill")
        s_pool = sem("s_pool")
        s_const = sem("s_const")
        s_var = sem("s_var")
        s_rstd = sem("s_rstd")
        s_msq = sem("s_msq")
        s_rr = sem("s_rr")
        s_xn = sem("s_xn")
        s_xtps = sem("s_xtps")
        s_xt = sem("s_xt")
        s_qkv = sem("s_qkv")
        s_qkve = sem("s_qkve")
        s_ss = sem("s_ss")
        s_rs1 = sem("s_rs1")
        s_ro = sem("s_ro")
        s_hi = sem("s_hi")
        s_hi2 = sem("s_hi2")
        s_pad = sem("s_pad")
        s_tps = sem("s_tps")
        s_tev = sem("s_tev")
        s_mps = sem("s_mps")
        s_mrd = sem("s_mrd")
        s_neg = sem("s_neg")
        s_rqps = sem("s_rqps")
        s_rq = sem("s_rq")
        s_sc = sem("s_sc")
        s_p = sem("s_p")
        s_pv = sem("s_pv")
        s_pve = sem("s_pve")
        s_na = sem("s_na")
        s_otps = sem("s_otps")
        s_on = sem("s_on")
        s_ontps = sem("s_ontps")
        s_ont = sem("s_ont")
        s_wo = sem("s_wo")
        s_woe = sem("s_woe")
        s_qkve1 = sem("s_qkve1")
        s_ve = sem("s_ve")
        s_tevk = sem("s_tevk")
        s_woe1 = sem("s_woe1")
        s_rd = sem("s_rd")
        s_lmax = sem("s_lmax")
        s_ex = sem("s_ex")
        s_sig = sem("s_sig")
        s_aw = sem("s_aw")
        s_awps = sem("s_awps")
        s_awt = sem("s_awt")
        s_up = sem("s_up")
        s_upe = sem("s_upe")
        s_lamd = sem("s_lamd")
        s_lame = sem("s_lame")
        s_rt = sem("s_rt")
        s_rte = sem("s_rte")
        s_rex = sem("s_rex")
        s_oh = sem("s_oh")
        s_rank = sem("s_rank")
        s_ediag = sem("s_ediag")
        s_eps = sem("s_eps")
        s_hi1 = sem("s_hi1")
        s_hot = sem("s_hot")
        s_lo1 = sem("s_lo1")
        s_tok = sem("s_tok")
        s_idx = sem("s_idx")
        s_hd = [sem(f"s_hd{b}") for b in range(B)]
        s_wgu = sem("s_wgu")
        s_wd = sem("s_wd")
        s_ws2 = sem("s_ws2")
        s_ws = sem("s_ws")
        s_gu = sem("s_gu")
        s_sg = sem("s_sg")
        s_gt = sem("s_gt")
        s_gx = [sem(f"s_gx{r}") for r in range(U)]
        s_tx = sem("s_tx")
        s_xe = sem("s_xe")
        s_gup = sem("s_gup")
        s_sgs = sem("s_sgs")
        s_a = sem("s_a")
        s_ta = sem("s_ta")
        s_ate = sem("s_ate")
        s_d = sem("s_d")
        s_ye = sem("s_ye")
        s_st = [sem(f"s_st{r}") for r in range(4)]
        s_yg = [sem(f"s_yg{r}") for r in range(U)]
        s_sd = sem("s_sd")
        s_mx = sem("s_mx")
        s_fin = sem("s_fin")
        s_out = sem("s_out")

        block = ctx.enter_context(nc.Block())

        def slot(l, m):
            per = P // SLOT[l]
            return m // per, SLOT[l] * (m % per)

        def tunits(l):
            return [(a, 4 * n) for a in (0, 1) for n in range(GROUPS[l] // 4)]

        MHEADS = (4, 2, 1, 1)
        MUNITS = [(i, u) for i in range(TB) for u in range(HEADS0 // MHEADS[i])]

        tile_ends = [max(m for m, (j, _) in enumerate(MUNITS) if j == i) for i in range(TB)]
        MAX_OPS = [op for m in range(len(MUNITS)) for op in
                   [("max", m)] + [("turn", i) for i in range(TB - 1) if m == tile_ends[i] + TURN_LATER]] + \
                  [("turn", TB - 1)]

        def max_ops(step):
            return [(k, op) for k, op in enumerate(MAX_OPS) if k * (MAX_STEPS - 1) // (len(MAX_OPS) - 1) == step]

        def norm_no(k, b):
            return NORMS.index((k, b)) + 1

        def turn_no(k, b):
            return TURNS.index((k, b)) + 1

        def map_of(l, n):
            q, c = n // 4, n % 4
            return 4 * c + q if l == 0 else 2 * (4 * (q // 2) + c) + q % 2

        def high_parts(sc, did, settle, qp, kp, rq, rk, d):
            did(sc.activation(qp[:, :, 0:d].bitcast(f32r), rq, ACT.Copy))
            did(sc.activation(kp[:, :, 0:d].bitcast(f32r), rk, ACT.Copy))
            did(sc.activation(qp[:, :, d:2 * d].bitcast(f32r), rq, ACT.Copy))
            did(sc.activation(kp[:, :, 2 * d:3 * d].bitcast(f32r), rk, ACT.Copy), s_hi)

        def high_parts1(sc, did, qp, kp, rq, rk, d):
            did(sc.activation(qp[:, :, 0:d].bitcast(f32r), rq, ACT.Copy))
            did(sc.activation(kp[:, :, 0:d].bitcast(f32r), rk, ACT.Copy), s_hi)

        def more_high_parts1(dv, did, qp, kp, rq, rk, d):
            did(dv.tensor_copy(qp[:, :, d:2 * d].bitcast(f32r), rq))
            did(dv.tensor_copy(kp[:, :, 2 * d:3 * d].bitcast(f32r), rk), s_hi2)

        def low_parts(pool, qp, kp, rq, rk, d):
            pool.tensor_tensor(qp[:, :, 2 * d:3 * d], rq, qp[:, :, 0:d], ALU.subtract)
            pool.tensor_tensor(kp[:, :, d:2 * d], rk, kp[:, :, 0:d], ALU.subtract).then_inc(s_pad, 1)

        def parts0(c):
            qp = QP0[:, c // TB, c % TB, :].rearrange("p (h c) -> p h c", c=32)
            kp = KP0[:, c % 2, :].rearrange("p (h c) -> p h c", c=32)
            ra = QK[:, 1, c % 2 * D:(c % 2 + 1) * D].rearrange("p (h f) -> p h f", f=ROT)
            return qp, kp, ra[:, 0:16, :], ra[:, 16:32, :], ROT

        def parts1(c):
            qp = QKP1[:, c % 2, 1, :].rearrange("p (h c) -> p h c", c=64)
            kp = QKP1[:, c % 2, 0, :].rearrange("p (h c) -> p h c", c=64)
            q16 = QK[:, c % 2, :].rearrange("p (m d) -> p m d", d=HH)
            return qp, kp, q16[:, 0:16, :], q16[:, 16:32, :], HH

        def weighs_at(at, step):
            q, j = divmod(step - 2 * len(UNITS) - WEIGH_AT[at], 2 * len(UNITS))
            if not 0 <= q < 3:
                return None, ()
            if SPREAD[at]:
                return (q, (j,)) if j < TB else (None, ())
            return (q, range(TB)) if j == 0 else (None, ())

        def weighed_at(at, step):
            q, tiles = weighs_at(at, step)
            return q if TB - 1 in tiles else None

        @block.sync
        def _(sp):
            sp.dma_start(X[:, 0:TB, :], x[0:S, :].rearrange("(t p) d -> p t d", p=P)).then_inc(s_x0, 16)
            sp.dma_start(ident[:, :], ident_in).then_inc(s_id, 16)
            sp.dma_start(X[:, TB:NT, :], x[S:TOK, :].rearrange("(t p) d -> p t d", p=P)).then_inc(s_x, 16)
            sp.dma_start(rms_sb[:, :], rms_w).then_inc(s_wc, 16)
            sp.dma_start(wq_sb[:, :, :], wqkv0.rearrange("(k p) n -> p k n", p=P)).then_inc(s_wc, 16)
            sp.dma_start(bqkv_sb[:, :], bqkv0.partition_broadcast(P)).then_inc(s_wc, 16)
            sp.dma_start(rope_sb[:, :, :, :], rope).then_inc(s_wc, 16)
            sp.dma_start(bo_sb[:, :], bo0.partition_broadcast(P)).then_inc(s_w0, 16)
            sp.dma_start(wo_sb[:, :, :], wo0.rearrange("(k p) n -> p k n", p=P)).then_inc(s_w0, 16)
            sp.dma_start(wrd_sb[:, :, :], wrd0.rearrange("(k p) n -> p k n", p=P)).then_inc(s_w0, 16)
            sp.dma_start(up_sb[:, :], up0).then_inc(s_w0, 16)
            sp.dma_start(RB[:, 0:2 * P].rearrange("p (a c) -> p a c", a=2), mask_in).then_inc(s_ld, 16)
            sp.dma_start(RA[:, 0:P], before_in).then_inc(s_ld, 16)
            sp.dma_start(lv_sb[:, :, :].rearrange("p a c -> p (a c)"), lvec.partition_broadcast(P)).then_inc(s_ld, 16)
            sp.dma_start(r1_sb[:, :, :], router1.rearrange("(k p) n -> p k n", p=P)).then_inc(s_ld, 16)
            sp.dma_start(rb_sb[:, :], rbias1.partition_broadcast(P)).then_inc(s_ld, 16)
            sp.wait_ge(s_qkv, NT)
            sp.dma_start(wq_sb[:, :, :], wqkv1.rearrange("(k p) n -> p k n", p=P)).then_inc(s_w1, 16)
            sp.wait_ge(s_wo, NT // 2)
            sp.dma_start(wo_sb[:, :, :], wo1.rearrange("(k p) n -> p k n", p=P)).then_inc(s_w1o, 16)
            sp.wait_ge(s_tps, 2 * NT + 4 * NT)
            sp.dma_start(WSGU, wsgu.rearrange("n p c -> p n c")).then_inc(s_ws, 16)
            sp.dma_start(WSD, wsd.rearrange("n p c -> p n c")).then_inc(s_ws, 16)
            sp.wait_ge(s_pv, 16)
            for n in range(4):
                e = slice(16 * n, 16 * (n + 1))
                sp.dma_start(WGU[:, n * 4096:(n + 1) * 4096].rearrange("p (e c) -> p e c", e=16),
                             wgu1[e, :, :].rearrange("e p c -> p e c")).then_inc(s_wgu, 16)
            sp.wait_ge(s_xn, turn_no(3, 0))
            sp.dma_start(h_dram[0:S, :].rearrange("(t p) d -> p t d", p=P), XN[:, 0:TB, :]).then_inc(s_hd[0], 16)
            sp.wait_ge(s_xn, turn_no(3, 1))
            sp.dma_start(h_dram[S:TOK, :].rearrange("(t p) d -> p t d", p=P), XN[:, TB:NT, :]).then_inc(s_hd[1], 16)
            sp.dma_start(WSG2, wsgu[LATE - NSB:NSB].rearrange("n p c -> p n c")).then_inc(s_ws2, 16)
            for n in range(2):
                sp.dma_start(WD[:, n * 4096:(n + 1) * 4096].rearrange("p (e c) -> p e c", e=16),
                             wd1[16 * n:16 * (n + 1), :, :].rearrange("e p c -> p e c")).then_inc(s_wd, 16)

            def store(i, m, row):
                sp.wait_ge(s_ye, i + 1)
                sp.dma_start(row, Y[:, m % 4, :]).then_inc(s_st[m % 4], 16)

            y_rows = y_dram.rearrange("(j m p) d -> j m p d", m=U, p=P)
            with sp.Fori(0, NBODY) as j:
                for m in range(U):
                    store(U * j + m, m, y_rows[bass.ds(j, 1), m].rearrange("a p d -> (a p) d"))
            sp.wait_ge(s_fin, 1)
            sp.dma_start(out[0:S, :].rearrange("(t p) d -> p t d", p=P), X[:, 0:TB, :]).then_inc(s_out, 16)
            sp.wait_ge(s_fin, 2)
            sp.dma_start(out[S:TOK, :].rearrange("(t p) d -> p t d", p=P), X[:, TB:NT, :]).then_inc(s_out, 16)
            sp.wait_ge(s_out, 32)

        @block.gpsimd
        def _(pool):
            pool.memset(VA[:, :, :, :], 0.0).then_inc(s_fill, 1)
            pool.memset(KP0[:, :, :], 0.0).then_inc(s_fill, 1)
            pool.memset(QP0[:, :, :, :], 0.0)
            pool.wait_ge(s_fill, 2)
            pool.memset(VA[:, :, :, HD0:HD0 + 1], 1.0)
            pool.memset(KP0[:, :, :].rearrange("p r (h c) -> p r h c", c=32)[:, :, :, 3 * ROT:3 * ROT + 2], 1.0).then_inc(s_pool, 1)
            for c in range(NT):
                pool.wait_ge(s_hi, c + 1)
                low_parts(pool, *parts0(c))
            pool.iota(iota_f[:, :], [[1, E1]], base=0, channel_multiplier=0,
                      allow_small_or_imprecise_dtypes=True)
            pool.iota(iotaf[:, :], [[1, P]], base=0, channel_multiplier=0,
                      allow_small_or_imprecise_dtypes=True)
            pool.iota(tokid[:, :], [[P, NT]], base=0, channel_multiplier=1,
                      allow_small_or_imprecise_dtypes=True)
            pool.iota(tile_no[:, :], [[1, 1]], base=0, channel_multiplier=1,
                      allow_small_or_imprecise_dtypes=True).then_inc(s_pool, 1)
            for c in range(NT):
                pool.wait_ge(s_hi, NT + c + 1)
                low_parts(pool, *parts1(c))

            def shared_gate(u):
                sact = SACT[u % NSB][u // NSB]
                pool.wait_ge(s_sg, u + 1)
                pool.tensor_tensor(sact, sact, (RA, RB)[u % 2][:, :], ALU.mult).then_inc(s_gt, 1)

            for u in range(LATE):
                if u == 5:
                    for b in range(B):
                        hot = HI1[:, b * NC // 2:(b + 1) * NC // 2, 0:NTILE].rearrange("p (t k) c -> p t k c", k=TOPK1)
                        pool.wait_ge(s_hi1, b + 1)
                        pool.tensor_tensor(hot, hot, tokid[:, b * TB:(b + 1) * TB].unsqueeze(2).unsqueeze(3).broadcast_to(
                            [P, TB, TOPK1, NTILE]), ALU.mult).then_inc(s_hot, 1)
                shared_gate(u)
            for b in range(B):
                pool.wait_ge(s_hd[b], 16)
            pool.wait_ge(s_idx, 1)
            for i in range(NTILE):
                if i >= U:
                    pool.wait_ge(s_tx, i - U + 1)
                pool.indirect_dma_start(out=XG[:, i % U, :], out_offset=None, in_=h_dram,
                                        in_offset=bass.IndirectOffsetOnAxis(ap=tok_of[:, i:i + 1], axis=0)
                                        ).then_inc(s_gx[i % U], 16)
            pool.wait_ge(s_tx, NTILE)
            for r in range(4):
                pool.wait_ge(s_st[r], 16 * NTILE // 4)
            for n in range(NC):
                if n and n % U == 0 and LATE + n // U - 1 < 2 * NSB:
                    shared_gate(LATE + n // U - 1)
                if n >= U:
                    pool.wait_ge(s_mx, n - U + 1)
                pool.indirect_dma_start(out=XG[:, n % U, :], out_offset=None, in_=y_dram,
                                        in_offset=bass.IndirectOffsetOnAxis(ap=slotu[:, n:n + 1], axis=0)
                                        ).then_inc(s_yg[n % U], 16)

        @block.tensor
        def _(pe):
            def turn_tokens(k, b, first):
                pe.wait_ge(s_xn, turn_no(k, b))
                for kt in range(KT):
                    for i in range(TB):
                        mm = pe.transpose(bank(first + kt)[:, i * P:(i + 1) * P],
                                          XN[:, b * TB + i, kt * P:(kt + 1) * P], ident[:, :])
                mm.then_inc(s_xtps, 1)

            def project(b, i, qk, v):
                for kt in range(KT):
                    pe.matmul(qk, XT[:, b, kt, i * P:(i + 1) * P], wq_sb[:, kt, 0:2 * D],
                              start=(kt == 0), stop=(kt == KT - 1))
                for kt in range(KT):
                    mm = pe.matmul(v[:, 0:D], XT[:, b, kt, i * P:(i + 1) * P],
                                   wq_sb[:, kt, 2 * D:3 * D], start=(kt == 0), stop=(kt == KT - 1))
                mm.then_inc(s_qkv, 1)

            def turn_padded0(b, i):
                c = b * TB + i
                pe.wait_ge(s_pad, c + 1)
                for n, (q, g0) in enumerate(tunits(0)):
                    u = 2 * c + n
                    if u >= 4:
                        pe.wait_ge(s_tev, u - 3)
                    src = QP0[:, b, i, :] if q else KP0[:, c % 2, :]
                    for g in range(4):
                        mm = pe.transpose(bank(u % 4)[:, g * P:(g + 1) * P], src[:, g * P:(g + 1) * P], ident[:, :])
                    mm.then_inc(s_tps, 1)

            def maxima(b, m, o):
                i, u = MUNITS[m]
                nk = (i + 1) * P
                for k in range(MHEADS[i]):
                    n = MHEADS[i] * u + k
                    g, row = n % 4, 32 * (n // 4)
                    blk = o[:, k * nk:(k + 1) * nk]
                    pe.matmul(blk, QT[row:row + 32, b, g, i * P:(i + 1) * P], KTr[row:row + 32, b, g, 0:nk],
                              start=True, stop=False)
                    mm = pe.matmul(blk[:, i * P:nk], identb[:, :], masksb[:, 1, :], start=False, stop=True)
                mm.then_inc(s_mps, 1)

            def turn_again(b, i, o):
                pe.wait_ge(s_neg, b * TB + i + 1)
                for g in range(4):
                    mm = pe.transpose(o[:, g * P:(g + 1) * P], QP0[:, b, i, g * P:(g + 1) * P], ident[:, :])
                mm.then_inc(s_rqps, 1)

            def weigh(l, b, q, j):
                at = 2 * l + b
                pe.wait_ge(s_p, at * STEPS + 2 * len(UNITS) * (q + 1) - (1 if j == 0 else 0))
                c = 4 * at + q
                if c >= 2 and j == 0:
                    pe.wait_ge(s_pve, c - 1 + l)
                for ones in range(1 + l):
                    for k in range(4):
                        m = map_of(l, 4 * q + k)
                        pair = at * MAPS // 2 + 2 * q + k // 2
                        col = PCOL[k % 2, j]
                        if ones:
                            o, lhs = bank(5), ones32[:, :]
                        elif l:
                            o, lhs = bank(4), V1[:, b * TB + j, m // 2 * HD1:(m // 2 + 1) * HD1]
                        else:
                            o, lhs = bank(4 + q % 2), VA[:, b * TB + j, m, :]
                        mm = pe.matmul(o[32 * k:32 * k + 32, j * P:S], lhs, PR[:, pair % PSLOTS, col:col + S - j * P],
                                       start=(j == 0), stop=(j == TB - 1), tile_position=(0, 32 * k))
                if j == TB - 1:
                    mm.then_inc(s_pv, 1)

            def scores(l, b, step):
                c = (2 * l + b) * STEPS + step
                if c >= 4:
                    pe.wait_ge(s_p, c - 3)
                pair, u = step // len(UNITS), step % len(UNITS)
                off = 0
                for which, j in UNITS[u]:
                    g, row = slot(l, map_of(l, 2 * pair + which))
                    w = S - j * P
                    blk = bank(c % 4)[:, off:off + w]
                    off += w
                    pe.matmul(blk, KTr[row:row + SLOT[l], b, g, j * P:(j + 1) * P],
                              QT[row:row + SLOT[l], b, g, j * P:S], start=True, stop=False)
                    mm = pe.matmul(blk[:, 0:P], identb[:, :], masksb[:, 0, :], start=False, stop=True)
                mm.then_inc(s_sc, 1)

            def attend(l, b, beside, steps):
                for step in range(max(STEPS + 1, steps)):
                    if step < STEPS:
                        scores(l, b, step)
                        q, tiles = weighs_at(2 * l + b, step)
                        for j in tiles:
                            weigh(l, b, q, j)
                    elif step == STEPS:
                        for j in range(TB):
                            weigh(l, b, 3, j)
                    if step < steps:
                        beside(step)

            def max_beside(step):
                for k, (kind, n) in max_ops(step):
                    if k >= 2:
                        before_kind, before_n = MAX_OPS[k - 2]
                        if before_kind == "max":
                            pe.wait_ge(s_mrd, len(MUNITS) + before_n + 1)
                        else:
                            pe.wait_ge(s_rq, TB + before_n + 1)
                    if kind == "max":
                        maxima(1, n, bank(6 + k % 2))
                    else:
                        turn_again(1, n, bank(6 + k % 2))

            def after0(b, step):
                for r in range(TB // 2):
                    tiles, at, n = (2 * r, 2 * r + 1), OUT0 + 3 * r, b * TB // 2 + r
                    if step == at:
                        if r == 0:
                            pe.wait_ge(s_pve, 4 * (b + 1))
                        else:
                            pe.wait_ge(s_ont, n)
                            pe.wait_ge(s_woe, n)
                        for t in range(2):
                            for g in range(4):
                                mm = pe.transpose(bank(6 + t)[:, g * P:(g + 1) * P],
                                                  OT[:, g, tiles[t] * P:(tiles[t] + 1) * P], ident[:, :])
                        mm.then_inc(s_otps, 1)
                    if step == at + 1:
                        pe.wait_ge(s_on, n + 1)
                        for kt in range(KT):
                            for t in range(2):
                                mm = pe.transpose(bank(6)[:, (2 * kt + t) * P:(2 * kt + t + 1) * P],
                                                  XN[:, b * TB + tiles[t], kt * P:(kt + 1) * P], ident[:, :])
                        mm.then_inc(s_ontps, 1)
                    if step == at + 2:
                        pe.wait_ge(s_ont, n + 1)
                        for t in range(2):
                            for kt in range(KT):
                                mm = pe.matmul(bank(7)[:, t * D:(t + 1) * D], XT[:, b, kt, tiles[t] * P:(tiles[t] + 1) * P],
                                               wo_sb[:, kt, :], start=(kt == 0), stop=(kt == KT - 1))
                        mm.then_inc(s_wo, 1)
                if step == TURN1:
                    turn_tokens(1, b, 6)
                if step == INNER:
                    pe.wait_ge(s_xt, turn_no(1, b))
                    for i in range(TB):
                        xt = [XT[:, b, kt, i * P:(i + 1) * P] for kt in range(KT)]
                        for kt in range(KT):
                            pe.matmul(bank(6)[:, i * E0:(i + 1) * E0], xt[kt], wrd_sb[:, kt, 0:E0],
                                      start=(kt == 0), stop=(kt == KT - 1))
                        for kt in range(KT):
                            mm = pe.matmul(bank(7)[:, i * P:(i + 1) * P], xt[kt], wrd_sb[:, kt, E0:E0 + E0 * I0],
                                           start=(kt == 0), stop=(kt == KT - 1))
                    mm.then_inc(s_rd, 1)
                if step == GATED:
                    pe.wait_ge(s_aw, b + 1)
                    for i in range(TB):
                        mm = pe.transpose(bank(6)[:, i * P:(i + 1) * P], RB[:, i * P:(i + 1) * P], ident[:, :])
                    mm.then_inc(s_awps, 1)
                if step == UP:
                    pe.wait_ge(s_awt, b + 1)
                    for i in range(TB):
                        mm = pe.matmul(bank(6 + i // 2)[:, i % 2 * D:(i % 2 + 1) * D], RA[:, i * P:(i + 1) * P],
                                       up_sb[:, :], start=True, stop=True)
                    mm.then_inc(s_up, 1)
                if step == TURN2:
                    turn_tokens(2, b, 6)
                i = step - PREP
                if 0 <= i < TB:
                    c = b * TB + i
                    if i == 0:
                        pe.wait_ge(s_w1, 16)
                        pe.wait_ge(s_xt, turn_no(2, b))
                    if i == 1:
                        pe.wait_ge(s_pve, 4 * (b + 2))
                    if i >= 2:
                        pe.wait_ge(s_qkve1, c - 1)
                        pe.wait_ge(s_ve, c - 1)
                    project(b, i, bank(6 - 2 * (i % 2)), bank(7 - 2 * (i % 2)))
                i = step - PREP - 2
                if 0 <= i < TB:
                    c = b * TB + i
                    pe.wait_ge(s_pad, NT + c + 1)
                    pe.wait_ge(s_hi2, c + 1)
                    for n, (q, g0) in enumerate(tunits(1)):
                        if i == 0:
                            pe.wait_ge(s_p, (b + 2) * STEPS)
                        elif q:
                            pe.wait_ge(s_tev, 2 * NT + 2 * (c - 1) + n - 1)
                        else:
                            pe.wait_ge(s_tevk, 2 * (c - 1) + n + 1)
                        for g in range(4):
                            mm = pe.transpose(bank(n)[:, g * P:(g + 1) * P],
                                              QKP1[:, c % 2, q, (g0 + g) * P:(g0 + g + 1) * P], ident[:, :])
                        mm.then_inc(s_tps, 1)

            def shared_up(u):
                if u == 0:
                    pe.wait_ge(s_ws, 32)
                    pe.wait_ge(s_p, 4 * STEPS)
                if u == LATE:
                    pe.wait_ge(s_ws2, 16)
                if u >= 2:
                    pe.wait_ge(s_sg, u - 1)
                w = WSGU[:, u % NSB, :] if u < LATE else WSG2[:, u - LATE, :]
                for part in range(2):
                    for kt in range(KT):
                        w0 = (part * KT + kt) * P
                        mm = pe.matmul(bank(2 * (u % 2) + part), w[:, w0:w0 + P], XT[:, u // NSB, kt, :],
                                       start=(kt == 0), stop=(kt == KT - 1))
                mm.then_inc(s_gu, 1)

            def after1(b, step):
                if b:
                    for u in SHARED_AT.get(step, ()):
                        shared_up(u)
                for i in range(TB):
                    if step == OUT1 + i:
                        c = b * TB + i
                        if i == 0:
                            pe.wait_ge(s_w1o, 16)
                            pe.wait_ge(s_pve, 8 + 4 * (b + 1))
                        if i >= 2:
                            pe.wait_ge(s_woe1, c - 1)
                        for kt in range(KT):
                            mm = pe.matmul(bank(6 + i % 2)[:, 0:D], XT[:, b, kt, i * P:(i + 1) * P], wo_sb[:, kt, :],
                                           start=(kt == 0), stop=(kt == KT - 1))
                        mm.then_inc(s_wo, 1)
                if step == TURN3:
                    turn_tokens(3, b, 6)
                if step == ROUTE:
                    pe.wait_ge(s_xt, turn_no(3, b))
                    for i in range(TB):
                        for kt in range(KT):
                            mm = pe.matmul(bank(6)[:, i * E1:(i + 1) * E1], XT[:, b, kt, i * P:(i + 1) * P],
                                           r1_sb[:, kt, :], start=(kt == 0), stop=(kt == KT - 1))
                    mm.then_inc(s_rt, 1)

            pe.wait_ge(s_id, 16)
            for b in range(B):
                turn_tokens(0, b, 2 * b)
            pe.wait_ge(s_wc, 64)
            pe.wait_ge(s_xt, 2)
            for c in range(NT):
                if c >= 2:
                    pe.wait_ge(s_qkve, c - 1)
                project(c // TB, c % TB, bank(4 + c % 2), bank(6 + c % 2))
                if c >= 1:
                    turn_padded0((c - 1) // TB, (c - 1) % TB)
            turn_padded0(B - 1, TB - 1)
            pe.wait_ge(s_tev, 2 * NT)
            pe.wait_ge(s_qkve, NT)
            pe.wait_ge(s_const, 2)
            pe.wait_ge(s_w0, 64)
            pe.wait_ge(s_ld, 80)
            for m in range(len(MUNITS)):
                if m >= 4:
                    pe.wait_ge(s_mrd, m - 3)
                maxima(0, m, bank(4 + m % 4))
            for i in range(TB):
                turn_again(0, i, bank(i))
            pe.wait_ge(s_rq, TB)
            pe.wait_ge(s_mrd, len(MUNITS))
            attend(0, 0, max_beside, MAX_STEPS)
            pe.wait_ge(s_rq, 2 * TB)
            attend(0, 1, lambda step: after0(0, step), AFTER0)
            pe.wait_ge(s_tev, 2 * NT + 2 * TB)
            pe.wait_ge(s_tevk, 2 * TB)
            pe.wait_ge(s_ve, TB)
            attend(1, 0, lambda step: after0(1, step), AFTER0)
            pe.wait_ge(s_tev, 2 * NT + 2 * NT)
            pe.wait_ge(s_tevk, 2 * NT)
            pe.wait_ge(s_ve, NT)
            attend(1, 1, lambda step: after1(0, step), AFTER1)
            for step in range(AFTER1):
                after1(1, step)

            pe.wait_ge(s_oh, B)
            for c in range(NT):
                o = bank(4)[:, c * E1:(c + 1) * E1]
                pe.matmul(o, before[:, :], MK[:, c, :], start=True, stop=(c == 0))
                for c2 in range(c):
                    pe.matmul(o, onesb[:, :], MK[:, c2, :], start=False, stop=(c2 == c - 1))
            for c in range(NT):
                mm = pe.matmul(bank(7)[:, 0:E1], onesb[:, :], MK[:, c, :], start=(c == 0), stop=(c == NT - 1))
            mm.then_inc(s_rank, 1)
            shared_up(4)
            pe.wait_ge(s_ediag, 1)
            pe.matmul(bank(7)[:, 0:P], onesb[:, :], ediag[:, :], start=True, stop=True).then_inc(s_eps, 1)
            shared_up(5)
            shared_up(6)
            for n in range(NC):
                if n % (NC // 2) == 0:
                    pe.wait_ge(s_hot, n // (NC // 2) + 1)
                    pe.wait_ge(s_lo1, n // (NC // 2) + 1)
                mm = pe.matmul(bank(5)[:, 0:NTILE], LO1[n // (NC // 2)][:, n % (NC // 2), :], HI1[:, n, 0:NTILE], start=(n == 0), stop=(n == NC - 1))
            mm.then_inc(s_tok, 1)

            def columns(tab, top, i):
                _, v = nc.values_load_multi_w_load_instructions(
                    tab[0:1, bass.ds(i, 4)], engines=[mybir.EngineType.PE], min_val=0, max_val=top,
                    skip_runtime_bounds_check_because="the expert is at most 63")
                return v

            cols = {}

            def step(i, m):
                fixed = isinstance(i, int)

                def has(lag):
                    return not fixed or 0 <= i - lag < NTILE

                def wait(s, value):
                    if not fixed or value > 0:
                        pe.wait_ge(s, value)

                if has(0):
                    pe.wait_ge(s_gx[m], 2 * i - 2 * m + 16)
                    wait(s_xe, i - 1)
                    for kt in range(KT):
                        mm = pe.transpose(bank(m % 2)[:, kt * P:(kt + 1) * P], XG[:, m, kt * P:(kt + 1) * P], ident[:, :])
                    mm.then_inc(s_tx, 1)
                if m % 4 == 0:
                    cols["down"] = columns(TABW, (E1 // 2 - 1) * D, i)
                if has(LAG_D):
                    t, r = i - LAG_D, (m - LAG_D) % 4
                    pe.wait_ge(s_ate, t + 1)
                    wait(s_ye, t - 1)
                    pe.matmul(bank(6 + r % 2)[:, 0:D], AT[:, r, :], WD[:, bass.ds(cols["down"][m % 4], D)],
                              start=True, stop=True).then_inc(s_d, 1)
                if m % 4 == 0:
                    cols["up"] = columns(TABG, (E1 - 1) * KT * P, i)
                if has(LAG_GU):
                    t, r = i - LAG_GU, (m - LAG_GU) % 4
                    pe.wait_ge(s_xe, t + 1)
                    wait(s_a, t - 1)
                    for kt in range(KT):
                        mm = pe.matmul(bank(2 + r % 2)[:, 0:P], XGT[:, r, kt * P:(kt + 1) * P],
                                       WGU[:, bass.ds(cols["up"][m % 4] + kt * P, P)], start=(kt == 0), stop=(kt == KT - 1))
                    mm.then_inc(s_gup, 1)
                if has(LAG_TA):
                    t, r = i - LAG_TA, (m - LAG_TA) % 4
                    pe.wait_ge(s_a, t + 1)
                    wait(s_ate, t - 1)
                    pe.transpose(bank(4 + r % 2)[:, 0:P], A[:, r, :], ident[:, :]).then_inc(s_ta, 1)

            pe.wait_ge(s_wgu, 64)
            pe.wait_ge(s_wd, 32)
            pe.wait_ge(s_idx, 1)
            pe.wait_ge(s_sg, LATE)
            for m in range(U):
                step(m, m)
            with pe.Fori(1, NBODY) as j:
                for m in range(U):
                    step(U * j + m, m)
            for m in range(LAG_D):
                step(NTILE + m, m)

            def shared_down(c):
                for n in range(NSB):
                    mm = pe.matmul(bank(4 + c // 2)[:, c % 2 * D:(c % 2 + 1) * D],
                                   SACT[n][c // TB][:, c % TB * P:(c % TB + 1) * P], WSD[:, n, :],
                                   start=(n == 0), stop=(n == NSB - 1))
                if c % 2:
                    mm.then_inc(s_sd, 1)

            pe.wait_ge(s_ye, NTILE)
            pe.wait_ge(s_gt, NSB)
            for c in range(TB):
                shared_down(c)
            for u in range(LATE, 2 * NSB):
                shared_up(u)
            pe.wait_ge(s_gt, 2 * NSB)
            for c in range(TB, NT):
                shared_down(c)

        @block.scalar
        def _(sc):
            last = [None, 0]
            counts = {}

            def did(ins, s=None):
                s = s or s_ac
                ins.then_inc(s, 1)
                counts[id(s)] = counts.get(id(s), 0) + 1
                last[:] = [s, counts[id(s)]]

            def settle():
                sc.wait_ge(last[0], last[1])

            def root(src, dst, bias, s):
                did(sc.activation(dst, src, ACT.Ln, bias=bias, scale=1.0))
                settle()
                did(sc.activation(dst, dst, ACT.Exp, scale=-0.5), s)

            def rstd_of(k, b):
                sc.wait_ge(s_var, norm_no(k, b))
                t = slice(b * TB, (b + 1) * TB)
                root(mv[:, t, 1], rstd[:, t], eps_sb[:, 0:1], s_rstd)

            def store_xt(k, b, first):
                sc.wait_ge(s_xtps, turn_no(k, b))
                for kt in range(KT):
                    ins = sc.activation(XT[:, b, kt, :], bank(first + kt), ACT.Copy,
                                        scale=rms_sb[:, kt:kt + 1] if k == 0 else 1.0)
                    did(ins, s_xt if kt == KT - 1 else None)

            def store_padded(b, i, u, q, g0, o):
                sc.wait_ge(s_tps, u + 1)
                dst = (QT if q else KTr)[:, b, g0:g0 + 4, i * P:(i + 1) * P]
                did(sc.activation(dst, o.rearrange("p (g c) -> p g c", g=4), ACT.Copy), s_tev)

            def store_again(b, i, o):
                sc.wait_ge(s_rqps, b * TB + i + 1)
                did(sc.activation(QT[:, b, 0:4, i * P:(i + 1) * P], o.rearrange("p (g c) -> p g c", g=4), ACT.Copy), s_rq)

            def attend(l, b, beside, steps):
                for step in range(max(STEPS + 1, steps)):
                    if step < STEPS:
                        c = (2 * l + b) * STEPS + step
                        pair, u = c // len(UNITS), c % len(UNITS)
                        sc.wait_ge(s_sc, c + 1)
                        if pair >= PSLOTS and u == 0:
                            sc.wait_ge(s_pv, (pair - PSLOTS) // 2 + 1)
                        did(sc.activation(PR[:, pair % PSLOTS, u * S:(u + 1) * S], bank(c % 4), ACT.Exp,
                                          scale=0.5 if l == 0 else 4.0), s_p)
                    if step < STEPS and weighed_at(2 * l + b, step) is not None:
                        sums(l, b, weighed_at(2 * l + b, step))
                    elif step == STEPS:
                        sums(l, b, 3)
                    if step < steps:
                        beside(step)

            def sums(l, b, q):
                if l:
                    n = b * 4 + q
                    sc.wait_ge(s_pv, 8 + n + 1)
                    if n:
                        sc.wait_ge(s_pve, 8 + n)
                    did(sc.activation(NA, bank(5), ACT.Ln))
                    settle()
                    did(sc.activation(NA, NA, ACT.Exp, scale=-1.0), s_na)

            def max_beside(step):
                for k, (kind, n) in max_ops(step):
                    if kind == "turn":
                        store_again(1, n, bank(6 + k % 2))

            def after0(b, step):
                for r in range(TB // 2):
                    if step == OUT0 + 3 * r + 1:
                        sc.wait_ge(s_ontps, b * TB // 2 + r + 1)
                        did(sc.activation(XT[:, b, :, 2 * r * P:2 * (r + 1) * P],
                                          bank(6).rearrange("p (k c) -> p k c", k=KT), ACT.Copy), s_ont)
                for k, at in ((1, ADD1), (2, NORM2), (3, ADD3), (4, NORM4)):
                    if step == at:
                        rstd_of(k, b)
                if step == TURN1:
                    store_xt(1, b, 6)
                if step == EXPS:
                    sc.wait_ge(s_lmax, b + 1)
                    did(sc.activation(exl[:, :, 0:E0], shl[:, :, 0:E0], ACT.Exp))
                    did(sc.activation(RB[:, :], RA[:, :], ACT.Exp, scale=-1.0), s_ex)
                    settle()
                    did(sc.activation(RB[:, :], RB[:, :], ACT.Ln, bias=eps_sb[:, 2:3], scale=1.0))
                    settle()
                    did(sc.activation(RB[:, :], RB[:, :], ACT.Exp, scale=-1.0), s_sig)
                if step == GATED:
                    sc.wait_ge(s_awps, b + 1)
                    did(sc.activation(RA[:, :], bank(6), ACT.Copy), s_awt)
                if step == TURN2:
                    store_xt(2, b, 6)
                for i in range(TB):
                    c = b * TB + i
                    if step == PREP + i + 2:
                        sc.wait_ge(s_ro, NT + c + 1)
                        if c >= 2:
                            sc.wait_ge(s_tps, 2 * NT + 4 * (c - 1))
                        high_parts1(sc, did, *parts1(c))
                    if step == PREP + i + 1:
                        sc.wait_ge(s_ss, c + 1)
                        root(ss[:, c % 2, :], rs1[:, c % 2, :], eps_sb[:, 1:2], s_rs1)
                    if step == PREP + i:
                        sc.wait_ge(s_qkv, NT + c + 1)
                        if c >= 2:
                            sc.wait_ge(s_pad, NT + c - 1)
                        if i:
                            sc.wait_ge(s_ss, c)
                        did(sc.activation(RA[:, :], bank(6 - 2 * (i % 2)), ACT.Square))
                        did(sc.activation(QK[:, c % 2, :], bank(6 - 2 * (i % 2)), ACT.Copy), s_qkve1)
                i = step - PREP - 2
                if 0 <= i < TB:
                    c = b * TB + i
                    for n in (2, 3):
                        store_padded(b, i, 2 * NT + 4 * c + n, *tunits(1)[n], bank(n))

            def shared_silu(u):
                sc.wait_ge(s_gu, u + 1)
                if u >= 2:
                    sc.wait_ge(s_gt, u - 1)
                if u % NSB == 2:
                    sc.wait_ge(s_hd[u // NSB], 16)
                did(sc.activation((RA, RB)[u % 2][:, :], bank(2 * (u % 2)), ACT.Silu))
                did(sc.activation(SACT[u % NSB][u // NSB], bank(2 * (u % 2) + 1), ACT.Copy), s_sg)

            def after1(b, step):
                for i in range(TB):
                    if step == OUT1 + i:
                        c = b * TB + i
                        sc.wait_ge(s_wo, NT // 2 + c + 1)
                        did(sc.activation(H[:, c, :], bank(6 + i % 2)[:, 0:D], ACT.Copy, scale=1.0 - LAMBDA_INIT), s_woe1)
                for k, at in ((5, ADD5), (6, NORM6)):
                    if step == at:
                        rstd_of(k, b)
                if step == TURN3:
                    store_xt(3, b, 6)
                if step == ROUTED_EXP:
                    sc.wait_ge(s_rte, b + 1)
                    did(sc.activation(exl[:, :, :], shl[:, :, :], ACT.Exp), s_rex)
                if b:
                    for u in SILU_AT.get(step, ()):
                        shared_silu(u)

            sc.preload_act_table_set("natural_log_exp_and_others")
            sc.wait_ge(s_const, 1)
            for b in range(B):
                rstd_of(0, b)
                sc.wait_ge(s_msq, b + 1)
                root(msq[:, b * TB:(b + 1) * TB], rr[:, b * TB:(b + 1) * TB], eps_sb[:, 0:1], s_rr)
            sc.wait_ge(s_wc, 64)
            for b in range(B):
                store_xt(0, b, 2 * b)
            sc.wait_ge(s_pool, 1)
            for c in range(NT + 1):
                if c < NT:
                    sc.wait_ge(s_ro, c + 1)
                    if c >= 2:
                        sc.wait_ge(s_tps, 2 * (c - 1))
                    high_parts(sc, did, settle, *parts0(c))
                for n in range(2 if c else 0):
                    u = 2 * (c - 1) + n
                    store_padded((c - 1) // TB, (c - 1) % TB, u, *tunits(0)[n], bank(u % 4))
            sc.wait_ge(s_lamd, 1)
            did(sc.activation(lam_sb[:, 2:4], lam_sb[:, 0:2], ACT.Exp), s_lame)
            for i in range(TB):
                store_again(0, i, bank(i))
            attend(0, 0, max_beside, MAX_STEPS)
            attend(0, 1, lambda step: after0(0, step), AFTER0)
            attend(1, 0, lambda step: after0(1, step), AFTER0)
            attend(1, 1, lambda step: after1(0, step), AFTER1)
            for step in range(AFTER1):
                after1(1, step)

            for u in range(4, LATE):
                shared_silu(u)

            def step(i, m):
                fixed = isinstance(i, int)

                def wait(s, value):
                    if not fixed or value > 0:
                        sc.wait_ge(s, value)

                if not fixed or i < NTILE:
                    sc.wait_ge(s_tx, i + 1)
                    wait(s_gup, i - 3)
                    sc.activation(XGT[:, m % 4, :], bank(m % 2)[:, 0:D], ACT.Copy).then_inc(s_xe, 1)
                if not fixed or i >= 1:
                    r = (m - 1) % 4
                    sc.wait_ge(s_gup, i)
                    wait(s_a, i - 4)
                    sc.activation(SG[:, r, :], bank(2 + r % 2)[:, 0:F1], ACT.Silu).then_inc(s_sgs, 1)

            for m in range(U):
                step(m, m)
            with sc.Fori(1, NBODY) as j:
                for m in range(U):
                    step(U * j + m, m)
            step(NTILE, 0)
            for u in range(LATE, 2 * NSB):
                shared_silu(u)
            for b in range(B):
                rstd_of(7, b)

        @block.vector
        def _(dv):
            last = [None, 0]
            counts = {}

            def did(ins, s=None):
                s = s or s_dv
                ins.then_inc(s, 1)
                counts[id(s)] = counts.get(id(s), 0) + 1
                last[:] = [s, counts[id(s)]]

            def settle():
                dv.wait_ge(last[0], last[1])

            def stats(k, b, src):
                for i in range(TB):
                    did(dv.bn_stats(st[:, b * TB + i, :], src[:, b * TB + i, :]))
                settle()
                for i in range(TB):
                    t = b * TB + i
                    did(dv.bn_aggr(mv[:, t, :], st[:, t, :]), s_var if i == TB - 1 else None)

            def normalise(k, b, src, dst, s=None):
                dv.wait_ge(s_rstd, norm_no(k, b))
                for i in range(TB):
                    t = b * TB + i
                    did(dv.tensor_scalar(dst[:, t, :], src[:, t, :], mv[:, t, 0:1], rstd[:, t:t + 1],
                                         ALU.subtract, ALU.mult), s if i == TB - 1 else None)

            def add_norm(k, b):
                normalise(k, b, H, H)
                settle()
                t = slice(b * TB, (b + 1) * TB)
                did(dv.tensor_tensor(X[:, t, :], X[:, t, :], H[:, t, :], ALU.add))
                settle()

            def bc(ap, n):
                return ap.unsqueeze(1).broadcast_to([P, n, ap.shape[-1]])

            did(dv.memset(eps_sb[:, 0:1], EPS))
            did(dv.memset(eps_sb[:, 1:2], HH * RMS_EPS1))
            did(dv.memset(eps_sb[:, 2:3], 1.0), s_const)
            for b in range(B):
                dv.wait_ge((s_x0, s_x)[b], 16)
                stats(0, b, X)
            for b in range(B):
                t = slice(b * TB, (b + 1) * TB)
                dv.wait_ge(s_rstd, b + 1)
                did(dv.tensor_tensor(msq[:, t], mv[:, t, 1], rstd[:, t], ALU.mult))
                settle()
                did(dv.tensor_tensor(msq[:, t], msq[:, t], rstd[:, t], ALU.mult), s_msq)
                normalise(0, b, X, H)
                dv.wait_ge(s_rr, b + 1)
                settle()
                for i in range(TB):
                    c = b * TB + i
                    did(dv.tensor_scalar(XN[:, c, :], H[:, c, :], rr[:, c:c + 1], None, ALU.mult),
                        s_xn if i == TB - 1 else None)
            did(dv.memset(ones32[:, :], 1.0))
            did(dv.memset(onesb[:, :], 1.0))
            did(dv.memset(ones64[:, :], 1.0))
            did(dv.memset(TABG[:, :], 0))
            did(dv.memset(TABW[:, :], 0))
            dv.wait_ge(s_pool, 1)
            dv.wait_ge(s_wc, 64)
            for b in range(B):
                for i in range(TB):
                    c = b * TB + i
                    if c == 2:
                        dv.wait_ge(s_ld, 80)
                        did(dv.tensor_copy(identb[:, :], ident[:, :]))
                        did(dv.tensor_copy(masksb[:, :, :], RB[:, 0:2 * P].rearrange("p (a c) -> p a c", a=2)))
                        did(dv.tensor_copy(before[:, :], RA[:, 0:P]), s_const)
                    dv.wait_ge(s_qkv, c + 1)
                    settle()
                    did(dv.tensor_tensor(VA[:, c, :, 0:HD0], bank(6 + i % 2)[:, 0:D].rearrange("p (h c) -> p h c", c=HD0),
                                         bqkv_sb[:, 2 * D:3 * D].rearrange("p (h c) -> p h c", c=HD0), ALU.add))
                    did(dv.tensor_tensor(QK[:, 0, :], bank(4 + i % 2), bqkv_sb[:, 0:2 * D], ALU.add), s_qkve)
                    settle()
                    if c >= 2:
                        dv.wait_ge(s_pad, c - 1)
                    pairs = QK[:, 0, :].rearrange("p (h f t) -> p h f t", f=ROT, t=2)
                    ra = QK[:, 1, c % 2 * D:(c % 2 + 1) * D].rearrange("p (h f) -> p h f", f=ROT)
                    rb = RT[:, :].rearrange("p (h f) -> p h f", f=ROT)
                    did(dv.tensor_tensor(ra, pairs[:, :, :, 0], bc(rope_sb[:, i, 0, :], 32), ALU.mult))
                    did(dv.tensor_tensor(rb, pairs[:, :, :, 1], bc(rope_sb[:, i, 1, :], 32), ALU.mult))
                    settle()
                    did(dv.tensor_tensor(ra, ra, rb, ALU.add), s_ro)
            def maxima(b, m, o):
                i, u = MUNITS[m]
                dv.wait_ge(s_mps, b * len(MUNITS) + m + 1)
                nh, nk, c = MHEADS[i], (i + 1) * P, b * TB + i
                did(dv.tensor_reduce(mx[:, c, nh * u:nh * u + nh], o[:, 0:nh * nk].rearrange("p (h k) -> p h k", h=nh),
                                     AX.X, ALU.max), s_mrd)
                if u == HEADS0 // nh - 1:
                    qp = QP0[:, b, i, :].rearrange("p (g r c) -> p g r c", r=4, c=32)
                    mxs = mx[:, c, :].rearrange("p (r g) -> p g r", g=4)
                    settle()
                    did(dv.tensor_scalar(qp[:, :, :, 3 * ROT].bitcast(f32r), mxs, -1.0, None, ALU.mult))
                    settle()
                    did(dv.scalar_tensor_tensor(out=qp[:, :, :, 3 * ROT + 1], in0=mxs, scalar=-1.0,
                                                in1=qp[:, :, :, 3 * ROT], op0=ALU.mult, op1=ALU.subtract), s_neg)

            def choose(b, E, k, lg, bias):
                src = lgs[:, :, 0:E]
                did(dv.tensor_reduce(red[:, 0:TB], lg, AX.X, ALU.max))
                if bias is not None:
                    did(dv.tensor_tensor(src, lg, bias, ALU.add))
                else:
                    did(dv.tensor_copy(src, lg))
                settle()
                did(dv.tensor_tensor(shl[:, :, 0:E], lg, red[:, 0:TB].unsqueeze(2).broadcast_to([P, TB, E]), ALU.subtract))
                for i in range(TB):
                    did(dv.max(top[:, i, :], lgs[:, i, 0:E]))
                settle()
                for i in range(TB):
                    did(dv.max_index(idx[:, i, :], top[:, i, :], lgs[:, i, 0:E]))
                settle()
                did(dv.tensor_copy(idxf[:, :, :], idx[:, :, :]))
                for n in range(k):
                    settle()
                    did(dv.tensor_tensor((oh if n == 0 else oh2)[:, :, 0:E], bc(iota_f[:, 0:E], TB),
                                         idxf[:, :, n].unsqueeze(2).broadcast_to([P, TB, E]), ALU.is_equal))
                    if n:
                        settle()
                        did(dv.tensor_tensor(oh[:, :, 0:E], oh[:, :, 0:E], oh2[:, :, 0:E], ALU.add))

            def evacuate(l, b, q):
                if l == 0:
                    if b and q == 0:
                        dv.wait_ge(s_otps, TB // 2)
                    dv.wait_ge(s_pv, b * 4 + q + 1)
                    did(dv.tensor_copy(OT[:, q, :], bank(4 + q % 2)), s_pve)
                    return
                dv.wait_ge(s_pv, 8 + b * 4 + q + 1)
                G, half = q // 2, q % 2
                dv.wait_ge(s_na, b * 4 + q + 1)
                settle()
                if half == 0:
                    did(dv.tensor_tensor(XT[:, b, G, :], bank(4), NA, ALU.mult), s_pve)
                else:
                    did(dv.scalar_tensor_tensor(out=NB, in0=bank(4), scalar=lam_sb[:, 1:2], in1=NA,
                                                op0=ALU.mult, op1=ALU.mult))
                    settle()
                    did(dv.tensor_tensor(XT[:, b, G, :], XT[:, b, G, :], NB, ALU.add), s_pve)

            def attend(l, b, beside, steps):
                for step in range(max(STEPS + 1, steps)):
                    if step < STEPS and weighed_at(2 * l + b, step) is not None:
                        evacuate(l, b, weighed_at(2 * l + b, step))
                    elif step == STEPS:
                        evacuate(l, b, 3)
                    if step < steps:
                        beside(step)

            def max_beside(step):
                for k, (kind, n) in max_ops(step):
                    if kind == "max":
                        maxima(1, n, bank(6 + k % 2))

            def after0(b, step):
                for r in range(TB // 2):
                    at, n = OUT0 + 3 * r, b * TB // 2 + r
                    if step == at:
                        dv.wait_ge(s_otps, n + 1)
                        settle()
                        did(dv.reciprocal(den[:, :, :], bank(6, 2).rearrange("p (t h c) -> p t h c", t=2, c=32)[:, :, :, HD0]))
                        settle()
                        for t in range(2):
                            did(dv.tensor_tensor(XN[:, b * TB + 2 * r + t, :].rearrange("p (k q c) -> p q k c", k=4, c=HD0),
                                                 bank(6 + t).rearrange("p (q k c) -> p q k c", q=4, c=32)[:, :, :, 0:HD0],
                                                 den[:, t, :].rearrange("p (q k) -> p q k", q=4).unsqueeze(3).broadcast_to(
                                                     [P, 4, 4, HD0]), ALU.mult), s_on if t else None)
                    if step == at + 2:
                        dv.wait_ge(s_wo, n + 1)
                        h = H[:, b * TB + 2 * r:b * TB + 2 * r + 2, :].rearrange("p t c -> p (t c)")
                        did(dv.tensor_tensor(h, h, bank(7), ALU.add), s_woe)
                if step == LN1:
                    settle()
                    stats(1, b, H)
                if step == ADD1:
                    add_norm(1, b)
                    stats(2, b, X)
                if step == NORM2:
                    normalise(2, b, X, XN, s_xn)
                if step == INNER:
                    dv.wait_ge(s_rd, b + 1)
                    if b:
                        dv.wait_ge(s_up, b)
                    lg = bank(6)[:, 0:TB * E0].rearrange("p (i e) -> p i e", e=E0)
                    settle()
                    did(dv.tensor_copy(RA[:, :], bank(7)))
                    choose(b, E0, 2, lg, None)
                    did(dv.memset(red[:, TB:2 * TB], 0.0), s_lmax)
                if step == EXPS:
                    dv.wait_ge(s_ex, b + 1)
                    settle()
                    did(dv.tensor_reduce(red[:, 0:TB], exl[:, :, 0:E0], AX.X, ALU.add))
                    did(dv.tensor_tensor(oh[:, :, 0:E0], oh[:, :, 0:E0], exl[:, :, 0:E0], ALU.mult))
                    settle()
                    did(dv.reciprocal(red[:, TB:2 * TB], red[:, 0:TB]))
                    dv.wait_ge(s_sig, b + 1)
                    settle()
                    did(dv.tensor_tensor(oh[:, :, 0:E0], oh[:, :, 0:E0],
                                         red[:, TB:2 * TB].unsqueeze(2).broadcast_to([P, TB, E0]), ALU.mult))
                    did(dv.tensor_tensor(RB[:, :], RB[:, :], RA[:, :], ALU.mult))
                    settle()
                    for i in range(TB):
                        v = RB[:, i * P:(i + 1) * P].rearrange("p (e i) -> p e i", i=I0)
                        did(dv.tensor_tensor(v, v, oh[:, i, 0:E0].unsqueeze(2).broadcast_to([P, E0, I0]), ALU.mult),
                            s_aw if i == TB - 1 else None)
                if step == UP:
                    dv.wait_ge(s_up, b + 1)
                    did(dv.tensor_copy(H[:, b * TB:(b + 1) * TB, :].rearrange("p t c -> p (t c)"), bank(6, 2)), s_upe)
                if step == LN3:
                    settle()
                    stats(3, b, H)
                if step == ADD3:
                    add_norm(3, b)
                    stats(4, b, X)
                if step == NORM4:
                    normalise(4, b, X, XN, s_xn)
                    if b == 0:
                        dv.wait_ge(s_rqps, 2 * TB)
                        did(dv.memset(QP0[:, :, :, :], 0.0))
                for i in range(TB):
                    c = b * TB + i
                    at = PREP + i
                    q16 = QK[:, c % 2, :].rearrange("p (m d) -> p m d", d=HH)
                    if step == at:
                        dv.wait_ge(s_qkv, NT + c + 1)
                        did(dv.tensor_copy(V1[:, c, :], bank(7 - 2 * (i % 2))[:, 0:D]), s_ve)
                        dv.wait_ge(s_qkve1, c + 1)
                        settle()
                        did(dv.tensor_reduce(ss[:, c % 2, :], RA[:, :].rearrange("p (m d) -> p m d", d=HH), AX.X, ALU.add), s_ss)
                    if step == at + 1:
                        dv.wait_ge(s_rs1, c + 1)
                        did(dv.tensor_tensor(q16, q16, rs1[:, c % 2, :].unsqueeze(2).broadcast_to([P, 32, HH]), ALU.mult), s_ro)
                        settle()
                        if c >= 2:
                            dv.wait_ge(s_tps, 2 * NT + 4 * (c - 1))
                        more_high_parts1(dv, did, *parts1(c))
                i = step - PREP - 2
                if 0 <= i < TB:
                    c = b * TB + i
                    for n in (0, 1):
                        q, g0 = tunits(1)[n]
                        dv.wait_ge(s_tps, 2 * NT + 4 * c + n + 1)
                        did(dv.tensor_copy(KTr[:, b, g0:g0 + 4, i * P:(i + 1) * P],
                                           bank(n).rearrange("p (g c) -> p g c", g=4)), s_tevk)

            def after1(b, step):
                if step == LN5:
                    dv.wait_ge(s_woe1, (b + 1) * TB)
                    stats(5, b, H)
                if step == ADD5:
                    add_norm(5, b)
                    stats(6, b, X)
                if step == NORM6:
                    normalise(6, b, X, XN, s_xn)
                t = slice(b * TB, (b + 1) * TB)
                if step == ROUTE:
                    dv.wait_ge(s_rt, b + 1)
                    lg = bank(6)[:, 0:TB * E1].rearrange("p (i e) -> p i e", e=E1)
                    if b:
                        dv.wait_ge(s_rex, b)
                    settle()
                    choose(b, E1, 0, lg, bc(rb_sb[:, :], TB))
                    settle()
                    did(dv.tensor_tensor(OHB[b], iota_f[:, :].unsqueeze(1).unsqueeze(1).broadcast_to([P, TB, TOPK1, E1]),
                                         idxf[:, :, 0:TOPK1].unsqueeze(3).broadcast_to([P, TB, TOPK1, E1]), ALU.is_equal), s_rte)
                    settle()
                    with nc.allow_low_precision(reason="zeros and ones"):
                        did(dv.tensor_reduce(MK[:, t, :], OHB[b].rearrange("p t k e -> p t e k"), AX.X, ALU.add), s_oh)
                if step == ROUTED_EXP:
                    dv.wait_ge(s_rex, b + 1)
                    settle()
                    did(dv.tensor_tensor(PRDB[b], OHB[b], exl[:, :, :].unsqueeze(2).broadcast_to([P, TB, TOPK1, E1]), ALU.mult))
                    settle()
                    did(dv.tensor_reduce(wk[:, b * TB * TOPK1:(b + 1) * TB * TOPK1].rearrange("p (t k) -> p t k", k=TOPK1),
                                         PRDB[b], AX.X, ALU.add))

            for m in range(len(MUNITS)):
                maxima(0, m, bank(4 + m % 4))
                if m == 3:
                    dv.wait_ge(s_w0, 64)
                    for h in range(B):
                        t = slice(h * TB, (h + 1) * TB)
                        did(dv.tensor_tensor(H[:, t, :], H[:, t, :], bc(bo_sb[:, :], TB), ALU.add))
                    did(dv.tensor_tensor(lv_sb[:, 0:4:2, :], lv_sb[:, 0:4:2, :], lv_sb[:, 1:4:2, :], ALU.mult))
                    settle()
                    did(dv.tensor_reduce(lam_sb[:, 0:2], lv_sb[:, 0:4:2, :], AX.X, ALU.add), s_lamd)
                    dv.wait_ge(s_pool, 2)
                    did(dv.tensor_copy(iota16[:, :], iotaf[:, :]))
            dv.wait_ge(s_lame, 1)
            did(dv.tensor_tensor(lam_sb[:, 0:1], lam_sb[:, 3:4], lam_sb[:, 2:3], ALU.subtract))
            settle()
            did(dv.tensor_scalar(lam_sb[:, 1:2], lam_sb[:, 0:1], -LAMBDA_INIT, None, ALU.add))
            attend(0, 0, max_beside, MAX_STEPS)
            attend(0, 1, lambda step: after0(0, step), AFTER0)
            attend(1, 0, lambda step: after0(1, step), AFTER0)
            attend(1, 1, lambda step: after1(0, step), AFTER1)
            for step in range(AFTER1):
                after1(1, step)
            dv.wait_ge(s_rank, 1)
            did(dv.tensor_scalar(tcnt[:, 0, :], bank(7)[:, 0:E1], (P - 1) / 2, 1.0 / P, ALU.add, ALU.mult))
            settle()
            did(dv.tensor_scalar(tcnt[:, 0, :], tcnt[:, 0, :], MAGIC, None, ALU.add))
            settle()
            did(dv.tensor_scalar(tcnt[:, 0, :], tcnt[:, 0, :], -MAGIC, None, ALU.add))
            settle()
            did(dv.tensor_tensor_scan(tcnt[:, 1, :], ones64[:, :], tcnt[:, 0, :], 0.0, ALU.mult, ALU.add))
            settle()
            did(dv.tensor_tensor(tcnt[:, 2, :], tcnt[:, 1, :], tcnt[:, 0, :], ALU.subtract))
            did(dv.tensor_scalar(tcnt[:, 3, :], tcnt[:, 1, :], tile_no[:, 0:1], None, ALU.is_le))
            settle()
            did(dv.tensor_reduce(ecol[:, 0:1], tcnt[:, 3, :], AX.X, ALU.add))
            did(dv.tensor_scalar(tcnt[:, 2, :], tcnt[:, 2, :], float(P), None, ALU.mult))
            settle()
            did(dv.tensor_scalar(ecol[:, 1:2], ecol[:, 0:1], float(E1 - 1), None, ALU.min))
            settle()
            did(dv.tensor_scalar(ediag[:, :], ident[:, :], ecol[:, 1:2], None, ALU.mult), s_ediag)
            rank = bank(4).rearrange("p (t e) -> p t e", e=E1)
            did(dv.tensor_tensor(MKF, rank, bc(tcnt[:, 2, :], NT), ALU.add))
            settle()
            for b in range(B):
                did(dv.tensor_tensor(PRDB[b], OHB[b], MKF[:, b * TB:(b + 1) * TB, :].unsqueeze(2).broadcast_to(
                    [P, TB, TOPK1, E1]), ALU.mult))
            settle()
            for b in range(B):
                did(dv.tensor_reduce(slotf[:, b * TB * TOPK1:(b + 1) * TB * TOPK1].rearrange("p (t k) -> p t k", k=TOPK1),
                                     PRDB[b], AX.X, ALU.add))
            settle()
            did(dv.tensor_scalar(hi[:, :], slotf[:, :], -(P - 1) / 2, 1.0 / P, ALU.add, ALU.mult))
            settle()
            did(dv.tensor_scalar(hi[:, :], hi[:, :], MAGIC, None, ALU.add))
            settle()
            did(dv.tensor_scalar(hi[:, :], hi[:, :], -MAGIC, None, ALU.add))
            settle()
            did(dv.scalar_tensor_tensor(out=lo[:, :], in0=hi[:, :], scalar=-float(P), in1=slotf[:, :],
                                        op0=ALU.mult, op1=ALU.add))
            did(dv.tensor_copy(slotu[:, :], slotf[:, :]))
            settle()
            half = NC // 2
            for b in range(B):
                n = slice(b * half, (b + 1) * half)
                did(dv.tensor_tensor(HI1[:, n, 0:NTILE], bc(iota16[:, 0:NTILE], half),
                                     hi[:, n].unsqueeze(2).broadcast_to([P, half, NTILE]), ALU.is_equal), s_hi1)
                did(dv.tensor_tensor(LO1[b], bc(iota16[:, :], half), lo[:, n].unsqueeze(2).broadcast_to([P, half, P]),
                                     ALU.is_equal), s_lo1)
            dv.wait_ge(s_eps, 1)
            did(dv.tensor_copy(erow[:, 0, :], bank(7)[:, 0:NTILE]))
            settle()
            did(dv.tensor_scalar(erow[:, 1, :], erow[:, 0, :], -0.5, 0.5, ALU.add, ALU.mult))
            settle()
            did(dv.tensor_scalar(erow[:, 1, :], erow[:, 1, :], MAGIC, None, ALU.add))
            settle()
            did(dv.tensor_scalar(erow[:, 1, :], erow[:, 1, :], -MAGIC, None, ALU.add))
            settle()
            did(dv.scalar_tensor_tensor(out=odd[:, 1, :], in0=erow[:, 1, :], scalar=-2.0, in1=erow[:, 0, :],
                                        op0=ALU.mult, op1=ALU.add))
            did(dv.tensor_scalar(TABG[:, LAG_GU:LAG_GU + NTILE], erow[0:1, 0, :], float(KT * P), None, ALU.mult))
            did(dv.tensor_scalar(TABW[:, LAG_D:LAG_D + NTILE], erow[0:1, 1, :], float(D), None, ALU.mult))
            settle()
            did(dv.tensor_scalar(odd[:, 0, :], odd[:, 1, :], -1.0, 1.0, ALU.mult, ALU.add))
            dv.wait_ge(s_tok, 1)
            did(dv.tensor_copy(tok_of[:, :], bank(5)[:, 0:NTILE]), s_idx)
            did(dv.tensor_reduce(wsum[:, 0:NT], wk[:, :].rearrange("p (t k) -> p t k", k=TOPK1), AX.X, ALU.add))
            settle()
            did(dv.reciprocal(wsum[:, NT:2 * NT], wsum[:, 0:NT]))
            settle()
            w3 = wk[:, :].rearrange("p (t k) -> p t k", k=TOPK1)
            did(dv.tensor_tensor(w3, w3, wsum[:, NT:2 * NT].unsqueeze(2).broadcast_to([P, NT, TOPK1]), ALU.mult))

            def step(i, m):
                fixed = isinstance(i, int)

                def has(lag):
                    return not fixed or 0 <= i - lag < NTILE

                def wait(s, value):
                    if not fixed or value > 0:
                        dv.wait_ge(s, value)

                if has(LAG_D):
                    t, r = i - LAG_D, (m - LAG_D) % 4
                    dv.wait_ge(s_d, t + 1)
                    if m:
                        wait(s_st[r], 4 * (i - m) + 16 * ((m - LAG_D) // 4))
                    if m == U - 1:
                        wait(s_st[(U - LAG_D) % 4], 4 * (i - m) + 16 * ((U - LAG_D) // 4))
                    dv.tensor_copy(Y[:, r, :], bank(6 + r % 2)[:, 0:D]).then_inc(s_ye, 1)
                if has(LAG_TA):
                    t, r = i - LAG_TA, (m - LAG_TA) % 4
                    dv.wait_ge(s_ta, t + 1)
                    wait(s_d, t - 3)
                    dv.tensor_copy(AT[:, r, :], bank(4 + r % 2)[:, 0:P]).then_inc(s_ate, 1)
                if has(LAG_GU):
                    t, r = i - LAG_GU, (m - LAG_GU) % 4
                    dv.wait_ge(s_sgs, t + 1)
                    wait(s_ta, t - 3)
                    for half in range(2):
                        par = odd[:, half, t:t + 1] if fixed else odd[:, half, bass.ds(t, 1)]
                        ins = dv.scalar_tensor_tensor(out=A[:, r, half * F1:(half + 1) * F1], in0=SG[:, r, :], scalar=par,
                                                      in1=bank(2 + r % 2)[:, F1:2 * F1], op0=ALU.mult, op1=ALU.mult)
                    ins.then_inc(s_a, 1)

            for m in range(U):
                step(m, m)
            with dv.Fori(1, NBODY) as j:
                for m in range(U):
                    step(U * j + m, m)
            for m in range(LAG_D):
                step(NTILE + m, m)
            for n in range(NC):
                c = n // TOPK1
                dv.wait_ge(s_yg[n % U], 16 * (n // U + 1))
                if n % TOPK1 == 0:
                    dv.wait_ge(s_sd, c // 2 + 1)
                settle()
                did(dv.scalar_tensor_tensor(out=H[:, c, :], in0=XG[:, n % U, :], scalar=wk[:, n:n + 1],
                                            in1=bank(4 + c // 2)[:, c % 2 * D:(c % 2 + 1) * D] if n % TOPK1 == 0 else H[:, c, :],
                                            op0=ALU.mult, op1=ALU.add), s_mx)
                if n % TOPK1 == TOPK1 - 1:
                    settle()
                    did(dv.bn_stats(st[:, c, :], H[:, c, :]))
                    settle()
                    did(dv.bn_aggr(mv[:, c, :], st[:, c, :]), s_var if c % TB == TB - 1 else None)
                if n == NC // 2 + 1:
                    normalise(7, 0, H, H)
                    settle()
                    did(dv.tensor_tensor(X[:, 0:TB, :], X[:, 0:TB, :], H[:, 0:TB, :], ALU.add), s_fin)
            normalise(7, B - 1, H, H)
            settle()
            for i in range(TB, NT):
                did(dv.tensor_tensor(X[:, i, :], X[:, i, :], H[:, i, :], ALU.add), s_fin if i == NT - 1 else None)


_ORDER = ["x", "rms_w", "wqkv0", "bqkv0", "wo0", "bo0", "wrd0", "up0", "wqkv1", "wo1", "lvec", "router1", "rbias1",
          "wgu1", "wd1", "wsgu", "wsd", "rope", "ident_in", "mask_in", "before_in"]


def constants():
    j = np.arange(ROT, dtype=np.float32)
    freqs = (10000.0 ** (j.astype(np.float64) * (-2.0 / HD0))).astype(np.float32)
    ang = (np.arange(S, dtype=np.float32)[:, None] * freqs[None, :]).astype(np.float64)
    cos, sin = np.cos(ang), np.sin(ang)
    even = (np.arange(ROT) % 2 == 0)[None, :]
    rope = np.stack([np.where(even, cos, sin), np.where(even, -sin, cos), cos, sin], axis=1).astype(np.float32)
    rope = np.ascontiguousarray(rope.reshape(TB, P, 4, ROT).transpose(1, 0, 2, 3))
    a = np.arange(P)
    keyq = np.where(a[None, :] >= a[:, None], 0.0, NEG).astype(np.float32)
    return {"rope": rope, "ident_in": np.eye(P, dtype=np.float32),
            "before_in": (a[:, None] < a[None, :]).astype(np.float32),
            "mask_in": np.ascontiguousarray(np.stack([keyq, keyq.T], axis=1))}


def layouts(a):
    c = np.ascontiguousarray
    wg, wu, wd = a["L1_ffn_wg"], a["L1_ffn_wu"], a["L1_ffn_wd"]

    def experts(w):
        return w.reshape(E1, KT, P, F1).transpose(0, 2, 1, 3)

    def shared(w):
        return w.reshape(SH, KT, P, HS // P, P).transpose(0, 3, 2, 1, 4).reshape(NSB, P, KT * P)

    return {
        "x": c(a["L0_attn_x"].reshape(TOK, D)),
        "rms_w": c(a["L0_attn_rms_w"].reshape(KT, P).T),
        "wqkv0": c(np.concatenate([a["L0_attn_wq"], a["L0_attn_wk"], a["L0_attn_wv"]], axis=1)),
        "bqkv0": c(np.concatenate([a["L0_attn_bq"], a["L0_attn_bk"], a["L0_attn_bv"]])),
        "wo0": c(a["L0_attn_wo"]), "bo0": c(a["L0_attn_bo"]),
        "wrd0": c(np.concatenate([a["L0_ffn_router_w"].T, a["L0_ffn_down_w"].reshape(E0 * I0, D).T], axis=1)),
        "up0": c(a["L0_ffn_up_w"].transpose(0, 2, 1).reshape(E0 * I0, D)),
        "wqkv1": c(np.concatenate([a["L1_attn_wq"].T, a["L1_attn_wk"].T, a["L1_attn_wv"].T], axis=1)),
        "wo1": c(a["L1_attn_wo"].T),
        "lvec": c(np.concatenate([a["L1_attn_lq1"], a["L1_attn_lk1"], a["L1_attn_lq2"], a["L1_attn_lk2"]])),
        "router1": c(a["L1_ffn_router_w"]), "rbias1": c(a["L1_ffn_router_bias"]),
        "wgu1": c(np.concatenate([experts(wg), experts(wu)], axis=3).reshape(E1, P, KT * P)),
        "wd1": c(wd.reshape(E1 // 2, P, D)),
        "wsgu": c(np.concatenate([shared(a["L1_ffn_swg"]), shared(a["L1_ffn_swu"])], axis=2)),
        "wsd": c(a["L1_ffn_swd"].reshape(NSB, P, D)),
    }


def kernel(**inputs):
    import concourse.bacc as bacc
    from concourse.bass_utils import run_bass_kernel_spmd

    arrays = {**layouts({k: np.asarray(v) for k, v in inputs.items()}), **constants()}
    nc = bacc.Bacc("TRN2", target_bir_lowering=False, num_devices=1)
    aps = [nc.dram_tensor(f"in_{n}", arrays[n].shape, mybir.dt.float32, kind="ExternalInput").ap() for n in _ORDER]
    out = nc.dram_tensor("out_x", (TOK, D), mybir.dt.float32, kind="ExternalOutput").ap()
    h_dram = nc.dram_tensor("tokens", (TOK, D), mybir.dt.float32).ap()
    y_dram = nc.dram_tensor("expert_outputs", (NTILE * P, D), mybir.dt.float32).ap()
    build(nc, *aps, out, h_dram, y_dram)
    r = run_bass_kernel_spmd(nc, [{f"in_{n}": arrays[n] for n in _ORDER}], core_ids=[0])
    return r.results[0]["out_x"].reshape(B, S, D)
```
